# Optimizing a Trainium2 kernel written in Bass

```python
import numpy as np
import jax
import jax.numpy as jnp

def _softmax(x, axis=-1):
    return jax.nn.softmax(x, axis=axis)

def _gelu(x):
    return jax.nn.gelu(x, approximate=True)

def _silu(x):
    return jax.nn.silu(x)

def _sigmoid(x):
    return jax.nn.sigmoid(x)

def _layernorm(x, axis=-1, eps=1e-05):
    m = jnp.mean(x, axis=axis, keepdims=True)
    v = jnp.var(x, axis=axis, keepdims=True)
    return (x - m) / jnp.sqrt(v + eps)

def _scatter_add(tgt, idx, src, axis=0):
    return tgt.at[idx].add(src)

def _segment_sum(src, seg, n):
    return jax.ops.segment_sum(src, seg, n)
kernel_name = 'mk_lm_tower_d1_tok_ids768_r4_78b94b'

def setup_inputs(seed: int=0):
    np.random.seed(seed)
    _w = jnp.asarray

    def _rec_inputs():
        import jax
        import jax.numpy as jnp
        _rk = jax.random.key(seed)
        x = jax.random.randint(jax.random.fold_in(_rk, 1), (16, 128), 0, 12564, jnp.int32)
        mask_BS_i1_0 = jnp.where(jnp.ones((16, 128), dtype=bool), 1, 0).astype(jnp.int32)
        return (x, mask_BS_i1_0)
    x, mask_BS_i1_0 = _rec_inputs()

    def _L0_tok_setup():
        import jax, jax.numpy as jnp
        import numpy as np
        VOCAB = 50257
        HIDDEN = 192
        MAX_POS = 512
        NUM_TYPES = 2
        BATCH = 8
        SEQ = 512
        LN_EPS = 1e-05

        def _layer_norm(x, gamma, beta, eps=LN_EPS):
            mu = jnp.mean(x, axis=-1, keepdims=True)
            var = jnp.mean(jnp.square(x - mu), axis=-1, keepdims=True)
            return (x - mu) * jax.lax.rsqrt(var + eps) * gamma + beta
        key = jax.random.key(seed)
        k1, k2, k3, k4, k5 = jax.random.split(key, 5)
        input_ids = jax.random.randint(k1, (BATCH, SEQ), 0, VOCAB, dtype=jnp.int64 if jax.config.jax_enable_x64 else jnp.int32)
        token_type_ids = jax.random.randint(k2, (BATCH, SEQ), 0, NUM_TYPES, dtype=input_ids.dtype)
        word_emb = jax.random.normal(k3, (VOCAB, HIDDEN), dtype=jnp.float32) * 0.02
        pos_emb = jax.random.normal(k4, (MAX_POS, HIDDEN), dtype=jnp.float32) * 0.02
        type_emb = jax.random.normal(k5, (NUM_TYPES, HIDDEN), dtype=jnp.float32) * 0.02
        ln_gamma = jnp.ones((HIDDEN,), dtype=jnp.float32)
        ln_beta = jnp.zeros((HIDDEN,), dtype=jnp.float32)
        return {'input_ids': input_ids, 'token_type_ids': token_type_ids, 'word_emb': word_emb, 'pos_emb': pos_emb, 'type_emb': type_emb, 'ln_gamma': ln_gamma, 'ln_beta': ln_beta}
    _L0_tok_all = _L0_tok_setup()
    _L0_tok_in = {k: v for k, v in _L0_tok_all.items() if k in ('word_emb', 'pos_emb', 'type_emb', 'ln_gamma', 'ln_beta')}
    del _L0_tok_all

    def _L0_attn_setup():
        import jax, jax.numpy as jnp
        import numpy as np
        DIM = 192
        NUM_HEADS = 12
        HEAD_DIM = DIM // NUM_HEADS
        SCALE = HEAD_DIM ** (-0.5)
        key = jax.random.key(seed)
        k_x, k_qkv, k_pw, k_pb = jax.random.split(key, 4)
        x = jax.random.normal(k_x, (1, 1024, DIM), dtype=jnp.float32)
        w_qkv = jax.random.normal(k_qkv, (3 * DIM, DIM), dtype=jnp.float32) * DIM ** (-0.5)
        w_proj = jax.random.normal(k_pw, (DIM, DIM), dtype=jnp.float32) * DIM ** (-0.5)
        b_proj = jax.random.normal(k_pb, (DIM,), dtype=jnp.float32) * 0.01
        return {'x': x, 'w_qkv': w_qkv, 'w_proj': w_proj, 'b_proj': b_proj}
    _L0_attn_all = _L0_attn_setup()
    _L0_attn_in = {k: v for k, v in _L0_attn_all.items() if k in ('w_qkv', 'w_proj', 'b_proj')}
    del _L0_attn_all

    def _L0_ffn_setup():
        import jax, jax.numpy as jnp
        import numpy as np
        B, S, H, F = (4, 256, 192, 768)
        EC, EU = (4, 4)
        CAP_FACTOR = 1.0

        def _ffn(x, W1, b1, W2, b2):
            return jax.nn.gelu(x @ W1 + b1, approximate=False) @ W2 + b2

        def _expert_mix(h, route, W1, b1, W2, b2, n_exp):
            out = jnp.zeros_like(h)
            for e in range(n_exp):
                m = (route == e).astype(h.dtype)[:, None]
                out = out + m * _ffn(h, W1[e], b1[e], W2[e], b2[e])
            return out

        def _drop_mask(route, pmax, capacity):
            N = route.shape[0]
            order = jnp.lexsort((-jax.lax.stop_gradient(pmax), route))
            rs = route[order]
            starts = jnp.searchsorted(rs, rs, side='left')
            rank_sorted = jnp.arange(N) - starts
            rank = jnp.zeros((N,), jnp.int32).at[order].set(rank_sorted.astype(jnp.int32))
            return rank >= capacity
        key = jax.random.key(seed)
        ks = jax.random.split(key, 8)

        def w(k, shape, s=0.02):
            return jax.random.normal(k, shape, jnp.float32) * s
        return {'hidden_states': jax.random.normal(ks[0], (B, S, H), jnp.float32), 'Wsc': w(ks[1], (H, EC)), 'bsc': jnp.zeros((EC,), jnp.float32), 'W1c': w(ks[2], (EC, H, F)), 'b1c': jnp.zeros((EC, F), jnp.float32), 'W2c': w(ks[3], (EC, F, H)), 'b2c': jnp.zeros((EC, H), jnp.float32), 'Wsu': w(ks[4], (H, EU)), 'bsu': jnp.zeros((EU,), jnp.float32), 'W1u': w(ks[5], (EU, H, F)), 'b1u': jnp.zeros((EU, F), jnp.float32), 'W2u': w(ks[6], (EU, F, H)), 'b2u': jnp.zeros((EU, H), jnp.float32)}
    _L0_ffn_all = _L0_ffn_setup()
    _L0_ffn_in = {k: v for k, v in _L0_ffn_all.items() if k in ('Wsc', 'bsc', 'W1c', 'b1c', 'W2c', 'b2c', 'Wsu', 'bsu', 'W1u', 'b1u', 'W2u', 'b2u')}
    del _L0_ffn_all
    return {'x': x, 'mask_BS_i1_0': mask_BS_i1_0, 'L0_tok_word_emb': _L0_tok_in['word_emb'], 'L0_tok_pos_emb': _L0_tok_in['pos_emb'], 'L0_tok_type_emb': _L0_tok_in['type_emb'], 'L0_tok_ln_gamma': _L0_tok_in['ln_gamma'], 'L0_tok_ln_beta': _L0_tok_in['ln_beta'], 'L0_attn_w_qkv': _L0_attn_in['w_qkv'], 'L0_attn_w_proj': _L0_attn_in['w_proj'], 'L0_attn_b_proj': _L0_attn_in['b_proj'], 'L0_ffn_Wsc': _L0_ffn_in['Wsc'], 'L0_ffn_bsc': _L0_ffn_in['bsc'], 'L0_ffn_W1c': _L0_ffn_in['W1c'], 'L0_ffn_b1c': _L0_ffn_in['b1c'], 'L0_ffn_W2c': _L0_ffn_in['W2c'], 'L0_ffn_b2c': _L0_ffn_in['b2c'], 'L0_ffn_Wsu': _L0_ffn_in['Wsu'], 'L0_ffn_bsu': _L0_ffn_in['bsu'], 'L0_ffn_W1u': _L0_ffn_in['W1u'], 'L0_ffn_b1u': _L0_ffn_in['b1u'], 'L0_ffn_W2u': _L0_ffn_in['W2u'], 'L0_ffn_b2u': _L0_ffn_in['b2u']}

def reference(x, mask_BS_i1_0, L0_tok_word_emb, L0_tok_pos_emb, L0_tok_type_emb, L0_tok_ln_gamma, L0_tok_ln_beta, L0_attn_w_qkv, L0_attn_w_proj, L0_attn_b_proj, L0_ffn_Wsc, L0_ffn_bsc, L0_ffn_W1c, L0_ffn_b1c, L0_ffn_W2c, L0_ffn_b2c, L0_ffn_Wsu, L0_ffn_bsu, L0_ffn_W1u, L0_ffn_b1u, L0_ffn_W2u, L0_ffn_b2u):
    import jax
    import jax.numpy as jnp

    def _L0_tok_ref(input_ids, token_type_ids, word_emb, pos_emb, type_emb, ln_gamma, ln_beta):
        import jax, jax.numpy as jnp
        import numpy as np
        VOCAB = 50257
        HIDDEN = 192
        MAX_POS = 512
        NUM_TYPES = 2
        BATCH = 8
        SEQ = 512
        LN_EPS = 1e-05

        def _layer_norm(x, gamma, beta, eps=LN_EPS):
            mu = jnp.mean(x, axis=-1, keepdims=True)
            var = jnp.mean(jnp.square(x - mu), axis=-1, keepdims=True)
            return (x - mu) * jax.lax.rsqrt(var + eps) * gamma + beta
        seq = input_ids.shape[1]
        e = word_emb[input_ids]
        e = e + pos_emb[jnp.arange(seq)][None, :, :]
        e = e + type_emb[token_type_ids]
        return _layer_norm(e, ln_gamma, ln_beta)

    def _L0_attn_ref(x, w_qkv, w_proj, b_proj):
        import jax, jax.numpy as jnp
        import numpy as np
        DIM = 192
        NUM_HEADS = 12
        HEAD_DIM = DIM // NUM_HEADS
        SCALE = HEAD_DIM ** (-0.5)
        b, s, d = x.shape
        qkv = jnp.einsum('bsd,ed->bse', x, w_qkv)
        qkv = qkv.reshape(b, s, 3, NUM_HEADS, HEAD_DIM)
        qkv = jnp.transpose(qkv, (2, 0, 3, 1, 4))
        q, k, v = (qkv[0], qkv[1], qkv[2])
        scores = jnp.einsum('bhqe,bhke->bhqk', q, k) * SCALE
        probs = jax.nn.softmax(scores, axis=-1)
        attended = jnp.einsum('bhqk,bhke->bhqe', probs, v)
        attended = jnp.transpose(attended, (0, 2, 1, 3)).reshape(b, s, d)
        return jnp.einsum('bsd,ed->bse', attended, w_proj) + b_proj

    def _L0_ffn_ref(hidden_states, Wsc, bsc, W1c, b1c, W2c, b2c, Wsu, bsu, W1u, b1u, W2u, b2u):
        import jax, jax.numpy as jnp
        import numpy as np
        B, S, H, F = (4, 256, 192, 768)
        EC, EU = (4, 4)
        CAP_FACTOR = 1.0

        def _ffn(x, W1, b1, W2, b2):
            return jax.nn.gelu(x @ W1 + b1, approximate=False) @ W2 + b2

        def _expert_mix(h, route, W1, b1, W2, b2, n_exp):
            out = jnp.zeros_like(h)
            for e in range(n_exp):
                m = (route == e).astype(h.dtype)[:, None]
                out = out + m * _ffn(h, W1[e], b1[e], W2[e], b2[e])
            return out

        def _drop_mask(route, pmax, capacity):
            N = route.shape[0]
            order = jnp.lexsort((-jax.lax.stop_gradient(pmax), route))
            rs = route[order]
            starts = jnp.searchsorted(rs, rs, side='left')
            rank_sorted = jnp.arange(N) - starts
            rank = jnp.zeros((N,), jnp.int32).at[order].set(rank_sorted.astype(jnp.int32))
            return rank >= capacity
        shp = hidden_states.shape
        h = hidden_states.reshape(-1, shp[-1])
        N = h.shape[0]
        capacity = int(CAP_FACTOR * N / EC)
        pc = jax.nn.softmax(h @ Wsc + bsc, axis=-1)
        pmax_c = jnp.max(pc, axis=-1)
        route_c = jnp.argmax(pc, axis=-1)
        dropped = _drop_mask(route_c, pmax_c, capacity)
        scale_c = (pmax_c / jax.lax.stop_gradient(pmax_c))[:, None]
        common = _expert_mix(h, route_c, W1c, b1c, W2c, b2c, EC) * scale_c
        pu = jax.nn.softmax(h @ Wsu + bsu, axis=-1)
        pmax_u = jnp.max(pu, axis=-1)
        route_u = jnp.argmax(pu, axis=-1)
        scale_u = (pmax_u / jax.lax.stop_gradient(pmax_u))[:, None]
        unique = _expert_mix(h, route_u, W1u, b1u, W2u, b2u, EU) * scale_u
        out = common + dropped[:, None].astype(h.dtype) * unique
        return out.reshape(shp)
    h = _L0_tok_ref(x, mask_BS_i1_0, L0_tok_word_emb, L0_tok_pos_emb, L0_tok_type_emb, L0_tok_ln_gamma, L0_tok_ln_beta)
    h = h + _L0_attn_ref(_layernorm(h, axis=-1), L0_attn_w_qkv, L0_attn_w_proj, L0_attn_b_proj)
    h = h + _L0_ffn_ref(_layernorm(h, axis=-1), L0_ffn_Wsc, L0_ffn_bsc, L0_ffn_W1c, L0_ffn_b1c, L0_ffn_W2c, L0_ffn_b2c, L0_ffn_Wsu, L0_ffn_bsu, L0_ffn_W1u, L0_ffn_b1u, L0_ffn_W2u, L0_ffn_b2u)
    return h

_drawn_inputs = setup_inputs


def setup_inputs(seed=0):
    import zlib

    import numpy as np

    out = dict(_drawn_inputs(seed))
    spreads = {'L0_tok_ln_gamma': (1.0, 0.2),
     'L0_tok_ln_beta': (0.0, 0.1),
     'L0_ffn_bsc': (0.0, 0.1),
     'L0_ffn_b1c': (0.0, 0.327),
     'L0_ffn_b2c': (0.0, 0.1),
     'L0_ffn_bsu': (0.0, 0.512),
     'L0_ffn_b1u': (0.0, 0.533),
     'L0_ffn_b2u': (0.0, 0.1)}
    factors = {'L0_attn_b_proj': 4.677}
    for name, (base, spread) in spreads.items():
        noise = np.random.default_rng([zlib.crc32(name.encode()), seed]).standard_normal(out[name].shape)
        drawn = base * np.exp(spread * noise) if base else spread * noise
        out[name] = jnp.asarray(drawn.astype(out[name].dtype))
    for name, factor in factors.items():
        out[name] = (out[name] * factor).astype(out[name].dtype)
    return out
```

```python
from contextlib import ExitStack

import concourse.bass as bass
from concourse import mybir

F32 = mybir.dt.float32
F16 = mybir.dt.float16
BF16 = mybir.dt.bfloat16
I32 = mybir.dt.int32
ALU = mybir.AluOpType
ACT = mybir.ActivationFunctionType
AX = mybir.AxisListType.X
ds = bass.ds

P = 128
SEQS = 16
NT = SEQS
N = NT * P
D = 192
D2 = D - P
DX = 2 * P
HEADS = 12
HD = D // HEADS
RG = 4
CH = HEADS // RG
QC = CH * P
F = 768
FC = F // P
E = 4
CAP = N // E
TC = NT + E - 1
TU = (N - CAP) // P + E - 1
TT = TC + TU
EPS = 1e-5

XS = 2.0 ** 11
QS = 2.0 ** 4
VS = 2.0 ** -3
GS = 2.0 ** 6
UN = 1.0 / (XS * XS)
SCORE = HD ** -0.5 / (QS * QS)
TIE = 2.0 ** -28
WE = 2 * F + FC * D


def upto(engine, semaphore, count):
    if not isinstance(count, int) or count > 0:
        engine.wait_ge(semaphore, count)


def alone(engine, passed):
    engine.sem_inc(passed, 1)


def within(i, n):
    return not isinstance(i, int) or 0 <= i < n


def build(nc, ids, types, word, pos, type_emb, gamma, beta, wqkvp, b_proj,
          wr, br, wexp, b1, b2, xrows, prow_dram, out):
    with ExitStack() as ctx:
        def sb(name, shape, dt):
            return ctx.enter_context(nc.sbuf_tensor(name, shape, dt))

        def sem(name):
            return ctx.enter_context(nc.semaphore(name))

        ident = sb("ident", [P, P], F32)
        before = sb("before", [P, P], F16)
        ones = sb("ones", [P, P], F16)
        low_rows = sb("low_rows", [P, 1], F32)
        low_heads_i = sb("low_heads_i", [P, 1], I32)
        low_heads = sb("low_heads", [P, 1], F32)
        minus_half = sb("minus_half", [P, 1], F32)
        iota_s = sb("iota_s", [P, P], F32)
        iota_t = sb("iota_t", [P, TC], F32)
        token1 = sb("token1", [P, NT], F32)
        tie = sb("tie", [P, 2 * N - P], BF16)
        ids_sb = sb("ids_sb", [P, NT], I32)
        types_sb = sb("types_sb", [P, NT], I32)
        types_f = sb("types_f", [P, NT], F32)
        pos_sb = sb("pos_sb", [P, D], F32)
        ty = sb("ty", [P, 2, D], F32)
        gamma_sb = sb("gamma_sb", [P, D], F32)
        beta_sb = sb("beta_sb", [P, D], F32)
        bproj_sb = sb("bproj_sb", [P, D], F32)
        wr_sb = sb("wr_sb", [P, 2, 2 * E], F32)
        br_sb = sb("br_sb", [P, 2 * E], F32)
        b1_sb = sb("b1_sb", [P, 2 * E, FC], F32)
        b2_sb = sb("b2_sb", [P, 2 * E, D], F32)
        AC = 2 * QC + D + D
        w_hi = sb("w_hi", [P, AC], F16)
        w_lo = sb("w_lo", [P, AC], F16)
        w_mix = sb("w_mix", [P, AC], F16)
        w_tmp = sb("w_tmp", [P, AC], F16)
        stage = sb("stage", [P, 2, WE], F32)
        e_hi = sb("e_hi", [P, 2 * E, WE], F16)
        e_lo = sb("e_lo", [P, 2 * E, WE], F16)

        we = sb("we", [P, 2, D], F32)
        tsel = sb("tsel", [P, D], F32)
        h1 = sb("h1", [P, D], F32)
        h = sb("h", [P, 2, D], F32)
        hb = sb("hb", [P, 4, D], F32)
        stats = sb("stats", [P, 3, 6], F32)
        mv = sb("mv", [P, 3, 2], F32)
        vare = sb("vare", [P, 3, 1], F32)
        rstd = sb("rstd", [P, 3, 1], F32)
        xn = sb("xn", [P, 2, DX], F32)
        att = sb("att", [P, DX], F32)
        t_hi = sb("t_hi", [P, 2 * DX], F16)
        t_lo = sb("t_lo", [P, 2 * DX], F16)
        q_low = sb("q_low", [P, QC], F16)
        q_sb = sb("q_sb", [P, 2, QC], F16)
        k_hi = sb("k_hi", [P, 2, QC], F16)
        k_lo = sb("k_lo", [P, 2, QC], F16)
        v_sb = sb("v_sb", [P, 2, HEADS, HD + 1], F32)
        rawmax = sb("rawmax", [P, RG, CH], F32)
        negmax = sb("negmax", [P, RG, CH], F32)
        probs = sb("probs", [P, RG, CH, P], F32)
        probs_t = sb("probs_t", [P, RG, CH, P], F32)
        rden = sb("rden", [P, HEADS, 1], F32)
        h2 = sb("h2", [P, NT, D], F32)
        xn2 = sb("xn2", [P, 2, DX], F32)
        x2t = sb("x2t", [P, DX], F32)
        logits = sb("logits", [P, NT, 2 * E], F32)

        R2 = NT * 2
        top = sb("top", [P, R2], F32)
        lg = sb("lg", [P, R2, E], F32)
        ex = sb("ex", [P, R2, E], F32)
        den = sb("den", [P, R2], F32)
        rec = sb("rec", [P, R2], F32)
        pr = sb("pr", [P, R2, E], F32)
        pmax = sb("pmax", [P, R2], F32)
        eq = sb("eq", [P, R2, E], F32)
        seen = sb("seen", [P, 2, R2], F32)
        oh = sb("oh", [P, R2, E], F16)
        pm_rec = sb("pm_rec", [P, R2], F32)
        scale = sb("scale", [P, R2], F32)
        pm_c = sb("pm_c", [P, NT], F32)
        pmt = sb("pmt", [NT, P], F32)
        prow = sb("prow", [P, N], F32)
        less = sb("less", [P, 2, N], F16)
        rank4 = sb("rank4", [P, NT, E], F32)
        rank = sb("rank", [P, NT], F32)
        dropped = sb("dropped", [P, NT], F32)
        ohx = sb("ohx", [P, NT, E], F16)
        cum = sb("cum", [P, 2, 2 * NT, E], F32)
        tot = sb("tot", [P, E], F32)
        tiles_i = sb("tiles_i", [P, E], I32)
        ends = sb("ends", [P, 3, 2 * E], F32)
        ge = sb("ge", [P, TC, E - 1], F32)
        tile_e = sb("tile_e", [P, TC], F32)
        posn = sb("posn", [P, NT, E], F32)
        pos2 = sb("pos2", [P, NT, E], F32)
        pos3 = sb("pos3", [P, NT, E], F32)
        slot = sb("slot", [P, NT], F32)
        slot_i = sb("slot_i", [P, NT], I32)
        slot_hi = sb("slot_hi", [P, NT], I32)
        slot_lo = sb("slot_lo", [P, NT], I32)
        slot_hf = sb("slot_hf", [P, NT], F32)
        slot_lf = sb("slot_lf", [P, NT], F32)
        valid = sb("valid", [P, NT], F32)
        tokv = sb("tokv", [P, NT], F32)
        scv = sb("scv", [P, NT], F32)
        st = stage[:, :, :].rearrange("p a n -> p (a n)")
        oh_s = st[:, 0:N // 2].bitcast(F16).rearrange("p (t s) -> p t s", t=NT)
        at0 = N // 2 + 3 * F
        oh_t = st[:, at0:at0 + NT * TC].rearrange("p (i t) -> p i t", i=NT)
        oh_m = st[:, at0 + NT * TC:at0 + 2 * NT * TC].bitcast(F16).rearrange("p (i a t) -> p i a t", i=NT, a=2)
        inv = sb("inv", [P, 2, TC], F32)
        empty = sb("empty", [P, TC], F32)
        out_f = sb("out_f", [P, TC], F32)
        experts = sb("experts", [1, TT], I32)
        idx_in = sb("idx_in", [P, TT], I32)
        idx_out = sb("idx_out", [P, TT], I32)
        slot_scale = sb("slot_scale", [P, TT], F32)

        now_in = sb("now_in", [P, 2, 1], I32)
        now_out = sb("now_out", [P, 2, 1], I32)
        act = st[:, N // 2:N // 2 + 2 * F].rearrange("p (a f) -> p a f", a=2)
        act_hi = st[:, N // 2 + 2 * F:N // 2 + 3 * F].bitcast(F16).rearrange("p (a f) -> p a f", a=2)
        hs = h2[:, :, :].rearrange("p t d -> p (t d)")
        act_lo = hs[:, 0:F].bitcast(F16).rearrange("p (a f) -> p a f", a=2)
        xg = hs[:, F:F + 2 * DX].rearrange("p (a d) -> p a d", a=2)
        xg_hi = hs[:, F + 2 * DX:F + 3 * DX].bitcast(F16).rearrange("p (a d) -> p a d", a=2)
        xg_lo = hs[:, F + 3 * DX:F + 4 * DX].bitcast(F16).rearrange("p (a d) -> p a d", a=2)
        yb = hs[:, F + 4 * DX:F + 4 * DX + D]
        y = hs[:, F + 4 * DX + D:F + 4 * DX + 3 * D].rearrange("p (a d) -> p a d", a=2)

        bank = ctx.enter_context(nc.psum_tensor("bank", [P, 8, 512], F32))
        T_BANK, Q_BANK = 6, 7

        s_ids, s_small, s_wqkv, s_biases = sem("s_ids"), sem("s_small"), sem("s_wqkv"), sem("s_biases")
        s_exp = [sem("s_exp0"), sem("s_exp1")]
        s_word = sem("s_word")
        s_out0, s_x = sem("s_out0"), sem("s_x")
        s_pm_st, s_pm_ld = sem("s_pm_st"), sem("s_pm_ld")
        s_gather, s_scatter = sem("s_gather"), sem("s_scatter")
        s_const, s_pconst, s_types, s_pt = sem("s_const"), sem("s_pconst"), sem("s_types"), sem("s_pt")
        s_dconst = sem("s_dconst")
        s_whi, s_wsplit, s_ehi, s_esplit = sem("s_whi"), sem("s_wsplit"), sem("s_ehi"), sem("s_esplit")
        s_warm = sem("s_warm")
        s_past_dve, s_past_pool, s_past_sp = sem("s_past_dve"), sem("s_past_pool"), sem("s_past_sp")
        s_tsel, s_e0, s_e = sem("s_tsel"), sem("s_e0"), sem("s_e")
        s_st = [sem(f"s_st{n}") for n in range(3)]
        s_mv = [sem(f"s_mv{n}") for n in range(3)]
        s_ve = [sem(f"s_ve{n}") for n in range(3)]
        s_rs = [sem(f"s_rs{n}") for n in range(3)]
        s_h1, s_hg, s_h, s_hb, s_xn = sem("s_h1"), sem("s_hg"), sem("s_h"), sem("s_hb"), sem("s_xn")
        s_T, s_Thi, s_Tlo = sem("s_T"), sem("s_Thi"), sem("s_Tlo")
        s_Q, s_K, s_VY = sem("s_Q"), sem("s_K"), sem("s_VY")
        s_qlow, s_q, s_khi, s_klo = sem("s_qlow"), sem("s_q"), sem("s_khi"), sem("s_klo")
        s_v, s_h2 = sem("s_v"), sem("s_h2")
        s_S = [sem(f"s_S{r}") for r in range(RG)]
        s_max, s_nmax = sem("s_max"), sem("s_nmax")
        s_P = [sem(f"s_P{r}") for r in range(RG)]
        s_PT = [sem(f"s_PT{r}") for r in range(RG)]
        s_PTe = [sem(f"s_PTe{r}") for r in range(RG)]
        s_O, s_rd, s_att = sem("s_O"), sem("s_rd"), sem("s_att")
        s_xn2 = sem("s_xn2")
        s_X2, s_x2t, s_L, s_lg = sem("s_X2"), sem("s_x2t"), sem("s_L"), sem("s_lg")
        s_r = sem("s_r")
        s_ex = sem("s_ex")
        s_ohx, s_pre, s_perm, s_inv = sem("s_ohx"), sem("s_pre"), sem("s_perm"), sem("s_inv")
        s_route = sem("s_route")
        s_pmc, s_pmT, s_pmt = sem("s_pmc"), sem("s_pmT"), sem("s_pmt")
        s_less, s_cnt = sem("s_less"), sem("s_cnt")
        s_now_in, s_now_out = sem("s_now_in"), sem("s_now_out")
        s_XT, s_xhi, s_xlo = sem("s_XT"), sem("s_xhi"), sem("s_xlo")
        s_H = [sem("s_H0"), sem("s_H1")]
        s_g = [sem("s_g0"), sem("s_g1")]
        s_ghi, s_glo = sem("s_ghi"), sem("s_glo")
        s_Y, s_yb, s_y = sem("s_Y"), sem("s_yb"), sem("s_y")
        N_CONST = 8

        wide = lambda t: t.rearrange("p t d -> p (t d)")

        def steps(engine, body):
            for i in range(-2, 3):
                body(i, i % 2)
            with engine.Fori(3, NT - 4, 2) as i:
                body(i, 1)
                body(i + 1, 0)
            for i in range(NT - 3, NT + 2):
                body(i, i % 2)

        def slot_steps(engine, body, after):
            for t in range(-2, 4):
                body(t, t % 2, ranks=True)
            with engine.Fori(4, NT - 1, 2) as t:
                body(t, 0, ranks=True)
                body(t + 1, 1, ranks=True)
            for t in range(NT, TC + 1):
                body(t, t % 2)
                if t in after:
                    after[t]()
            with engine.Fori(TC + 1, TT - 3, 2) as t:
                body(t, 0)
                body(t + 1, 1)
            for t in range(TT - 2, TT + 3):
                body(t, t % 2)

        block = ctx.enter_context(nc.Block())

        @block.sync
        def _(sp):
            sp.dma_start(ids_sb[:, :], ids).then_inc(s_ids, 16)
            sp.dma_start(types_sb[:, :], types).then_inc(s_small, 16)
            sp.dma_start(pos_sb[:, :], pos).then_inc(s_small, 16)
            for n in range(2):
                sp.dma_start(ty[:, n, :], type_emb[n:n + 1, :].broadcast_to([P, D])).then_inc(s_small, 16)
            sp.dma_start(gamma_sb[:, :], gamma.broadcast_to([P, D])).then_inc(s_small, 16)
            sp.dma_start(beta_sb[:, :], beta.broadcast_to([P, D])).then_inc(s_small, 16)
            sp.dma_start(bproj_sb[:, :], b_proj.broadcast_to([P, D])).then_inc(s_small, 16)
            sp.dma_start(stage[:, 0, 0:AC], wqkvp[0]).then_inc(s_wqkv, 16)
            sp.dma_start(stage[:, 1, 0:AC], wqkvp[1]).then_inc(s_wqkv, 16)
            sp.dma_start(wr_sb[:, :, :], wr).then_inc(s_biases, 16)
            sp.dma_start(br_sb[:, :], br.broadcast_to([P, 2 * E])).then_inc(s_biases, 16)
            sp.dma_start(b1_sb[:, :, :], b1).then_inc(s_biases, 16)
            sp.dma_start(wide(b2_sb[:, :, :]), b2.broadcast_to([P, 2 * E * D])).then_inc(s_biases, 16)
            for e in range(2 * E):
                upto(sp, s_wsplit, 2)
                upto(sp, s_esplit, e - 1)
                sp.dma_start(stage[:, e % 2, :], wexp[e]).then_inc(s_exp[e % 2], 16)
            def store(b):
                sp.wait_ge(s_h2, b + 1)
                alone(sp, s_past_sp)
                sp.dma_start(out[ds(b * P, P), :], wide(h2[:, ds(b, 1), :])).then_inc(s_out0, 16)
                sp.wait_ge(s_xn2, 2 * b + 2)
                alone(sp, s_past_sp)
                upto(sp, s_x, 16 * b)
                alone(sp, s_past_sp)
                sp.dma_start(xrows[ds(b * P, P), :], wide(xn2[:, ds(b % 2, 1), :])).then_inc(s_x, 16)

            store(0)
            with sp.Fori(1, NT) as b:
                store(b)
            sp.wait_ge(s_pmt, 1)
            sp.dma_start(prow_dram.rearrange("(i p) -> i p", p=P), pmt[:, :]).then_inc(s_pm_st, 16)
            sp.wait_ge(s_pm_st, 16)
            sp.dma_start(prow[:, :], prow_dram.unsqueeze(0).broadcast_to([P, N])).then_inc(s_pm_ld, 16)
            sp.wait_ge(s_pm_ld, 16)

        @block.gpsimd
        def _(pool):
            pool.wait_ge(s_ids, 16)

            pool.memset(minus_half[:, :], -0.5).then_inc(s_const, 1)
            pool.memset(ident[:, :], 0.0).then_inc(s_pconst, 1)
            pool.memset(ones[:, :], 1.0).then_inc(s_pconst, 1)
            pool.memset(tie[:, :], 0.0).then_inc(s_pconst, 1)
            pool.memset(low_rows[:, :], 0.0).then_inc(s_pconst, 1)
            pool.wait_ge(s_pconst, 4)
            pool.affine_select(out=ident[:, :], in_=ident[:, :], compare_op=ALU.not_equal, fill=1.0,
                               base=0, pattern=[[-1, P]], channel_multiplier=1).then_inc(s_const, 1)
            pool.affine_select(out=before[:, :], in_=ones[:, :], compare_op=ALU.is_gt, fill=0.0,
                               base=0, pattern=[[1, P]], channel_multiplier=-1).then_inc(s_const, 1)
            pool.wait_ge(s_const, 3)
            pool.memset(low_rows[P // 2:P, :], XS).then_inc(s_const, 1)
            pool.wait_ge(s_const, 4)
            pool.iota(low_heads_i[:, :], pattern=[[0, 1]], base=0, channel_multiplier=1).then_inc(s_const, 1)
            pool.wait_ge(s_small, 16 * 7)
            pool.tensor_tensor(pos_sb[:, :], pos_sb[:, :], ty[:, 0, :], ALU.add).then_inc(s_pt, 1)
            pool.tensor_tensor(ty[:, 1, :], ty[:, 1, :], ty[:, 0, :], ALU.subtract).then_inc(s_pt, 1)
            pool.tensor_copy(types_f[:, :], types_sb[:, :]).then_inc(s_types, 1)
            pool.wait_ge(s_const, 1)
            pool.wait_ge(s_pt, 2)
            pool.wait_ge(s_types, 1)

            def embed_ahead(j, par):
                if isinstance(j, int) and j >= NT:
                    return
                upto(pool, s_word, j * 16)
                upto(pool, s_e, j - 1)
                pool.tensor_copy(now_in[:, par, :], ids_sb[:, ds(j, 1)]).then_inc(s_now_in, 1)
                pool.wait_ge(s_now_in, j + 1)
                alone(pool, s_past_pool)
                pool.indirect_dma_start(
                    out=we[:, par, :], out_offset=None, in_=word,
                    in_offset=bass.IndirectOffsetOnAxis(ap=now_in[:, par, :], axis=0)).then_inc(s_word, 16)

            def rstd_of(n, count):
                pool.wait_ge(s_mv[n], count)
                alone(pool, s_past_pool)
                pool.tensor_scalar(vare[:, n, :], mv[:, n, 1:2], EPS, None, ALU.add).then_inc(s_ve[n], 1)
                pool.wait_ge(s_ve[n], count)
                pool.tensor_tensor(rstd[:, n, :], vare[:, n, :], minus_half[:, :], ALU.pow).then_inc(s_rs[n], 1)

            embed_ahead(0, 0)

            def body(i, par):
                j = i + 2
                if within(j, NT):
                    upto(pool, s_e, j)
                    pool.wait_ge(s_word, 16 * (j + 1))
                    pool.tensor_tensor(tsel[:, :], ty[:, 1, :], types_f[:, ds(j, 1)].broadcast_to([P, D]),
                                       ALU.mult).then_inc(s_tsel, 1)
                    pool.tensor_tensor(we[:, par, :], we[:, par, :], pos_sb[:, :], ALU.add).then_inc(s_e0, 1)
                    pool.wait_ge(s_tsel, j + 1)
                    pool.wait_ge(s_e0, j + 1)
                    pool.tensor_tensor(we[:, par, :], we[:, par, :], tsel[:, :], ALU.add).then_inc(s_e, 1)
                    if within(j + 1, NT) and not (isinstance(j, int) and j + 1 >= NT):
                        upto(pool, s_h1, j)
                        embed_ahead(j + 1, 1 - par)
                    rstd_of(0, j + 1)
                    pool.wait_ge(s_h1, j + 1)
                    upto(pool, s_hb, j)
                    upto(pool, s_xn, 2 * (j - 1))
                    pool.tensor_tensor(h[:, par, :], h1[:, :], gamma_sb[:, :], ALU.mult).then_inc(s_hg, 1)
                    pool.wait_ge(s_hg, j + 1)
                    pool.tensor_tensor(h[:, par, :], h[:, par, :], beta_sb[:, :], ALU.add).then_inc(s_h, 1)
                    pool.wait_ge(s_h, j + 1)
                    upto(pool, s_h2, j - 3)
                    pool.tensor_tensor(wide(hb[:, ds(j % 4, 1), :]), h[:, par, :], bproj_sb[:, :],
                                       ALU.add).then_inc(s_hb, 1)
                    rstd_of(1, j + 1)
                if within(i - 1, NT):
                    rstd_of(2, i)

            steps(pool, body)

            pool.iota(iota_s[:, :], pattern=[[1, P]], base=0, channel_multiplier=0,
                      allow_small_or_imprecise_dtypes=True).then_inc(s_const, 1)
            pool.iota(iota_t[:, :], pattern=[[1, TC]], base=0, channel_multiplier=0,
                      allow_small_or_imprecise_dtypes=True).then_inc(s_const, 1)
            pool.iota(token1[:, :], pattern=[[P, NT]], base=1, channel_multiplier=1,
                      allow_small_or_imprecise_dtypes=True).then_inc(s_const, 1)
            pool.affine_select(out=tie[:, :], in_=tie[:, :], compare_op=ALU.is_ge, fill=TIE,
                               base=N - P, pattern=[[-1, 2 * N - P]], channel_multiplier=1).then_inc(s_dconst, 1)

            pool.wait_ge(s_x, 16 * NT)
            pool.wait_ge(s_out0, 16 * NT)

            def tiles(t, par, ranks=False):
                g = t + 2
                if within(g, TT):
                    if isinstance(g, int) and g in (0, TC):
                        pool.wait_ge(s_route, 1 + (g == TC))
                    upto(pool, s_gather, 16 * g)
                    pool.tensor_copy(now_in[:, par, :], idx_in[:, ds(g, 1)]).then_inc(s_now_in, 1)
                    pool.wait_ge(s_now_in, NT + g + 1)
                    upto(pool, s_XT, g - 1)
                    alone(pool, s_past_pool)
                    pool.indirect_dma_start(
                        out=xg[:, par, :], out_offset=None, in_=xrows,
                        in_offset=bass.IndirectOffsetOnAxis(ap=now_in[:, par, :], axis=0)).then_inc(s_gather, 16)
                o, opar = t - 2, par
                if within(o, TT):
                    upto(pool, s_scatter, 16 * o)
                    pool.tensor_copy(now_out[:, opar, :], idx_out[:, ds(o, 1)]).then_inc(s_now_out, 1)
                    pool.wait_ge(s_now_out, o + 1)
                    pool.wait_ge(s_y, o + 1)
                    alone(pool, s_past_pool)
                    pool.indirect_dma_start(
                        out=out, out_offset=bass.IndirectOffsetOnAxis(ap=now_out[:, opar, :], axis=0),
                        in_=y[:, opar, :], in_offset=None, bounds_check=N - 1, oob_is_err=False,
                        compute_op=ALU.add).then_inc(s_scatter, 16)

            slot_steps(pool, tiles, {})
            pool.wait_ge(s_scatter, 16 * TT)

        @block.scalar
        def _(act_e):
            act_e.wait_ge(s_wqkv, 32)
            act_e.wait_ge(s_const, 5)
            act_e.activation(w_hi[:, :], stage[:, 0, 0:AC], ACT.Copy, scale=XS).then_inc(s_whi, 1)
            act_e.activation(w_tmp[:, :], stage[:, 1, 0:AC], ACT.Copy, scale=low_rows[:, :]).then_inc(s_whi, 1)
            for e in range(2 * E):
                act_e.wait_ge(s_exp[e % 2], 16 * (e // 2 + 1))
                act_e.activation(e_hi[:, e, 0:F], stage[:, e % 2, 0:F], ACT.Copy, scale=XS).then_inc(s_ehi, 1)
                act_e.activation(e_hi[:, e, F:2 * F], stage[:, e % 2, F:2 * F], ACT.Copy,
                                 scale=low_rows[:, :]).then_inc(s_ehi, 1)
                act_e.activation(e_hi[:, e, 2 * F:WE], stage[:, e % 2, 2 * F:WE], ACT.Copy,
                                 scale=XS).then_inc(s_ehi, 1)
            act_e.activation(q_low[0:1, 0:1], ident[0:1, 0:1], ACT.Exp).then_inc(s_warm, 1)
            act_e.wait_ge(s_warm, 1)
            act_e.wait_ge(s_dconst, 1)

            def body(i, par):
                def exps(r):
                    if within(i, NT):
                        act_e.wait_ge(s_nmax, 4 * i + r + 1)
                        upto(act_e, s_PT[r], i)
                        for c in range(CH):
                            ins = act_e.activation(probs[:, r, c, :], bank[:, r, c * P:(c + 1) * P], ACT.Exp,
                                                   bias=negmax[:, r, c:c + 1], scale=SCORE)
                        ins.then_inc(s_P[r], 1)

                def evac_pt(r):
                    if within(i, NT):
                        act_e.wait_ge(s_PT[r], i + 1)
                        upto(act_e, s_O, i)
                        act_e.activation(probs_t[:, r, :, :].rearrange("p c k -> p (c k)"),
                                         bank[:, 4 + r % 2, 0:QC], ACT.Copy).then_inc(s_PTe[r], 1)

                exps(0)
                exps(1)
                if within(i + 1, NT + 2):
                    n = i + 2
                    act_e.wait_ge(s_T, n)
                    upto(act_e, s_VY, n - 1)
                    lo, hi = (0 if within(i + 1, NT) else DX), (2 * DX if within(i - 1, NT) else DX)
                    act_e.activation(t_hi[:, lo:hi], bank[:, T_BANK, lo:hi], ACT.Copy, scale=XS).then_inc(s_Thi, 1)
                exps(2)
                if within(i + 1, NT):
                    act_e.wait_ge(s_Q, i + 2)
                    upto(act_e, s_q, i + 1)
                    act_e.activation(q_low[:, :], bank[:, Q_BANK, 0:QC], ACT.Copy,
                                     scale=low_heads[:, :]).then_inc(s_qlow, 1)
                    act_e.wait_ge(s_K, i + 2)
                    act_e.activation(k_hi[:, 1 - par, :], bank[:, T_BANK, 0:QC], ACT.Copy,
                                     scale=UN * QS).then_inc(s_khi, 1)
                exps(3)
                evac_pt(0)
                evac_pt(2)
                if within(i - 2, NT):
                    act_e.wait_ge(s_X2, i - 1)
                    upto(act_e, s_L, i - 2)
                    act_e.activation(x2t[:, :], bank[:, T_BANK, 0:DX], ACT.Copy).then_inc(s_x2t, 1)

            steps(act_e, body)

            act_e.wait_ge(s_r, 3)
            act_e.activation(ex[:, :, :], lg[:, :, :], ACT.Exp).then_inc(s_ex, 1)
            act_e.wait_ge(s_pmT, 1)
            act_e.activation(pmt[:, :], bank[0:NT, 2, 0:P], ACT.Copy).then_inc(s_pmt, 1)
            act_e.activation(q_low[0:1, 0:1], ident[0:1, 0:1], ACT.Gelu).then_inc(s_warm, 1)
            act_e.wait_ge(s_warm, 2)

            def tiles(t, par, ranks=False):
                if within(t, TT):
                    if isinstance(t, int) and t in (0, TC):
                        act_e.wait_ge(s_route, 1 + (t == TC))
                    e = act_e.value_load(experts[0:1, ds(t, 1)], min_val=0, max_val=2 * E - 1)
                    upto(act_e, s_glo, 2 * (t - 1))
                    for half in range(2):
                        act_e.wait_ge(s_H[half], t + 1)
                        for f in range(half * 3, half * 3 + 3):
                            ins = act_e.activation(
                                act[:, par, f * P:(f + 1) * P],
                                bank[:, 2 * par + half, (f % 3) * P:(f % 3 + 1) * P],
                                ACT.Gelu, bias=b1_sb[:, ds(e, 1), f:f + 1].rearrange("p a b -> p (a b)"),
                                scale=UN)
                        ins.then_inc(s_g[half], 1)
                if within(t + 1, TT):
                    act_e.wait_ge(s_XT, t + 2)
                    upto(act_e, s_H[1], t)
                    act_e.activation(xg_hi[:, 1 - par, :], bank[:, 4, 0:DX], ACT.Copy, scale=XS).then_inc(s_xhi, 1)

            slot_steps(act_e, tiles, {})

        @block.vector
        def _(dve):
            stt = dve.scalar_tensor_tensor
            dve.wait_ge(s_const, 5)
            dve.tensor_scalar(low_heads_i[:, :], low_heads_i[:, :], HD, None, ALU.bitwise_and).then_inc(s_r, 1)
            dve.wait_ge(s_r, 1)
            dve.memset(v_sb[:, :, :, HD:HD + 1], 1.0).then_inc(s_v, 1)
            dve.wait_ge(s_v, 1)
            dve.tensor_scalar(low_heads[:, :], low_heads_i[:, :], UN * QS / HD, None, ALU.mult).then_inc(s_dconst, 1)
            dve.wait_ge(s_whi, 1)
            stt(out=w_lo[:, :], in0=stage[:, 0, 0:AC], scalar=XS, in1=w_hi[:, :], op0=ALU.mult,
                op1=ALU.subtract).then_inc(s_wsplit, 1)
            dve.wait_ge(s_whi, 2)
            stt(out=w_mix[:, :], in0=stage[:, 1, 0:AC], scalar=XS, in1=w_tmp[:, :], op0=ALU.mult,
                op1=ALU.subtract).then_inc(s_wsplit, 1)
            for e in range(2 * E):
                dve.wait_ge(s_ehi, 3 * (e + 1))
                stt(out=e_lo[:, e, :], in0=stage[:, e % 2, :], scalar=XS, in1=e_hi[:, e, :],
                    op0=ALU.mult, op1=ALU.subtract).then_inc(s_esplit, 1)

            def norm_stats(n, source, ready, count):
                dve.wait_ge(ready, count)
                alone(dve, s_past_dve)
                dve.bn_stats(out=stats[:, n, :], in_=source).then_inc(s_st[n], 1)
                dve.wait_ge(s_st[n], count)
                alone(dve, s_past_dve)
                dve.bn_aggr(out=mv[:, n, :], in_=stats[:, n, :]).then_inc(s_mv[n], 1)

            def body(i, par):
                j, k = i + 2, i + 1

                def maxima(r):
                    if within(i, NT):
                        dve.wait_ge(s_S[r], i + 1)
                        dve.tensor_reduce(rawmax[:, r, :],
                                          bank[:, r, 0:QC].rearrange("p (c k) -> p c k", c=CH),
                                          AX, ALU.max, negate=True).then_inc(s_max, 1)

                def scaled(r):
                    if within(i, NT):
                        dve.wait_ge(s_max, 4 * i + r + 1)
                        upto(dve, s_P[r], i)
                        dve.tensor_scalar(negmax[:, r, :], rawmax[:, r, :], SCORE, None,
                                          ALU.mult).then_inc(s_nmax, 1)

                def evac_pt(r):
                    if within(i, NT):
                        dve.wait_ge(s_PT[r], i + 1)
                        upto(dve, s_O, i)
                        dve.tensor_copy(probs_t[:, r, :, :].rearrange("p c k -> p (c k)"),
                                        bank[:, 4 + r % 2, 0:QC]).then_inc(s_PTe[r], 1)

                maxima(0)
                maxima(1)
                scaled(0)
                scaled(1)
                if within(j, NT):
                    norm_stats(0, we[:, par, :], s_e, j + 1)
                if within(i + 1, NT + 2):
                    n = i + 2
                    dve.wait_ge(s_Thi, n)
                    lo, hi = (0 if within(i + 1, NT) else DX), (2 * DX if within(i - 1, NT) else DX)
                    stt(out=t_lo[:, lo:hi], in0=bank[:, T_BANK, lo:hi], scalar=XS, in1=t_hi[:, lo:hi],
                        op0=ALU.mult, op1=ALU.subtract).then_inc(s_Tlo, 1)
                maxima(2)
                maxima(3)
                scaled(2)
                scaled(3)
                if within(j, NT):
                    dve.wait_ge(s_rs[0], j + 1)
                    upto(dve, s_hg, j)
                    dve.tensor_scalar(h1[:, :], we[:, par, :], mv[:, 0, 0:1], rstd[:, 0, :], ALU.subtract,
                                      ALU.mult).then_inc(s_h1, 1)
                if within(k, NT):
                    dve.wait_ge(s_qlow, k + 1)
                    upto(dve, s_S[RG - 1], k - 1)
                    stt(out=q_sb[:, 1 - par, :], in0=bank[:, Q_BANK, 0:QC], scalar=UN * QS, in1=q_low[:, :],
                        op0=ALU.mult, op1=ALU.subtract).then_inc(s_q, 1)
                    dve.wait_ge(s_khi, k + 1)
                    stt(out=k_lo[:, 1 - par, :], in0=bank[:, T_BANK, 0:QC], scalar=UN * QS,
                        in1=k_hi[:, 1 - par, :], op0=ALU.mult, op1=ALU.subtract).then_inc(s_klo, 1)
                evac_pt(1)
                if within(k, NT + 2):
                    dve.wait_ge(s_VY, i + 2)
                if within(k, NT):
                    upto(dve, s_O, i)
                    dve.tensor_scalar(v_sb[:, 1 - par, :, 0:HD],
                                      bank[:, Q_BANK, 0:D].rearrange("p (h e) -> p h e", h=HEADS),
                                      UN * VS, None, ALU.mult).then_inc(s_v, 1)
                if within(i - 1, NT):
                    dve.wait_ge(s_hb, i)
                    stt(out=wide(h2[:, ds(i - 1, 1), :]), in0=bank[:, Q_BANK, D:2 * D], scalar=UN / VS,
                        in1=wide(hb[:, ds((i - 1) % 4, 1), :]), op0=ALU.mult, op1=ALU.add).then_inc(s_h2, 1)
                    norm_stats(2, wide(h2[:, ds(i - 1, 1), :]), s_h2, i)
                if within(j, NT):
                    norm_stats(1, h[:, par, :], s_h, j + 1)
                evac_pt(3)
                if within(i - 1, NT):
                    dve.wait_ge(s_rs[2], i)
                    upto(dve, s_X2, i - 2)
                    upto(dve, s_x, 16 * (i - 2))
                    for lo, hi, at in ((0, D, 0), (P, D, D)):
                        dve.tensor_scalar(xn2[:, 1 - par, at:at + hi - lo],
                                          wide(h2[:, ds(i - 1, 1), lo:hi]), mv[:, 2, 0:1], rstd[:, 2, :],
                                          ALU.subtract, ALU.mult).then_inc(s_xn2, 1)
                if within(j, NT):
                    dve.wait_ge(s_rs[1], j + 1)
                    upto(dve, s_T, j - 1)
                    for lo, hi, at in ((0, D, 0), (P, D, D)):
                        dve.tensor_scalar(xn[:, par, at:at + hi - lo], h[:, par, lo:hi], mv[:, 1, 0:1],
                                          rstd[:, 1, :], ALU.subtract, ALU.mult).then_inc(s_xn, 1)
                if within(i - 2, NT):
                    dve.wait_ge(s_L, i - 1)
                    dve.tensor_copy(wide(logits[:, ds(i - 2, 1), :]),
                                    bank[:, T_BANK, DX:DX + 2 * E]).then_inc(s_lg, 1)
                if within(i, NT):
                    dve.wait_ge(s_O, i + 1)
                    o = bank[:, Q_BANK, 0:HEADS * (HD + 1)].rearrange("p (h e) -> p h e", h=HEADS)
                    dve.reciprocal(rden[:, :, :], o[:, :, HD:HD + 1]).then_inc(s_rd, 1)
                    dve.wait_ge(s_rd, i + 1)
                    upto(dve, s_T, i + 1)
                    for h0, at in ((0, 0), (P // HD, D)):
                        n = HEADS - h0
                        dve.tensor_tensor(att[:, at:at + n * HD].rearrange("p (h e) -> p h e", h=n),
                                          o[:, h0:HEADS, 0:HD], rden[:, h0:HEADS, :].broadcast_to([P, n, HD]),
                                          ALU.mult).then_inc(s_att, 1)

            steps(dve, body)

            count = [1]

            def own(ins):
                count[0] += 1
                ins.then_inc(s_r, 1)
                dve.wait_ge(s_r, count[0])

            dve.wait_ge(s_lg, NT)
            dve.wait_ge(s_biases, 16 * 4)
            by_router = logits[:, :, :].rearrange("p i (r e) -> p (i r) e", r=2)
            spread = lambda t, n: t.unsqueeze(2).broadcast_to([P, n, E])
            own(dve.tensor_tensor(logits[:, :, :], logits[:, :, :],
                                  br_sb[:, :].unsqueeze(1).broadcast_to([P, NT, 2 * E]), ALU.add))
            dve.tensor_reduce(top[:, :], by_router, AX, ALU.max).then_inc(s_rd, 1)
            dve.wait_ge(s_rd, NT + 1)
            own(dve.tensor_tensor(lg[:, :, :], by_router, spread(top[:, :], R2), ALU.subtract))
            dve.wait_ge(s_ex, 1)
            own(dve.tensor_reduce(den[:, :], ex[:, :, :], AX, ALU.add))
            own(dve.reciprocal(rec[:, :], den[:, :]))
            own(dve.tensor_tensor(pr[:, :, :], ex[:, :, :], spread(rec[:, :], R2), ALU.mult))
            own(dve.tensor_reduce(pmax[:, :], pr[:, :, :], AX, ALU.max))
            common = pmax[:, :].rearrange("p (i r) -> p i r", r=2)[:, :, 0]
            dve.tensor_copy(pm_c[:, :], common).then_inc(s_pmc, 1)
            own(dve.tensor_tensor(eq[:, :, :], pr[:, :, :], spread(pmax[:, :], R2), ALU.is_equal))
            own(dve.tensor_copy(oh[:, :, 0], eq[:, :, 0]))
            seen_at = eq[:, :, 0]
            for e in range(1, E):
                own(dve.tensor_tensor(oh[:, :, e], eq[:, :, e], seen_at, ALU.is_gt))
                if e < E - 1:
                    own(dve.tensor_tensor(seen[:, e % 2, :], eq[:, :, e], seen_at, ALU.max))
                    seen_at = seen[:, e % 2, :]
            own(dve.reciprocal(pm_rec[:, :], pmax[:, :]))
            own(dve.tensor_tensor(scale[:, :], pmax[:, :], pm_rec[:, :], ALU.mult))
            own(dve.memset(cum[:, :, 0:NT, :], 0.0))
            own(dve.memset(ends[:, :, 0:E], 0.0))
            dve.wait_ge(s_const, N_CONST)
            oh_r = oh[:, :, :].rearrange("p (i r) e -> p i r e", r=2)
            scale_r = scale[:, :].rearrange("p (i r) -> p i r", r=2)

            def route_in(u):
                if u == 0:
                    dve.tensor_copy(ohx[:, :, :], oh_r[:, :, 0, :]).then_inc(s_ohx, 1)
                    return
                dve.wait_ge(s_cnt, NT)
                own(dve.tensor_tensor(rank4[:, :, :], bank[:, 6, 0:NT * E].rearrange("p (i e) -> p i e", e=E),
                                      oh_r[:, :, 0, :], ALU.mult))
                own(dve.tensor_reduce(rank[:, :], rank4[:, :, :], AX, ALU.add))
                own(dve.tensor_scalar(dropped[:, :], rank[:, :], float(CAP), None, ALU.is_ge))
                dve.tensor_tensor(ohx[:, :, :], oh_r[:, :, 1, :], spread(dropped[:, :], NT),
                                  ALU.mult).then_inc(s_ohx, 1)

            def route_slots(u):
                n_t, t0 = (TC, 0) if u == 0 else (TU, TC)
                pre = bank[:, 7, 0:NT * E].rearrange("p (i e) -> p i e", e=E)
                sums = bank[:, 7, NT * E:2 * NT * E].rearrange("p (i e) -> p i e", e=E)
                dve.wait_ge(s_pre, u + 1)
                own(dve.tensor_copy(cum[:, 0, NT:, :], sums))
                at = 0
                for step in (1, 2, 4, 8):
                    own(dve.tensor_tensor(cum[:, 1 - at, NT:, :], cum[:, at, NT:, :],
                                          cum[:, at, NT - step:2 * NT - step, :], ALU.add))
                    at = 1 - at
                own(dve.tensor_scalar(tot[:, :], cum[:, at, 2 * NT - 1, :], float(P - 1), None, ALU.add))
                own(dve.tensor_copy(tiles_i[:, :], tot[:, :]))
                own(dve.tensor_scalar(tiles_i[:, :], tiles_i[:, :], 7, None, ALU.logical_shift_right))
                own(dve.tensor_copy(ends[:, 0, E:], tiles_i[:, :]))
                own(dve.tensor_tensor(ends[:, 1, E:], ends[:, 0, E:], ends[:, 0, E - 1:2 * E - 1], ALU.add))
                own(dve.tensor_tensor(ends[:, 2, E:], ends[:, 1, E:], ends[:, 1, E - 2:2 * E - 2], ALU.add))
                own(dve.tensor_tensor(ge[:, 0:n_t, :], iota_t[:, 0:n_t].unsqueeze(2).broadcast_to([P, n_t, E - 1]),
                                      ends[:, 2, E:2 * E - 1].unsqueeze(1).broadcast_to([P, n_t, E - 1]), ALU.is_ge))
                own(dve.tensor_reduce(tile_e[:, 0:n_t], ge[:, 0:n_t, :], AX, ALU.add))
                own(dve.tensor_scalar(experts[0:1, t0:t0 + n_t], tile_e[0:1, 0:n_t], float(E * u), None, ALU.add))
                own(dve.tensor_tensor(posn[:, :, :], pre, cum[:, at, NT - 1:2 * NT - 1, :], ALU.add))
                own(stt(out=pos2[:, :, :], in0=ends[:, 2, E - 1:2 * E - 1].unsqueeze(1).broadcast_to([P, NT, E]),
                        scalar=float(P), in1=posn[:, :, :], op0=ALU.mult, op1=ALU.add))
                own(dve.tensor_tensor(pos3[:, :, :], pos2[:, :, :], ohx[:, :, :], ALU.mult))
                own(dve.tensor_reduce(slot[:, :], pos3[:, :, :], AX, ALU.add))
                own(dve.tensor_reduce(valid[:, :], ohx[:, :, :], AX, ALU.add))
                own(dve.tensor_copy(slot_i[:, :], slot[:, :]))
                own(dve.tensor_scalar(slot_hi[:, :], slot_i[:, :], 7, None, ALU.logical_shift_right))
                own(dve.tensor_scalar(slot_lo[:, :], slot_i[:, :], P - 1, None, ALU.bitwise_and))
                own(dve.tensor_copy(slot_hf[:, :], slot_hi[:, :]))
                own(dve.tensor_copy(slot_lf[:, :], slot_lo[:, :]))
                own(dve.tensor_tensor(tokv[:, :], token1[:, :], valid[:, :], ALU.mult))
                own(dve.tensor_tensor(scv[:, :], scale_r[:, :, u], valid[:, :], ALU.mult))
                own(dve.tensor_tensor(oh_t[:, :, 0:n_t], slot_hf[:, :].unsqueeze(2).broadcast_to([P, NT, n_t]),
                                      iota_t[:, 0:n_t].unsqueeze(1).broadcast_to([P, NT, n_t]), ALU.is_equal))
                own(dve.tensor_tensor(oh_m[:, :, 0, 0:n_t], oh_t[:, :, 0:n_t],
                                      tokv[:, :].unsqueeze(2).broadcast_to([P, NT, n_t]), ALU.mult))
                own(dve.tensor_tensor(oh_m[:, :, 1, 0:n_t], oh_t[:, :, 0:n_t],
                                      scv[:, :].unsqueeze(2).broadcast_to([P, NT, n_t]), ALU.mult))
                dve.tensor_tensor(oh_s[:, :, :], slot_lf[:, :].unsqueeze(2).broadcast_to([P, NT, P]),
                                  iota_s[:, :].unsqueeze(1).broadcast_to([P, NT, P]), ALU.is_equal).then_inc(s_perm, 1)

            def route_out(u):
                n_t, t0 = (TC, 0) if u == 0 else (TU, TC)
                dve.wait_ge(s_inv, u + 1)
                own(dve.tensor_copy(inv[:, :, 0:n_t],
                                    bank[:, 7, 256:256 + 2 * n_t].rearrange("p (a t) -> p a t", a=2)))
                own(dve.tensor_scalar(empty[:, 0:n_t], inv[:, 0, 0:n_t], 0.0, float(2 * N), ALU.is_equal, ALU.mult))
                own(stt(out=out_f[:, 0:n_t], in0=inv[:, 0, 0:n_t], scalar=-1.0, in1=empty[:, 0:n_t],
                        op0=ALU.add, op1=ALU.add))
                own(dve.tensor_copy(idx_out[:, t0:t0 + n_t], out_f[:, 0:n_t]))
                own(dve.tensor_copy(slot_scale[:, t0:t0 + n_t], inv[:, 1, 0:n_t]))
                dve.tensor_scalar(idx_in[:, t0:t0 + n_t], inv[:, 0, 0:n_t], -1.0, 0.0, ALU.add,
                                  ALU.max).then_inc(s_route, 1)

            route_in(0)
            route_slots(0)
            route_out(0)

            def tiles(t, par, ranks=False):
                if ranks and within(t, NT):
                    if isinstance(t, int) and t == 0:
                        dve.wait_ge(s_pm_ld, 16)
                        dve.wait_ge(s_dconst, 2)
                    upto(dve, s_cnt, t - 1)
                    stt(out=less[:, par, :], in0=prow[:, :], scalar=pm_c[:, ds(t, 1)],
                        in1=tie[:, ds(N - P - t * P, N)], op0=ALU.subtract, op1=ALU.is_lt).then_inc(s_less, 1)
                if within(t, TT):
                    for half in range(2):
                        cols = slice(half * (F // 2), (half + 1) * (F // 2))
                        dve.wait_ge(s_g[half], t + 1)
                        upto(dve, s_Y, t - 1)
                        dve.tensor_scalar(act_hi[:, par, cols], act[:, par, cols], GS, None,
                                          ALU.mult).then_inc(s_ghi, 1)
                        dve.wait_ge(s_ghi, 2 * t + half + 1)
                        stt(out=act_lo[:, par, cols], in0=act[:, par, cols], scalar=GS, in1=act_hi[:, par, cols],
                            op0=ALU.mult, op1=ALU.subtract).then_inc(s_glo, 1)
                if within(t + 1, TT):
                    dve.wait_ge(s_xhi, t + 2)
                    stt(out=xg_lo[:, 1 - par, :], in0=bank[:, 4, 0:DX], scalar=XS, in1=xg_hi[:, 1 - par, :],
                        op0=ALU.mult, op1=ALU.subtract).then_inc(s_xlo, 1)
                if within(t - 2, TT):
                    o = t - 2
                    e = dve.value_load(experts[0:1, ds(o, 1)], min_val=0, max_val=2 * E - 1)
                    dve.wait_ge(s_Y, o + 1)
                    upto(dve, s_y, o)
                    stt(out=yb[:, :], in0=bank[:, 5, 0:D], scalar=1.0 / (XS * GS),
                        in1=wide(b2_sb[:, ds(e, 1), :]), op0=ALU.mult, op1=ALU.add).then_inc(s_yb, 1)
                    dve.wait_ge(s_yb, o + 1)
                    upto(dve, s_scatter, 16 * (o - 1))
                    dve.tensor_scalar(y[:, par, :], yb[:, :], slot_scale[:, ds(o, 1)], None,
                                      ALU.mult).then_inc(s_y, 1)

            def second_slots():
                route_in(1)
                route_slots(1)

            slot_steps(dve, tiles, {NT: second_slots, NT + 1: lambda: route_out(1)})

        @block.tensor
        def _(pe):
            pe.wait_ge(s_const, 5)
            pe.wait_ge(s_wsplit, 2)

            def five(out_ap, terms):
                for n, (lhs, rhs) in enumerate(terms):
                    ins = pe.matmul(out_ap, lhs, rhs, start=(n == 0), stop=(n == 4))
                return ins

            def parts(col, n):
                return w_hi[:, col:col + n], w_lo[:, col:col + n], w_mix[:, col:col + n]

            def body(i, par):
                k = i + 1
                if within(i, NT):
                    pe.wait_ge(s_q, i + 1)
                    pe.wait_ge(s_klo, i + 1)
                    for r in range(RG):
                        upto(pe, s_P[r], i)
                        rows = slice(32 * r, 32 * r + 32)
                        for c in range(CH):
                            cols = slice(c * P, (c + 1) * P)
                            pe.matmul(bank[:, r, cols], q_sb[rows, par, cols], k_hi[rows, par, cols],
                                      start=True, stop=False)
                            ins = pe.matmul(bank[:, r, cols], q_sb[rows, par, cols], k_lo[rows, par, cols],
                                            start=False, stop=True)
                        ins.then_inc(s_S[r], 1)
                if within(k, NT + 2):
                    upto(pe, s_lg, i - 2)
                    if within(k, NT):
                        pe.wait_ge(s_xn, 2 * k + 2)
                        for a in range(2):
                            ins = pe.transpose(bank[:, T_BANK, a * P:(a + 1) * P],
                                               xn[:, 1 - par, a * P:(a + 1) * P], ident[:, :])
                    if within(i - 1, NT):
                        pe.wait_ge(s_att, 2 * i)
                        for a in range(2):
                            ins = pe.transpose(bank[:, T_BANK, DX + a * P:DX + (a + 1) * P],
                                               att[:, a * P:(a + 1) * P], ident[:, :])
                    ins.then_inc(s_T, 1)
                    pe.wait_ge(s_Tlo, i + 2)
                if within(k, NT):
                    upto(pe, s_att, 2 * i)
                    x0h, x1h = t_hi[:, 0:P], t_hi[:, P:DX]
                    x0l, x1l = t_lo[:, 0:P], t_lo[:, P:DX]
                    for base, b, done in ((0, Q_BANK, s_Q), (QC, T_BANK, s_K)):
                        for c in range(CH):
                            hi, lo, mix = parts(base + c * P, P)
                            ins = five(bank[:, b, c * P:(c + 1) * P],
                                       ((hi, x0h), (lo, x0h), (hi, x0l), (mix, x1h), (mix, x1l)))
                        ins.then_inc(done, 1)

                def transposes(r):
                    pe.wait_ge(s_P[r], i + 1)
                    if r < 2:
                        upto(pe, s_PTe[r + 2], i)
                    else:
                        pe.wait_ge(s_PTe[r - 2], i + 1)
                    for c in range(CH):
                        ins = pe.transpose(bank[:, 4 + r % 2, c * P:(c + 1) * P], probs[:, r, c, :], ident[:, :])
                    ins.then_inc(s_PT[r], 1)

                def weighted(r):
                    pe.wait_ge(s_PTe[r], i + 1)
                    for c in range(CH):
                        hd = RG * c + r
                        ins = pe.matmul(bank[:, Q_BANK, hd * (HD + 1):(hd + 1) * (HD + 1)], probs_t[:, r, c, :],
                                        v_sb[:, par, hd, :], start=True, stop=True)
                    return ins

                if within(i, NT):
                    transposes(0)
                    transposes(1)
                if within(k, NT + 2):
                    ins = None
                    if within(k, NT):
                        pe.wait_ge(s_q, k + 1)
                        hi, lo, mix = parts(2 * QC, D)
                        ins = five(bank[:, Q_BANK, 0:D],
                                   ((x0h, hi), (x0h, lo), (x0l, hi), (x1h, mix), (x1l, mix)))
                    if within(i - 1, NT):
                        a0h, a1h = t_hi[:, DX:DX + P], t_hi[:, DX + P:]
                        a0l, a1l = t_lo[:, DX:DX + P], t_lo[:, DX + P:]
                        hi, lo, mix = parts(2 * QC + D, D)
                        ins = five(bank[:, Q_BANK, D:2 * D],
                                   ((a0h, hi), (a0h, lo), (a0l, hi), (a1h, mix), (a1l, mix)))
                    ins.then_inc(s_VY, 1)
                if within(i - 2, NT):
                    if within(k, NT):
                        pe.wait_ge(s_klo, k + 1)
                    upto(pe, s_lg, i - 2)
                    upto(pe, s_xn2, 2 * (i - 1))
                    for a in range(2):
                        ins = pe.transpose(bank[:, T_BANK, a * P:(a + 1) * P],
                                           xn2[:, par, a * P:(a + 1) * P], ident[:, :])
                    ins.then_inc(s_X2, 1)
                if within(i, NT):
                    pe.wait_ge(s_v, i + 2)
                    if within(k, NT):
                        pe.wait_ge(s_v, k + 2)
                    upto(pe, s_h2, i)
                    weighted(0)
                    transposes(2)
                    weighted(1)
                    transposes(3)
                    weighted(2)
                    weighted(3).then_inc(s_O, 1)
                if within(i - 2, NT):
                    pe.wait_ge(s_x2t, i - 1)
                    pe.matmul(bank[:, T_BANK, DX:DX + 2 * E], x2t[:, 0:P], wr_sb[:, 0, :], start=True, stop=False)
                    pe.matmul(bank[:, T_BANK, DX:DX + 2 * E], x2t[0:D2, P:DX], wr_sb[0:D2, 1, :],
                              start=False, stop=True).then_inc(s_L, 1)

            pe.wait_ge(s_biases, 16 * 4)
            steps(pe, body)

            pe.wait_ge(s_pmc, 1)
            pe.transpose(bank[0:NT, 2, 0:P], pm_c[:, :], ident[:, :]).then_inc(s_pmT, 1)

            def counts(u):
                pe.wait_ge(s_ohx, u + 1)
                flat = ohx[:, :, :].rearrange("p i e -> p (i e)")
                pe.matmul(bank[:, 7, 0:NT * E], before[:, :], flat, start=True, stop=True)
                pe.matmul(bank[:, 7, NT * E:2 * NT * E], ones[:, :], flat, start=True, stop=True).then_inc(s_pre, 1)

            def invert(u):
                n_t = TC if u == 0 else TU
                pe.wait_ge(s_perm, u + 1)
                at = bank[:, 7, 256:256 + 2 * n_t].rearrange("p (a t) -> p a t", a=2)
                for n in range(NT):
                    ins = pe.matmul(at, oh_s[:, n, :], oh_m[:, n, :, 0:n_t], start=(n == 0), stop=(n == NT - 1))
                ins.then_inc(s_inv, 1)

            counts(0)
            invert(0)

            pe.wait_ge(s_esplit, 2 * E)
            pe.wait_ge(s_route, 1)
            pe.wait_ge(s_pmt, 1)

            def tiles(t, par, ranks=False):
                if within(t, TT):
                    e = pe.value_load(experts[0:1, ds(t, 1)], min_val=0, max_val=2 * E - 1)
                    x0h, x1h = xg_hi[:, par, 0:P], xg_hi[:, par, P:DX]
                    x0l, x1l = xg_lo[:, par, 0:P], xg_lo[:, par, P:DX]
                    pe.wait_ge(s_xlo, t + 1)
                    for half in range(2):
                        upto(pe, s_g[half], t - 1)
                        for f in range(3 * half, 3 * half + 3):
                            def w(src, part, f=f):
                                return wide(src[:, ds(e, 1), part * F + f * P:part * F + (f + 1) * P])
                            ins = five(bank[:, 2 * par + half, (f % 3) * P:(f % 3 + 1) * P],
                                       ((w(e_hi, 0), x0h), (w(e_lo, 0), x0h), (w(e_hi, 0), x0l),
                                        (w(e_lo, 1), x1h), (w(e_lo, 1), x1l)))
                        ins.then_inc(s_H[half], 1)
                if within(t + 1, TT):
                    pe.wait_ge(s_gather, 16 * (t + 2))
                    upto(pe, s_xlo, t + 1)
                    for a in range(2):
                        ins = pe.transpose(bank[:, 4, a * P:(a + 1) * P], xg[:, 1 - par, a * P:(a + 1) * P],
                                           ident[:, :])
                    ins.then_inc(s_XT, 1)
                if ranks and within(t - 1, NT):
                    b = t - 1
                    first = isinstance(b, int) and b == 0
                    pe.wait_ge(s_less, b + 1)
                    for n in range(NT):
                        ins = pe.matmul(bank[:, 6, n * E:(n + 1) * E], less[:, 1 - par, n * P:(n + 1) * P],
                                        wide(oh[:, ds(2 * b, 1), :]), start=(first and n == 0), stop=False,
                                        skip_group_check=True)
                    ins.then_inc(s_cnt, 1)
                if within(t - 2, TT):
                    o = t - 2
                    e2 = pe.value_load(experts[0:1, ds(o, 1)], min_val=0, max_val=2 * E - 1)
                    pe.wait_ge(s_glo, 2 * (o + 1))
                    upto(pe, s_yb, o)
                    for c in range(FC):
                        ah, al = act_hi[:, par, c * P:(c + 1) * P], act_lo[:, par, c * P:(c + 1) * P]
                        cols = slice(2 * F + c * D, 2 * F + (c + 1) * D)
                        wh, wl = wide(e_hi[:, ds(e2, 1), cols]), wide(e_lo[:, ds(e2, 1), cols])
                        pe.matmul(bank[:, 5, 0:D], ah, wh, start=(c == 0), stop=False)
                        pe.matmul(bank[:, 5, 0:D], ah, wl, start=False, stop=False)
                        ins = pe.matmul(bank[:, 5, 0:D], al, wh, start=False, stop=(c == FC - 1))
                    ins.then_inc(s_Y, 1)

            def last_rank():
                b = NT - 1
                pe.wait_ge(s_less, b + 1)
                for n in range(NT):
                    ins = pe.matmul(bank[:, 6, n * E:(n + 1) * E], less[:, b % 2, n * P:(n + 1) * P],
                                    oh[:, 2 * b, :], start=False, stop=True, skip_group_check=True)
                ins.then_inc(s_cnt, 1)
                counts(1)

            slot_steps(pe, tiles, {NT: last_rank, NT + 1: lambda: invert(1)})


_ORDER = ["ids", "types", "word", "pos", "type_emb", "gamma", "beta", "wqkvp", "b_proj", "wr", "br",
          "wexp", "b1", "b2"]


def kernel(**inputs):
    import numpy as np
    import concourse.bacc as bacc
    from concourse import mybir as mb
    from concourse.bass_utils import run_bass_kernel_spmd as run

    a = {k: np.asarray(v) for k, v in inputs.items()}
    laid = {}
    laid["ids"] = a["x"].T
    laid["types"] = a["mask_BS_i1_0"].T
    laid["word"] = a["L0_tok_word_emb"]
    laid["pos"] = a["L0_tok_pos_emb"][:P]
    laid["type_emb"] = a["L0_tok_type_emb"]
    laid["gamma"] = a["L0_tok_ln_gamma"][None]
    laid["beta"] = a["L0_tok_ln_beta"][None]
    laid["b_proj"] = a["L0_attn_b_proj"][None]

    def halves(w):
        return np.stack([w[:P], np.concatenate([w[P:], w[P:]])])

    w = a["L0_attn_w_qkv"].T
    twice = [np.repeat(w[:, n * D:(n + 1) * D].reshape(D, HEADS, 1, HD), 2, axis=2).reshape(D, QC)
             for n in range(2)]
    laid["wqkvp"] = halves(np.concatenate(twice + [w[:, 2 * D:], a["L0_attn_w_proj"].T], axis=1))
    wr = np.concatenate([a["L0_ffn_Wsc"], a["L0_ffn_Wsu"]], axis=1)
    laid["wr"] = halves(wr).transpose(1, 0, 2)
    laid["br"] = np.concatenate([a["L0_ffn_bsc"], a["L0_ffn_bsu"]])[None]
    w1 = np.concatenate([a["L0_ffn_W1c"], a["L0_ffn_W1u"]])
    w2 = np.concatenate([a["L0_ffn_W2c"], a["L0_ffn_W2u"]])
    laid["wexp"] = np.stack([
        np.concatenate([*halves(w1[e]), w2[e].reshape(FC, P, D).transpose(1, 0, 2).reshape(P, FC * D)], axis=1)
        for e in range(2 * E)])
    laid["b1"] = np.concatenate([a["L0_ffn_b1c"], a["L0_ffn_b1u"]]).reshape(2 * E, FC, P).transpose(2, 0, 1)
    laid["b2"] = np.concatenate([a["L0_ffn_b2c"], a["L0_ffn_b2u"]]).reshape(1, 2 * E * D)

    nc = bacc.Bacc("TRN2", target_bir_lowering=False, num_devices=1)
    arrays, args = {}, []
    for name in _ORDER:
        arrays[f"in_{name}"] = np.ascontiguousarray(laid[name])
        args.append(nc.dram_tensor(f"in_{name}", laid[name].shape, mb.dt.from_np(laid[name].dtype),
                                   kind="ExternalInput").ap())
    args.append(nc.dram_tensor("xrows", (N, DX), mb.dt.float32).ap())
    args.append(nc.dram_tensor("prow_dram", (N,), mb.dt.float32).ap())
    out = nc.dram_tensor("out_0", (N, D), mb.dt.float32, kind="ExternalOutput").ap()
    build(nc, *args, out)
    got = run(nc, [arrays], core_ids=[0]).results[0]["out_0"]
    return got.reshape(SEQS, P, D)
```

```python
from contextlib import ExitStack

import concourse.bass as bass
from concourse import mybir

F32 = mybir.dt.float32
F16 = mybir.dt.float16
BF16 = mybir.dt.bfloat16
I32 = mybir.dt.int32
ALU = mybir.AluOpType
ACT = mybir.ActivationFunctionType
AX = mybir.AxisListType.X
ds = bass.ds

P = 128
SEQS = 16
NT = SEQS
N = NT * P
D = 192
D2 = D - P
DX = 2 * P
HEADS = 12
HD = D // HEADS
RG = 4
CH = HEADS // RG
QC = CH * P
F = 768
FC = F // P
E = 4
CAP = N // E
TC = NT + E - 1
TU = (N - CAP) // P + E - 1
TT = TC + TU
EPS = 1e-5

XS = 2.0 ** 11
QS = 2.0 ** 4
VS = 2.0 ** -3
GS = 2.0 ** 6
UN = 1.0 / (XS * XS)
SCORE = HD ** -0.5 / (QS * QS)
TIE = 2.0 ** -28
WE = 2 * F + FC * D


def upto(engine, semaphore, count):
    if not isinstance(count, int) or count > 0:
        engine.wait_ge(semaphore, count)


def alone(engine, passed):
    engine.sem_inc(passed, 1)


def clip(count, most):
    return min(count, most) if isinstance(count, int) else count


def within(i, n):
    return not isinstance(i, int) or 0 <= i < n


def build(nc, ids, types, word, pos, type_emb, gamma, beta, wqkvp, b_proj,
          wr, br, wexp, b1, b2, xrows, prow_dram, out):
    with ExitStack() as ctx:
        def sb(name, shape, dt):
            return ctx.enter_context(nc.sbuf_tensor(name, shape, dt))

        def sem(name):
            return ctx.enter_context(nc.semaphore(name))

        ident = sb("ident", [P, P], F32)
        before = sb("before", [P, P], F16)
        ones = sb("ones", [P, P], F16)
        low_rows = sb("low_rows", [P, 1], F32)
        low_heads_i = sb("low_heads_i", [P, 1], I32)
        low_heads = sb("low_heads", [P, 1], F32)
        minus_half = sb("minus_half", [P, 1], F32)
        iota_s = sb("iota_s", [P, P], F32)
        iota_t = sb("iota_t", [P, TC], F32)
        token1 = sb("token1", [P, NT], F32)
        tie = sb("tie", [P, 2 * N - P], BF16)
        ids_sb = sb("ids_sb", [P, NT + 1], I32)
        types_sb = sb("types_sb", [P, NT + 1], I32)
        types_f = sb("types_f", [P, NT + 1], F32)
        pos_sb = sb("pos_sb", [P, D], F32)
        ty = sb("ty", [P, 2, D], F32)
        gamma_sb = sb("gamma_sb", [P, D], F32)
        beta_sb = sb("beta_sb", [P, D], F32)
        bproj_sb = sb("bproj_sb", [P, D], F32)
        wr_sb = sb("wr_sb", [P, 2, 2 * E], F32)
        br_sb = sb("br_sb", [P, 2 * E], F32)
        b1_sb = sb("b1_sb", [P, 2 * E, FC], F32)
        b2_sb = sb("b2_sb", [P, 2 * E, D], F32)
        AC = 2 * QC + D + D
        w_hi = sb("w_hi", [P, AC], F16)
        w_lo = sb("w_lo", [P, AC], F16)
        w_mix = sb("w_mix", [P, AC], F16)
        w_tmp = sb("w_tmp", [P, AC], F16)
        stage = sb("stage", [P, 2, WE], F32)
        e_hi = sb("e_hi", [P, 2 * E, WE], F16)
        e_lo = sb("e_lo", [P, 2 * E, WE], F16)
        piece_cols = ((0, 2 * F), (2 * F, WE))

        we = sb("we", [P, 2, D], F32)
        hg = sb("hg", [P, D], F32)
        h = sb("h", [P, 2, D], F32)
        hb = sb("hb", [P, 4, D], F32)
        stats = sb("stats", [P, 3, 6], F32)
        mv = sb("mv", [P, 3, 2], F32)
        vare = sb("vare", [P, 3, 1], F32)
        mneg = sb("mneg", [P, 3, 1], F32)
        rstd = sb("rstd", [P, 3, 1], F32)
        xn = sb("xn", [P, 2, DX], F32)
        att = sb("att", [P, DX], F32)
        t_hi = sb("t_hi", [P, 2 * DX], F16)
        t_lo = sb("t_lo", [P, 2 * DX], F16)
        q_low = sb("q_low", [P, QC], F16)
        q_sb = sb("q_sb", [P, 2, QC], F16)
        k_hi = sb("k_hi", [P, 2, QC], F16)
        k_lo = sb("k_lo", [P, 2, QC], F16)
        v_sb = sb("v_sb", [P, 2, HEADS, HD + 1], F32)
        rawmax = sb("rawmax", [P, RG, CH], F32)
        negmax = sb("negmax", [P, RG, CH], F32)
        probs = sb("probs", [P, RG, CH, P], F32)
        probs_t = sb("probs_t", [P, RG, CH, P], F32)
        rden = sb("rden", [P, HEADS, 1], F32)
        HS = F + 4 * DX + 3 * D
        hs = sb("hs", [P, HS], F32)
        h2 = hs[:, 0:2 * D].rearrange("p (a d) -> p a d", a=2)
        xn2 = sb("xn2", [P, 2, DX], F32)
        x2t = sb("x2t", [P, 2, P], F32)
        logits = sb("logits", [P, NT, 2 * E], F32)

        R2 = NT * 2
        top = sb("top", [P, R2], F32)
        lg = sb("lg", [P, R2, E], F32)
        ex = sb("ex", [P, R2, E], F32)
        den = sb("den", [P, R2], F32)
        rec = sb("rec", [P, R2], F32)
        pr = sb("pr", [P, R2, E], F32)
        pmax = sb("pmax", [P, R2], F32)
        eq = sb("eq", [P, R2, E], F32)
        seen = sb("seen", [P, 2, R2], F32)
        oh = sb("oh", [P, R2, E], F16)
        pm_rec = sb("pm_rec", [P, R2], F32)
        scale = sb("scale", [P, R2], F32)
        pm_c = sb("pm_c", [P, NT], F32)
        pmt = sb("pmt", [NT, P], F32)
        prow = sb("prow", [P, N], F32)
        less = sb("less", [P, 2, N], F16)
        rank4 = sb("rank4", [P, NT, E], F32)
        rank = sb("rank", [P, NT], F32)
        dropped = sb("dropped", [P, NT], F32)
        ohx = sb("ohx", [P, NT, E], F16)
        cum = sb("cum", [P, 2, 2 * NT, E], F32)
        tot = sb("tot", [P, E], F32)
        tiles_i = sb("tiles_i", [P, E], I32)
        ends = sb("ends", [P, 3, 2 * E], F32)
        ge = sb("ge", [P, TC, E - 1], F32)
        tile_e = sb("tile_e", [P, TC], F32)
        posn = sb("posn", [P, NT, E], F32)
        pos2 = sb("pos2", [P, NT, E], F32)
        pos3 = sb("pos3", [P, NT, E], F32)
        slot = sb("slot", [P, NT], F32)
        slot_i = sb("slot_i", [P, NT], I32)
        slot_hi = sb("slot_hi", [P, NT], I32)
        slot_lo = sb("slot_lo", [P, NT], I32)
        slot_hf = sb("slot_hf", [P, NT], F32)
        slot_lf = sb("slot_lf", [P, NT], F32)
        valid = sb("valid", [P, NT], F32)
        tokv = sb("tokv", [P, NT], F32)
        scv = sb("scv", [P, NT], F32)
        st = stage[:, :, :].rearrange("p a n -> p (a n)")
        oh_s = st[:, 0:N // 2].bitcast(F16).rearrange("p (t s) -> p t s", t=NT)
        at0 = N // 2 + 3 * F
        oh_t = st[:, at0:at0 + NT * TC].rearrange("p (i t) -> p i t", i=NT)
        oh_m = st[:, at0 + NT * TC:at0 + 2 * NT * TC].bitcast(F16).rearrange("p (i a t) -> p i a t", i=NT, a=2)
        inv = sb("inv", [P, 2, TC], F32)
        empty = sb("empty", [P, TC], F32)
        out_f = sb("out_f", [P, TC], F32)
        experts = sb("experts", [1, TT], I32)
        idx_in = sb("idx_in", [P, TT], I32)
        idx_out = sb("idx_out", [P, TT], I32)
        slot_scale = sb("slot_scale", [P, TT], F32)

        now_in = sb("now_in", [P, 2, 1], I32)
        now_out = sb("now_out", [P, 2, 1], I32)
        act = st[:, N // 2:N // 2 + 2 * F].rearrange("p (a f) -> p a f", a=2)
        act_hi = st[:, N // 2 + 2 * F:N // 2 + 3 * F].bitcast(F16).rearrange("p (a f) -> p a f", a=2)
        act_lo = hs[:, 0:F].bitcast(F16).rearrange("p (a f) -> p a f", a=2)
        xg = hs[:, F:F + 2 * DX].rearrange("p (a d) -> p a d", a=2)
        xg_hi = hs[:, F + 2 * DX:F + 3 * DX].bitcast(F16).rearrange("p (a d) -> p a d", a=2)
        xg_lo = hs[:, F + 3 * DX:F + 4 * DX].bitcast(F16).rearrange("p (a d) -> p a d", a=2)
        yb = hs[:, F + 4 * DX:F + 4 * DX + D]
        y = hs[:, F + 4 * DX + D:F + 4 * DX + 3 * D].rearrange("p (a d) -> p a d", a=2)

        bank = ctx.enter_context(nc.psum_tensor("bank", [P, 8, 512], F32))
        V_BANK, X2_BANK, T_BANK, Q_BANK = 4, 5, 6, 7

        s_ids, s_small, s_wqkv, s_biases = sem("s_ids"), sem("s_small"), sem("s_wqkv"), sem("s_biases")
        s_exp = [sem("s_exp0"), sem("s_exp1")]
        s_word = sem("s_word")
        s_out0, s_x = sem("s_out0"), sem("s_x")
        s_pm_st, s_pm_ld = sem("s_pm_st"), sem("s_pm_ld")
        s_gather, s_scatter = sem("s_gather"), sem("s_scatter")
        s_const, s_pconst, s_types, s_pt = sem("s_const"), sem("s_pconst"), sem("s_types"), sem("s_pt")
        s_dconst = sem("s_dconst")
        s_whi, s_wsplit, s_ehi, s_esplit = sem("s_whi"), sem("s_wsplit"), sem("s_ehi"), sem("s_esplit")
        s_warm = sem("s_warm")
        s_past_dve, s_past_pool, s_past_sp = sem("s_past_dve"), sem("s_past_pool"), sem("s_past_sp")
        s_tsel, s_e0 = sem("s_tsel"), sem("s_e0")
        s_st = [sem(f"s_st{n}") for n in range(3)]
        s_mv = [sem(f"s_mv{n}") for n in range(3)]
        s_ve = [sem(f"s_ve{n}") for n in range(3)]
        s_rs = [sem(f"s_rs{n}") for n in range(3)]
        s_mneg = [sem(f"s_mneg{n}") for n in range(3)]
        s_hg, s_h, s_hb, s_xn = sem("s_hg"), sem("s_h"), sem("s_hb"), sem("s_xn")
        s_T, s_Thi, s_Tlo = sem("s_T"), sem("s_Thi"), sem("s_Tlo")
        s_Q, s_K, s_VY = sem("s_Q"), sem("s_K"), sem("s_VY")
        s_qlow, s_q, s_khi, s_klo = sem("s_qlow"), sem("s_q"), sem("s_khi"), sem("s_klo")
        s_v, s_h2 = sem("s_v"), sem("s_h2")
        s_S = [sem(f"s_S{r}") for r in range(RG)]
        s_max, s_nmax = sem("s_max"), sem("s_nmax")
        s_P = [sem(f"s_P{r}") for r in range(RG)]
        s_PT = [sem(f"s_PT{r}") for r in range(RG)]
        s_PTe = [sem(f"s_PTe{r}") for r in range(RG)]
        s_O, s_rd, s_att = sem("s_O"), sem("s_rd"), sem("s_att")
        s_xn2 = sem("s_xn2")
        s_X2, s_x2t, s_lg = sem("s_X2"), sem("s_x2t"), sem("s_lg")
        s_r = sem("s_r")
        s_ex = sem("s_ex")
        s_ohx, s_pre, s_perm, s_inv = sem("s_ohx"), sem("s_pre"), sem("s_perm"), sem("s_inv")
        s_route = sem("s_route")
        s_pmc, s_pmT, s_pmt = sem("s_pmc"), sem("s_pmT"), sem("s_pmt")
        s_less, s_cnt = sem("s_less"), sem("s_cnt")
        s_now_in, s_now_out = sem("s_now_in"), sem("s_now_out")
        s_XT, s_xhi, s_xlo = sem("s_XT"), sem("s_xhi"), sem("s_xlo")
        s_H = [sem("s_H0"), sem("s_H1")]
        s_g = [sem("s_g0"), sem("s_g1")]
        s_ghi, s_glo = sem("s_ghi"), sem("s_glo")
        s_Y, s_yb, s_y = sem("s_Y"), sem("s_yb"), sem("s_y")
        N_CONST = 8

        wide = lambda t: t.rearrange("p t d -> p (t d)")
        all_hi, all_lo = wide(e_hi[:, :, :]), wide(e_lo[:, :, :])

        def steps(engine, body):
            for i in range(-2, 5):
                body(i, i % 2)
            with engine.Fori(5, NT - 4, 2) as i:
                body(i, 1)
                body(i + 1, 0)
            for i in range(NT - 3, NT + 4):
                body(i, i % 2)

        def has_piece(i):
            return within(i + 2, 4 * E)

        def piece_at(i, par, tensor):
            a, b = piece_cols[par]
            return tensor[:, ds((i + 2 - par) * (WE // 2) + a, b - a)]

        def slot_steps(engine, body, after, looked_up=None):
            def lookup(first, n):
                return nc.values_load_multi_w_load_instructions(
                    experts[0:1, ds(first, n)], engines=[looked_up], min_val=0, max_val=2 * E - 1,
                    skip_runtime_bounds_check_because="a count of E - 1 comparisons, plus 0 or E")[1]

            def one(t, **kw):
                e = (None, None)
                if looked_up and 0 <= t <= TT:
                    if t in (0, TC):
                        engine.wait_ge(s_route, 1 + (t == TC))
                    first = max(t - 1, 0)
                    found = lookup(first, min(t, TT - 1) - first + 1)
                    e = (found[0] if t > 0 else None, found[-1] if t < TT else None)
                body(t, t % 2, e, **kw)

            def two(t, **kw):
                e = lookup(t - 1, 3) if looked_up else (None, None, None)
                body(t, 0, e[0:2], **kw)
                body(t + 1, 1, e[1:3], **kw)

            for t in range(-2, 4):
                one(t, ranks=True)
            with engine.Fori(4, NT - 1, 2) as t:
                two(t, ranks=True)
            for t in range(NT, TC + 1):
                one(t)
                if t in after:
                    after[t]()
            with engine.Fori(TC + 1, TT - 3, 2) as t:
                two(t)
            for t in range(TT - 2, TT + 2):
                one(t)

        block = ctx.enter_context(nc.Block())

        @block.sync
        def _(sp):
            sp.dma_start(ids_sb[:, 0:NT], ids).then_inc(s_ids, 16)
            sp.dma_start(types_sb[:, 0:NT], types).then_inc(s_small, 16)
            sp.dma_start(pos_sb[:, :], pos).then_inc(s_small, 16)
            for n in range(2):
                sp.dma_start(ty[:, n, :], type_emb[n:n + 1, :].broadcast_to([P, D])).then_inc(s_small, 16)
            sp.dma_start(gamma_sb[:, :], gamma.broadcast_to([P, D])).then_inc(s_small, 16)
            sp.dma_start(beta_sb[:, :], beta.broadcast_to([P, D])).then_inc(s_small, 16)
            sp.dma_start(bproj_sb[:, :], b_proj.broadcast_to([P, D])).then_inc(s_small, 16)
            sp.dma_start(st[:, 0:AC], wqkvp[0]).then_inc(s_wqkv, 16)
            sp.dma_start(st[:, AC:2 * AC], wqkvp[1]).then_inc(s_wqkv, 16)
            sp.dma_start(wr_sb[:, :, :], wr).then_inc(s_biases, 16)
            sp.dma_start(br_sb[:, :], br.broadcast_to([P, 2 * E])).then_inc(s_biases, 16)
            sp.dma_start(b1_sb[:, :, :], b1).then_inc(s_biases, 16)
            sp.dma_start(wide(b2_sb[:, :, :]), b2.broadcast_to([P, 2 * E * D])).then_inc(s_biases, 16)
            def load_piece(i, par):
                a, b = piece_cols[par]
                sp.dma_start(stage[:, 1, a:b], piece_at(i, par, wexp)).then_inc(s_exp[par], 16)

            load_piece(-2, 0)

            def body(i, par):
                if has_piece(i + 1):
                    upto(sp, s_esplit, i + 2)
                    alone(sp, s_past_sp)
                    load_piece(i + 1, 1 - par)
                if within(i - 2, NT):
                    b = i - 2
                    sp.wait_ge(s_h2, b + 1)
                    alone(sp, s_past_sp)
                    upto(sp, s_out0, 16 * b)
                    alone(sp, s_past_sp)
                    sp.dma_start(out[ds(b * P, P), :], h2[:, par, :]).then_inc(s_out0, 16)
                    sp.wait_ge(s_xn2, 2 * b + 2)
                    alone(sp, s_past_sp)
                    upto(sp, s_x, 16 * b)
                    alone(sp, s_past_sp)
                    sp.dma_start(xrows[ds(b * P, P), :], xn2[:, par, :]).then_inc(s_x, 16)

            steps(sp, body)
            sp.wait_ge(s_pmt, 1)
            sp.dma_start(prow_dram.rearrange("(i p) -> i p", p=P), pmt[:, :]).then_inc(s_pm_st, 16)
            sp.wait_ge(s_pm_st, 16)
            sp.dma_start(prow[:, :], prow_dram.unsqueeze(0).broadcast_to([P, N])).then_inc(s_pm_ld, 16)
            sp.wait_ge(s_pm_ld, 16)

        @block.gpsimd
        def _(pool):
            pool.wait_ge(s_ids, 16)

            pool.memset(ids_sb[:, NT:], 0).then_inc(s_pconst, 1)
            pool.memset(types_sb[:, NT:], 0).then_inc(s_pconst, 1)
            pool.memset(minus_half[:, :], -0.5).then_inc(s_const, 1)
            pool.memset(ident[:, :], 0.0).then_inc(s_pconst, 1)
            pool.memset(ones[:, :], 1.0).then_inc(s_pconst, 1)
            pool.memset(tie[:, :], 0.0).then_inc(s_pconst, 1)
            pool.memset(low_rows[:, :], 0.0).then_inc(s_pconst, 1)
            pool.wait_ge(s_pconst, 6)
            pool.affine_select(out=ident[:, :], in_=ident[:, :], compare_op=ALU.not_equal, fill=1.0,
                               base=0, pattern=[[-1, P]], channel_multiplier=1).then_inc(s_const, 1)
            pool.affine_select(out=before[:, :], in_=ones[:, :], compare_op=ALU.is_gt, fill=0.0,
                               base=0, pattern=[[1, P]], channel_multiplier=-1).then_inc(s_const, 1)
            pool.wait_ge(s_const, 3)
            pool.memset(low_rows[P // 2:P, :], XS).then_inc(s_const, 1)
            pool.wait_ge(s_const, 4)
            pool.iota(low_heads_i[:, :], pattern=[[0, 1]], base=0, channel_multiplier=1).then_inc(s_const, 1)
            pool.wait_ge(s_small, 16 * 7)
            pool.tensor_tensor(pos_sb[:, :], pos_sb[:, :], ty[:, 0, :], ALU.add).then_inc(s_pt, 1)
            pool.tensor_tensor(ty[:, 1, :], ty[:, 1, :], ty[:, 0, :], ALU.subtract).then_inc(s_pt, 1)
            pool.tensor_copy(types_f[:, :], types_sb[:, :]).then_inc(s_types, 1)
            pool.wait_ge(s_const, 1)
            pool.wait_ge(s_pt, 2)
            pool.wait_ge(s_types, 1)

            def embed(j, par):
                pool.tensor_tensor(we[:, par, :], ty[:, 1, :], types_f[:, ds(j, 1)].broadcast_to([P, D]),
                                   ALU.mult).then_inc(s_tsel, 1)
                pool.tensor_copy(now_in[:, par, :], ids_sb[:, ds(j, 1)]).then_inc(s_now_in, 1)
                pool.wait_ge(s_tsel, j + 1)
                pool.tensor_tensor(we[:, par, :], we[:, par, :], pos_sb[:, :], ALU.add).then_inc(s_e0, 1)
                pool.wait_ge(s_now_in, j + 1)
                alone(pool, s_past_pool)
                pool.wait_ge(s_e0, j + 1)
                alone(pool, s_past_pool)
                pool.indirect_dma_start(
                    out=we[:, par, :], out_offset=None, in_=word,
                    in_offset=bass.IndirectOffsetOnAxis(ap=now_in[:, par, :], axis=0),
                    compute_op=ALU.add).then_inc(s_word, 16)

            def rstd_of(n, count):
                pool.wait_ge(s_mv[n], count)
                alone(pool, s_past_pool)
                pool.tensor_scalar(vare[:, n, :], mv[:, n, 1:2], EPS, None, ALU.add).then_inc(s_ve[n], 1)
                if n > 0:
                    pool.tensor_scalar(mneg[:, n, :], mv[:, n, 0:1], -1.0, None, ALU.mult).then_inc(s_mneg[n], 1)
                pool.wait_ge(s_ve[n], count)
                pool.tensor_tensor(rstd[:, n, :], vare[:, n, :], minus_half[:, :], ALU.pow).then_inc(s_rs[n], 1)

            def centred(to, source, n, count, done):
                pool.wait_ge(s_rs[n], count)
                alone(pool, s_past_pool)
                pool.wait_ge(s_mneg[n], count)
                alone(pool, s_past_pool)
                for lo, at in ((0, 0), (P, D)):
                    pool.tensor_scalar(to[:, at:at + D - lo], source[:, lo:], mneg[:, n, :], rstd[:, n, :],
                                       ALU.add, ALU.mult).then_inc(done, 1)

            embed(0, 0)
            pool.wait_ge(s_word, 16)
            embed(1, 1)

            def body(i, par):
                j = i + 2
                if within(j, NT):
                    rstd_of(0, j + 1)
                    if within(j + 2, NT + 1):
                        pool.wait_ge(s_hg, j + 1)
                        alone(pool, s_past_pool)
                        pool.wait_ge(s_word, 16 * (j + 2))
                        embed(j + 2, par)
                    rstd_of(1, j + 1)
                    upto(pool, s_T, j - 1)
                    alone(pool, s_past_pool)
                    centred(xn[:, par, :], h[:, par, :], 1, j + 1, s_xn)
                    upto(pool, s_h2, j - 3)
                    pool.tensor_tensor(wide(hb[:, ds(j % 4, 1), :]), h[:, par, :], bproj_sb[:, :],
                                       ALU.add).then_inc(s_hb, 1)
                if within(i - 2, NT):
                    rstd_of(2, i - 1)
                    upto(pool, s_X2, i - 3)
                    alone(pool, s_past_pool)
                    upto(pool, s_x, 16 * (i - 3))
                    alone(pool, s_past_pool)
                    centred(xn2[:, par, :], h2[:, par, :], 2, i - 1, s_xn2)

            steps(pool, body)

            pool.iota(iota_s[:, :], pattern=[[1, P]], base=0, channel_multiplier=0,
                      allow_small_or_imprecise_dtypes=True).then_inc(s_const, 1)
            pool.iota(iota_t[:, :], pattern=[[1, TC]], base=0, channel_multiplier=0,
                      allow_small_or_imprecise_dtypes=True).then_inc(s_const, 1)
            pool.iota(token1[:, :], pattern=[[P, NT]], base=1, channel_multiplier=1,
                      allow_small_or_imprecise_dtypes=True).then_inc(s_const, 1)
            pool.affine_select(out=tie[:, :], in_=tie[:, :], compare_op=ALU.is_ge, fill=TIE,
                               base=N - P, pattern=[[-1, 2 * N - P]], channel_multiplier=1).then_inc(s_dconst, 1)

            pool.wait_ge(s_x, 16 * NT)
            pool.wait_ge(s_word, 16 * (NT + 1))
            pool.wait_ge(s_out0, 16 * NT)

            def tiles(t, par, e, ranks=False):
                g = t + 2
                if within(g, TT):
                    if isinstance(g, int) and g in (0, TC):
                        pool.wait_ge(s_route, 1 + (g == TC))
                    upto(pool, s_gather, 16 * g)
                    pool.tensor_copy(now_in[:, par, :], idx_in[:, ds(g, 1)]).then_inc(s_now_in, 1)
                    pool.wait_ge(s_now_in, NT + 1 + g + 1)
                    upto(pool, s_XT, g - 1)
                    alone(pool, s_past_pool)
                    pool.indirect_dma_start(
                        out=xg[:, par, :], out_offset=None, in_=xrows,
                        in_offset=bass.IndirectOffsetOnAxis(ap=now_in[:, par, :], axis=0)).then_inc(s_gather, 16)
                o, opar = t - 2, par
                if within(o, TT):
                    upto(pool, s_scatter, 16 * o)
                    pool.tensor_copy(now_out[:, opar, :], idx_out[:, ds(o, 1)]).then_inc(s_now_out, 1)
                    pool.wait_ge(s_now_out, o + 1)
                    pool.wait_ge(s_y, o + 1)
                    alone(pool, s_past_pool)
                    pool.indirect_dma_start(
                        out=out, out_offset=bass.IndirectOffsetOnAxis(ap=now_out[:, opar, :], axis=0),
                        in_=y[:, opar, :], in_offset=None, bounds_check=N - 1, oob_is_err=False,
                        compute_op=ALU.add).then_inc(s_scatter, 16)

            slot_steps(pool, tiles, {})
            pool.wait_ge(s_scatter, 16 * TT)

        @block.scalar
        def _(act_e):
            act_e.wait_ge(s_wqkv, 32)
            act_e.wait_ge(s_const, 5)
            act_e.activation(w_hi[:, :], st[:, 0:AC], ACT.Copy, scale=XS).then_inc(s_whi, 1)
            act_e.activation(w_tmp[:, :], st[:, AC:2 * AC], ACT.Copy, scale=low_rows[:, :]).then_inc(s_whi, 1)
            act_e.activation(q_low[0:1, 0:1], ident[0:1, 0:1], ACT.Exp).then_inc(s_warm, 1)
            act_e.wait_ge(s_warm, 1)
            act_e.wait_ge(s_dconst, 1)

            def body(i, par):
                def exps(r):
                    if within(i, NT):
                        act_e.wait_ge(s_nmax, 2 * i + r // 2 + 1)
                        upto(act_e, s_PT[r], i)
                        for c in range(CH):
                            ins = act_e.activation(probs[:, r, c, :], bank[:, r, c * P:(c + 1) * P], ACT.Exp,
                                                   bias=negmax[:, r, c:c + 1], scale=SCORE)
                        ins.then_inc(s_P[r], 1)

                def evac_pt(r):
                    if within(i, NT):
                        act_e.wait_ge(s_PT[r], i + 1)
                        upto(act_e, s_O, i)
                        act_e.activation(probs_t[:, r, :, :].rearrange("p c k -> p (c k)"),
                                         bank[:, r, 0:QC], ACT.Copy).then_inc(s_PTe[r], 1)

                if within(i - 4, NT):
                    act_e.wait_ge(s_X2, i - 3)
                    upto(act_e, s_VY, i + 1)
                    act_e.activation(x2t[:, :, :].rearrange("p a t -> p (a t)"), bank[:, X2_BANK, 0:DX],
                                     ACT.Copy).then_inc(s_x2t, 1)
                if has_piece(i):
                    act_e.wait_ge(s_exp[par], 8 * (i + 2 - par) + 16)
                    to, (a, b) = piece_at(i, par, all_hi), piece_cols[par]
                    if par == 0:
                        act_e.activation(piece_at(i, par, all_hi)[:, 0:F], stage[:, 1, 0:F], ACT.Copy, scale=XS)
                        act_e.activation(piece_at(i, par, all_hi)[:, F:2 * F], stage[:, 1, F:2 * F], ACT.Copy,
                                         scale=low_rows[:, :]).then_inc(s_ehi, 1)
                    else:
                        act_e.activation(to, stage[:, 1, a:b], ACT.Copy, scale=XS).then_inc(s_ehi, 1)
                exps(0)
                exps(1)
                if within(i + 1, NT):
                    act_e.wait_ge(s_K, i + 2)
                    act_e.activation(k_hi[:, 1 - par, :], bank[:, T_BANK, 0:QC], ACT.Copy,
                                     scale=UN * QS).then_inc(s_khi, 1)
                exps(2)
                if within(i + 1, NT):
                    act_e.wait_ge(s_Q, i + 2)
                    upto(act_e, s_q, i + 1)
                    act_e.activation(q_low[:, :], bank[:, Q_BANK, 0:QC], ACT.Copy,
                                     scale=low_heads[:, :]).then_inc(s_qlow, 1)
                evac_pt(0)
                exps(3)
                evac_pt(1)
                evac_pt(2)
                if within(i + 2, NT + 3):
                    act_e.wait_ge(s_T, i + 3)
                    upto(act_e, s_VY, i + 2)
                    lo, hi = (0 if within(i + 2, NT) else DX), (2 * DX if within(i - 1, NT) else DX)
                    act_e.activation(t_hi[:, lo:hi], bank[:, T_BANK, lo:hi], ACT.Copy, scale=XS).then_inc(s_Thi, 1)
                evac_pt(3)

            steps(act_e, body)

            act_e.wait_ge(s_r, 3)
            act_e.activation(ex[:, :, :], lg[:, :, :], ACT.Exp).then_inc(s_ex, 1)
            act_e.wait_ge(s_pmT, 1)
            act_e.activation(pmt[:, :], bank[0:NT, 2, 0:P], ACT.Copy).then_inc(s_pmt, 1)
            act_e.activation(q_low[0:1, 0:1], ident[0:1, 0:1], ACT.Gelu).then_inc(s_warm, 1)
            act_e.wait_ge(s_warm, 2)

            def tiles(t, par, e, ranks=False):
                if within(t + 1, TT):
                    act_e.wait_ge(s_XT, t + 2)
                    upto(act_e, s_H[1], t)
                    act_e.activation(xg_hi[:, 1 - par, :], bank[:, 4, 0:DX], ACT.Copy, scale=XS).then_inc(s_xhi, 1)
                if within(t, TT):
                    upto(act_e, s_glo, 2 * (t - 1))
                    for half in range(2):
                        act_e.wait_ge(s_H[half], t + 1)
                        for f in range(half * 3, half * 3 + 3):
                            ins = act_e.activation(
                                act[:, par, f * P:(f + 1) * P],
                                bank[:, 2 * par + half, (f % 3) * P:(f % 3 + 1) * P],
                                ACT.Gelu, bias=b1_sb[:, ds(e[1], 1), f:f + 1].rearrange("p a b -> p (a b)"),
                                scale=UN)
                        ins.then_inc(s_g[half], 1)

            slot_steps(act_e, tiles, {}, mybir.EngineType.Activation)

        @block.vector
        def _(dve):
            stt = dve.scalar_tensor_tensor
            dve.wait_ge(s_const, 5)
            dve.tensor_scalar(low_heads_i[:, :], low_heads_i[:, :], HD, None, ALU.bitwise_and).then_inc(s_r, 1)
            dve.wait_ge(s_r, 1)
            dve.memset(v_sb[:, :, :, HD:HD + 1], 1.0).then_inc(s_v, 1)
            dve.wait_ge(s_v, 1)
            dve.tensor_scalar(low_heads[:, :], low_heads_i[:, :], UN * QS / HD, None, ALU.mult).then_inc(s_dconst, 1)
            dve.wait_ge(s_whi, 1)
            stt(out=w_lo[:, :], in0=st[:, 0:AC], scalar=XS, in1=w_hi[:, :], op0=ALU.mult,
                op1=ALU.subtract).then_inc(s_wsplit, 1)
            dve.wait_ge(s_whi, 2)
            stt(out=w_mix[:, :], in0=st[:, AC:2 * AC], scalar=XS, in1=w_tmp[:, :], op0=ALU.mult,
                op1=ALU.subtract).then_inc(s_wsplit, 1)

            def bn_stats(n, source, ready, count):
                dve.wait_ge(ready, count)
                alone(dve, s_past_dve)
                dve.bn_stats(out=stats[:, n, :], in_=source).then_inc(s_st[n], 1)

            def bn_aggr(n, count, used, used_count):
                upto(dve, used, used_count)
                alone(dve, s_past_dve)
                dve.wait_ge(s_st[n], count)
                alone(dve, s_past_dve)
                dve.bn_aggr(out=mv[:, n, :], in_=stats[:, n, :]).then_inc(s_mv[n], 1)

            def body(i, par):
                j, k = i + 2, i + 1

                def maxima(r):
                    if within(i, NT):
                        dve.wait_ge(s_S[r], i + 1)
                        dve.tensor_reduce(rawmax[:, r, :], bank[:, r, 0:QC].rearrange("p (c k) -> p c k", c=CH),
                                          AX, ALU.max, negate=True).then_inc(s_max, 1)

                def scaled(r0, r1):
                    if within(i, NT):
                        dve.wait_ge(s_max, RG * i + r1)
                        upto(dve, s_P[r1 - 1], i)
                        dve.tensor_scalar(negmax[:, r0:r1, :], rawmax[:, r0:r1, :], SCORE, None,
                                          ALU.mult).then_inc(s_nmax, 1)

                if within(j, NT):
                    dve.wait_ge(s_mv[0], j + 1)
                    upto(dve, s_h, j)
                    stt(out=hg[:, :], in0=we[:, par, :], scalar=mv[:, 0, 0:1], in1=gamma_sb[:, :],
                        op0=ALU.subtract, op1=ALU.mult).then_inc(s_hg, 1)
                if within(i - 1, NT):
                    dve.wait_ge(s_O, i)
                    o = bank[:, Q_BANK, 0:HEADS * (HD + 1)].rearrange("p (h e) -> p h e", h=HEADS)
                    dve.reciprocal(rden[:, :, :], o[:, :, HD:HD + 1]).then_inc(s_rd, 1)
                if within(i - 1, NT):
                    dve.wait_ge(s_rd, i)
                    dve.wait_ge(s_T, i + 2)
                    for h0, at in ((0, 0), (P // HD, D)):
                        n = HEADS - h0
                        dve.tensor_tensor(att[:, at:at + n * HD].rearrange("p (h e) -> p h e", h=n),
                                          o[:, h0:HEADS, 0:HD], rden[:, h0:HEADS, :].broadcast_to([P, n, HD]),
                                          ALU.mult).then_inc(s_att, 1)
                maxima(0)
                maxima(1)
                maxima(2)
                scaled(0, 2)
                maxima(3)
                if within(j, NT):
                    dve.wait_ge(s_rs[0], j + 1)
                    dve.wait_ge(s_hg, j + 1)
                    upto(dve, s_hb, j - 1)
                    upto(dve, s_xn, 2 * (j - 1))
                    stt(out=h[:, par, :], in0=hg[:, :], scalar=rstd[:, 0, :], in1=beta_sb[:, :],
                        op0=ALU.mult, op1=ALU.add).then_inc(s_h, 1)
                scaled(2, RG)
                if within(j, NT):
                    bn_stats(1, h[:, par, :], s_h, j + 1)
                if within(k, NT):
                    upto(dve, s_S[RG - 1], k - 1)
                    dve.wait_ge(s_khi, k + 1)
                    stt(out=k_lo[:, 1 - par, :], in0=bank[:, T_BANK, 0:QC], scalar=UN * QS,
                        in1=k_hi[:, 1 - par, :], op0=ALU.mult, op1=ALU.subtract).then_inc(s_klo, 1)
                if within(j, NT):
                    bn_aggr(1, j + 1, s_xn, 2 * j)
                if within(k, NT):
                    dve.wait_ge(s_qlow, k + 1)
                    stt(out=q_sb[:, 1 - par, :], in0=bank[:, Q_BANK, 0:QC], scalar=UN * QS, in1=q_low[:, :],
                        op0=ALU.mult, op1=ALU.subtract).then_inc(s_q, 1)
                if within(k, NT + 5):
                    dve.wait_ge(s_VY, i + 2)
                if within(k, NT):
                    upto(dve, s_O, i)
                    dve.tensor_scalar(v_sb[:, 1 - par, :, 0:HD],
                                      bank[:, V_BANK, 0:D].rearrange("p (h e) -> p h e", h=HEADS),
                                      UN * VS, None, ALU.mult).then_inc(s_v, 1)
                if within(i - 2, NT):
                    dve.wait_ge(s_hb, i - 1)
                    upto(dve, s_out0, 16 * (i - 3))
                    upto(dve, s_xn2, 2 * (i - 3))
                    stt(out=h2[:, par, :], in0=bank[:, V_BANK, D:2 * D], scalar=UN / VS,
                        in1=wide(hb[:, ds((i - 2) % 4, 1), :]), op0=ALU.mult, op1=ALU.add).then_inc(s_h2, 1)
                if within(i - 4, NT):
                    dve.tensor_copy(wide(logits[:, ds(i - 4, 1), :]),
                                    bank[:, V_BANK, QC:QC + 2 * E]).then_inc(s_lg, 1)
                if within(i - 2, NT):
                    bn_stats(2, h2[:, par, :], s_h2, i - 1)
                if has_piece(i):
                    dve.wait_ge(s_ehi, i + 3)
                    a, b = piece_cols[par]
                    stt(out=piece_at(i, par, all_lo), in0=stage[:, 1, a:b], scalar=XS,
                        in1=piece_at(i, par, all_hi), op0=ALU.mult, op1=ALU.subtract).then_inc(s_esplit, 1)
                if within(i - 2, NT):
                    bn_aggr(2, i - 1, s_xn2, 2 * (i - 2))
                if within(j + 1, NT):
                    bn_stats(0, we[:, 1 - par, :], s_word, 16 * (j + 2))
                if within(j, NT + 3):
                    dve.wait_ge(s_Thi, i + 3)
                    lo, hi = (0 if within(j, NT) else DX), (2 * DX if within(i - 1, NT) else DX)
                    stt(out=t_lo[:, lo:hi], in0=bank[:, T_BANK, lo:hi], scalar=XS, in1=t_hi[:, lo:hi],
                        op0=ALU.mult, op1=ALU.subtract).then_inc(s_Tlo, 1)
                if within(j + 1, NT):
                    bn_aggr(0, j + 2, s_rs[0], j + 1)

            dve.wait_ge(s_small, 16 * 7)
            bn_stats(0, we[:, 0, :], s_word, 16)
            bn_aggr(0, 1, s_rs[0], 0)
            steps(dve, body)

            count = [1]

            def own(ins):
                count[0] += 1
                ins.then_inc(s_r, 1)
                dve.wait_ge(s_r, count[0])

            dve.wait_ge(s_lg, NT)
            dve.wait_ge(s_biases, 16 * 4)
            by_router = logits[:, :, :].rearrange("p i (r e) -> p (i r) e", r=2)
            spread = lambda t, n: t.unsqueeze(2).broadcast_to([P, n, E])
            own(dve.tensor_tensor(logits[:, :, :], logits[:, :, :],
                                  br_sb[:, :].unsqueeze(1).broadcast_to([P, NT, 2 * E]), ALU.add))
            dve.tensor_reduce(top[:, :], by_router, AX, ALU.max).then_inc(s_rd, 1)
            dve.wait_ge(s_rd, NT + 1)
            own(dve.tensor_tensor(lg[:, :, :], by_router, spread(top[:, :], R2), ALU.subtract))
            dve.wait_ge(s_ex, 1)
            own(dve.tensor_reduce(den[:, :], ex[:, :, :], AX, ALU.add))
            own(dve.reciprocal(rec[:, :], den[:, :]))
            own(dve.tensor_tensor(pr[:, :, :], ex[:, :, :], spread(rec[:, :], R2), ALU.mult))
            own(dve.tensor_reduce(pmax[:, :], pr[:, :, :], AX, ALU.max))
            common = pmax[:, :].rearrange("p (i r) -> p i r", r=2)[:, :, 0]
            dve.tensor_copy(pm_c[:, :], common).then_inc(s_pmc, 1)
            own(dve.tensor_tensor(eq[:, :, :], pr[:, :, :], spread(pmax[:, :], R2), ALU.is_equal))
            own(dve.tensor_copy(oh[:, :, 0], eq[:, :, 0]))
            seen_at = eq[:, :, 0]
            for e in range(1, E):
                own(dve.tensor_tensor(oh[:, :, e], eq[:, :, e], seen_at, ALU.is_gt))
                if e < E - 1:
                    own(dve.tensor_tensor(seen[:, e % 2, :], eq[:, :, e], seen_at, ALU.max))
                    seen_at = seen[:, e % 2, :]
            own(dve.reciprocal(pm_rec[:, :], pmax[:, :]))
            own(dve.tensor_tensor(scale[:, :], pmax[:, :], pm_rec[:, :], ALU.mult))
            own(dve.memset(cum[:, :, 0:NT, :], 0.0))
            own(dve.memset(ends[:, :, 0:E], 0.0))
            dve.wait_ge(s_const, N_CONST)
            oh_r = oh[:, :, :].rearrange("p (i r) e -> p i r e", r=2)
            scale_r = scale[:, :].rearrange("p (i r) -> p i r", r=2)

            def route_in(u):
                if u == 0:
                    dve.tensor_copy(ohx[:, :, :], oh_r[:, :, 0, :]).then_inc(s_ohx, 1)
                    return
                dve.wait_ge(s_cnt, NT)
                own(dve.tensor_tensor(rank4[:, :, :], bank[:, 6, 0:NT * E].rearrange("p (i e) -> p i e", e=E),
                                      oh_r[:, :, 0, :], ALU.mult))
                own(dve.tensor_reduce(rank[:, :], rank4[:, :, :], AX, ALU.add))
                own(dve.tensor_scalar(dropped[:, :], rank[:, :], float(CAP), None, ALU.is_ge))
                dve.tensor_tensor(ohx[:, :, :], oh_r[:, :, 1, :], spread(dropped[:, :], NT),
                                  ALU.mult).then_inc(s_ohx, 1)

            def route_slots(u):
                n_t, t0 = (TC, 0) if u == 0 else (TU, TC)
                pre = bank[:, 7, 0:NT * E].rearrange("p (i e) -> p i e", e=E)
                sums = bank[:, 7, NT * E:2 * NT * E].rearrange("p (i e) -> p i e", e=E)
                dve.wait_ge(s_pre, u + 1)
                own(dve.tensor_copy(cum[:, 0, NT:, :], sums))
                at = 0
                for step in (1, 2, 4, 8):
                    own(dve.tensor_tensor(cum[:, 1 - at, NT:, :], cum[:, at, NT:, :],
                                          cum[:, at, NT - step:2 * NT - step, :], ALU.add))
                    at = 1 - at
                own(dve.tensor_scalar(tot[:, :], cum[:, at, 2 * NT - 1, :], float(P - 1), None, ALU.add))
                own(dve.tensor_copy(tiles_i[:, :], tot[:, :]))
                own(dve.tensor_scalar(tiles_i[:, :], tiles_i[:, :], 7, None, ALU.logical_shift_right))
                own(dve.tensor_copy(ends[:, 0, E:], tiles_i[:, :]))
                own(dve.tensor_tensor(ends[:, 1, E:], ends[:, 0, E:], ends[:, 0, E - 1:2 * E - 1], ALU.add))
                own(dve.tensor_tensor(ends[:, 2, E:], ends[:, 1, E:], ends[:, 1, E - 2:2 * E - 2], ALU.add))
                own(dve.tensor_tensor(ge[:, 0:n_t, :], iota_t[:, 0:n_t].unsqueeze(2).broadcast_to([P, n_t, E - 1]),
                                      ends[:, 2, E:2 * E - 1].unsqueeze(1).broadcast_to([P, n_t, E - 1]), ALU.is_ge))
                own(dve.tensor_reduce(tile_e[:, 0:n_t], ge[:, 0:n_t, :], AX, ALU.add))
                own(dve.tensor_scalar(experts[0:1, t0:t0 + n_t], tile_e[0:1, 0:n_t], float(E * u), None, ALU.add))
                own(dve.tensor_tensor(posn[:, :, :], pre, cum[:, at, NT - 1:2 * NT - 1, :], ALU.add))
                own(stt(out=pos2[:, :, :], in0=ends[:, 2, E - 1:2 * E - 1].unsqueeze(1).broadcast_to([P, NT, E]),
                        scalar=float(P), in1=posn[:, :, :], op0=ALU.mult, op1=ALU.add))
                own(dve.tensor_tensor(pos3[:, :, :], pos2[:, :, :], ohx[:, :, :], ALU.mult))
                own(dve.tensor_reduce(slot[:, :], pos3[:, :, :], AX, ALU.add))
                own(dve.tensor_reduce(valid[:, :], ohx[:, :, :], AX, ALU.add))
                own(dve.tensor_copy(slot_i[:, :], slot[:, :]))
                own(dve.tensor_scalar(slot_hi[:, :], slot_i[:, :], 7, None, ALU.logical_shift_right))
                own(dve.tensor_scalar(slot_lo[:, :], slot_i[:, :], P - 1, None, ALU.bitwise_and))
                own(dve.tensor_copy(slot_hf[:, :], slot_hi[:, :]))
                own(dve.tensor_copy(slot_lf[:, :], slot_lo[:, :]))
                own(dve.tensor_tensor(tokv[:, :], token1[:, :], valid[:, :], ALU.mult))
                own(dve.tensor_tensor(scv[:, :], scale_r[:, :, u], valid[:, :], ALU.mult))
                own(dve.tensor_tensor(oh_t[:, :, 0:n_t], slot_hf[:, :].unsqueeze(2).broadcast_to([P, NT, n_t]),
                                      iota_t[:, 0:n_t].unsqueeze(1).broadcast_to([P, NT, n_t]), ALU.is_equal))
                own(dve.tensor_tensor(oh_m[:, :, 0, 0:n_t], oh_t[:, :, 0:n_t],
                                      tokv[:, :].unsqueeze(2).broadcast_to([P, NT, n_t]), ALU.mult))
                own(dve.tensor_tensor(oh_m[:, :, 1, 0:n_t], oh_t[:, :, 0:n_t],
                                      scv[:, :].unsqueeze(2).broadcast_to([P, NT, n_t]), ALU.mult))
                dve.tensor_tensor(oh_s[:, :, :], slot_lf[:, :].unsqueeze(2).broadcast_to([P, NT, P]),
                                  iota_s[:, :].unsqueeze(1).broadcast_to([P, NT, P]), ALU.is_equal).then_inc(s_perm, 1)

            def route_out(u):
                n_t, t0 = (TC, 0) if u == 0 else (TU, TC)
                dve.wait_ge(s_inv, u + 1)
                own(dve.tensor_copy(inv[:, :, 0:n_t],
                                    bank[:, 7, 256:256 + 2 * n_t].rearrange("p (a t) -> p a t", a=2)))
                own(dve.tensor_scalar(empty[:, 0:n_t], inv[:, 0, 0:n_t], 0.0, float(2 * N), ALU.is_equal, ALU.mult))
                own(stt(out=out_f[:, 0:n_t], in0=inv[:, 0, 0:n_t], scalar=-1.0, in1=empty[:, 0:n_t],
                        op0=ALU.add, op1=ALU.add))
                own(dve.tensor_copy(idx_out[:, t0:t0 + n_t], out_f[:, 0:n_t]))
                own(dve.tensor_copy(slot_scale[:, t0:t0 + n_t], inv[:, 1, 0:n_t]))
                dve.tensor_scalar(idx_in[:, t0:t0 + n_t], inv[:, 0, 0:n_t], -1.0, 0.0, ALU.add,
                                  ALU.max).then_inc(s_route, 1)

            route_in(0)
            route_slots(0)
            route_out(0)

            def tiles(t, par, e, ranks=False):
                if within(t + 1, TT):
                    dve.wait_ge(s_xhi, t + 2)
                    stt(out=xg_lo[:, 1 - par, :], in0=bank[:, 4, 0:DX], scalar=XS, in1=xg_hi[:, 1 - par, :],
                        op0=ALU.mult, op1=ALU.subtract).then_inc(s_xlo, 1)
                if ranks and within(t, NT):
                    if isinstance(t, int) and t == 0:
                        dve.wait_ge(s_pm_ld, 16)
                        dve.wait_ge(s_dconst, 2)
                    upto(dve, s_cnt, t - 1)
                    stt(out=less[:, par, :], in0=prow[:, :], scalar=pm_c[:, ds(t, 1)],
                        in1=tie[:, ds(N - P - t * P, N)], op0=ALU.subtract, op1=ALU.is_lt).then_inc(s_less, 1)
                if within(t, TT):
                    for half in range(2):
                        cols = slice(half * (F // 2), (half + 1) * (F // 2))
                        dve.wait_ge(s_g[half], t + 1)
                        upto(dve, s_Y, t - 1)
                        dve.tensor_scalar(act_hi[:, par, cols], act[:, par, cols], GS, None,
                                          ALU.mult).then_inc(s_ghi, 1)
                        dve.wait_ge(s_ghi, 2 * t + half + 1)
                        stt(out=act_lo[:, par, cols], in0=act[:, par, cols], scalar=GS, in1=act_hi[:, par, cols],
                            op0=ALU.mult, op1=ALU.subtract).then_inc(s_glo, 1)
                if within(t - 1, TT):
                    o = t - 1
                    dve.wait_ge(s_Y, o + 1)
                    upto(dve, s_y, o)
                    stt(out=yb[:, :], in0=bank[:, 5, 0:D], scalar=1.0 / (XS * GS),
                        in1=wide(b2_sb[:, ds(e[0], 1), :]), op0=ALU.mult, op1=ALU.add).then_inc(s_yb, 1)
                    dve.wait_ge(s_yb, o + 1)
                    upto(dve, s_scatter, 16 * (o - 1))
                    dve.tensor_scalar(y[:, 1 - par, :], yb[:, :], slot_scale[:, ds(o, 1)], None,
                                      ALU.mult).then_inc(s_y, 1)

            def second_slots():
                route_in(1)
                route_slots(1)

            slot_steps(dve, tiles, {NT: second_slots, NT + 1: lambda: route_out(1)},
                       mybir.EngineType.DVE)

        @block.tensor
        def _(pe):
            pe.wait_ge(s_const, 5)
            pe.wait_ge(s_wsplit, 2)

            def transposed(b, at, rows):
                pe.transpose(bank[:, b, at:at + P], rows[:, 0:P], ident[:, :])
                return pe.transpose(bank[:, b, at + P:at + DX], rows[:, P:DX], ident[:, :])

            def five(out_ap, terms):
                for n, (lhs, rhs) in enumerate(terms):
                    ins = pe.matmul(out_ap, lhs, rhs, start=(n == 0), stop=(n == 4))
                return ins

            def parts(col, n):
                return w_hi[:, col:col + n], w_lo[:, col:col + n], w_mix[:, col:col + n]

            def body(i, par):
                j, k = i + 2, i + 1
                if within(i, NT):
                    pe.wait_ge(s_q, i + 1)
                    pe.wait_ge(s_klo, i + 1)
                    for r in range(RG):
                        upto(pe, s_PTe[r], i)
                        rows = slice(32 * r, 32 * r + 32)
                        for c in range(CH):
                            cols, to = slice(c * P, (c + 1) * P), bank[:, r, c * P:(c + 1) * P]
                            pe.matmul(to, q_sb[rows, par, cols], k_hi[rows, par, cols], start=True, stop=False)
                            ins = pe.matmul(to, q_sb[rows, par, cols], k_lo[rows, par, cols],
                                            start=False, stop=True)
                        ins.then_inc(s_S[r], 1)
                if within(k, NT):
                    pe.wait_ge(s_Tlo, i + 2)
                    x0h, x1h = t_hi[:, 0:P], t_hi[:, P:DX]
                    x0l, x1l = t_lo[:, 0:P], t_lo[:, P:DX]
                    for base, b, done in ((QC, T_BANK, s_K), (0, Q_BANK, s_Q)):
                        if b == Q_BANK:
                            upto(pe, s_att, 2 * i)
                        for c in range(CH):
                            hi, lo, mix = parts(base + c * P, P)
                            ins = five(bank[:, b, c * P:(c + 1) * P],
                                       ((hi, x0h), (lo, x0h), (hi, x0l), (mix, x1h), (mix, x1l)))
                        ins.then_inc(done, 1)

                if within(k, NT + 5):
                    upto(pe, s_v, clip(i + 2, NT + 1))
                    upto(pe, s_h2, clip(i - 2, NT))
                    upto(pe, s_lg, i - 4)
                    ins = None
                    if within(i - 4, NT):
                        pe.wait_ge(s_x2t, i - 3)
                        at = bank[:, V_BANK, QC:QC + 2 * E]
                        pe.matmul(at, x2t[:, 0, :], wr_sb[:, 0, :], start=True, stop=False)
                        ins = pe.matmul(at, x2t[0:D2, 1, :], wr_sb[0:D2, 1, :], start=False, stop=True)
                    if within(k, NT):
                        hi, lo, mix = parts(2 * QC, D)
                        ins = five(bank[:, V_BANK, 0:D],
                                   ((x0h, hi), (x0h, lo), (x0l, hi), (x1h, mix), (x1l, mix)))
                    if within(i - 2, NT):
                        pe.wait_ge(s_Tlo, i + 2)
                        a0h, a1h = t_hi[:, DX:DX + P], t_hi[:, DX + P:]
                        a0l, a1l = t_lo[:, DX:DX + P], t_lo[:, DX + P:]
                        hi, lo, mix = parts(2 * QC + D, D)
                        ins = five(bank[:, V_BANK, D:2 * D],
                                   ((a0h, hi), (a0h, lo), (a0l, hi), (a1h, mix), (a1l, mix)))
                    if ins is not None:
                        ins.then_inc(s_VY, 1)
                    else:
                        pe.sem_inc(s_VY, 1)

                def transposes(r):
                    if within(i, NT):
                        pe.wait_ge(s_P[r], i + 1)
                        for c in range(CH):
                            ins = pe.transpose(bank[:, r, c * P:(c + 1) * P], probs[:, r, c, :], ident[:, :])
                        ins.then_inc(s_PT[r], 1)

                def weighted(r):
                    if within(i, NT):
                        pe.wait_ge(s_PTe[r], i + 1)
                        for c in range(CH):
                            hd = RG * c + r
                            ins = pe.matmul(bank[:, Q_BANK, hd * (HD + 1):(hd + 1) * (HD + 1)],
                                            probs_t[:, r, c, :], v_sb[:, par, hd, :], start=True, stop=True)
                        if r == RG - 1:
                            ins.then_inc(s_O, 1)

                transposes(0)
                transposes(1)
                if within(i, NT):
                    pe.wait_ge(s_v, i + 2)
                    pe.wait_ge(s_q, clip(i + 2, NT))
                    upto(pe, s_att, 2 * i)
                weighted(0)
                transposes(2)
                if within(i - 3, NT):
                    pe.wait_ge(s_xn2, 2 * (i - 2))
                    upto(pe, s_x2t, i - 3)
                    ins = transposed(X2_BANK, 0, xn2[:, 1 - par, :])
                    ins.then_inc(s_X2, 1)
                if within(j, NT + 3):
                    upto(pe, s_klo, clip(i + 2, NT))
                    upto(pe, s_Tlo, i + 2)
                    if within(j, NT):
                        pe.wait_ge(s_xn, 2 * j + 2)
                        ins = transposed(T_BANK, 0, xn[:, par, :])
                    if within(i - 1, NT):
                        pe.wait_ge(s_att, 2 * i)
                        ins = transposed(T_BANK, DX, att[:, :])
                    ins.then_inc(s_T, 1)
                weighted(1)
                transposes(3)
                weighted(2)
                weighted(3)

            pe.wait_ge(s_biases, 16 * 4)
            steps(pe, body)

            pe.wait_ge(s_pmc, 1)
            pe.transpose(bank[0:NT, 2, 0:P], pm_c[:, :], ident[:, :]).then_inc(s_pmT, 1)

            def counts(u):
                pe.wait_ge(s_ohx, u + 1)
                flat = ohx[:, :, :].rearrange("p i e -> p (i e)")
                pe.matmul(bank[:, 7, 0:NT * E], before[:, :], flat, start=True, stop=True)
                pe.matmul(bank[:, 7, NT * E:2 * NT * E], ones[:, :], flat, start=True, stop=True).then_inc(s_pre, 1)

            def invert(u):
                n_t = TC if u == 0 else TU
                pe.wait_ge(s_perm, u + 1)
                at = bank[:, 7, 256:256 + 2 * n_t].rearrange("p (a t) -> p a t", a=2)
                for n in range(NT):
                    ins = pe.matmul(at, oh_s[:, n, :], oh_m[:, n, :, 0:n_t], start=(n == 0), stop=(n == NT - 1))
                ins.then_inc(s_inv, 1)

            counts(0)
            invert(0)

            pe.wait_ge(s_esplit, 4 * E)
            pe.wait_ge(s_route, 1)
            pe.wait_ge(s_pmt, 1)

            def tiles(t, par, e, ranks=False):
                if within(t + 1, TT):
                    pe.wait_ge(s_gather, 16 * (t + 2))
                    upto(pe, s_xlo, t + 1)
                    ins = transposed(4, 0, xg[:, 1 - par, :])
                    ins.then_inc(s_XT, 1)
                if within(t, TT):
                    x0h, x1h = xg_hi[:, par, 0:P], xg_hi[:, par, P:DX]
                    x0l, x1l = xg_lo[:, par, 0:P], xg_lo[:, par, P:DX]
                    pe.wait_ge(s_xlo, t + 1)
                    for half in range(2):
                        upto(pe, s_g[half], t - 1)
                        for f in range(3 * half, 3 * half + 3):
                            def w(src, part, f=f):
                                return wide(src[:, ds(e[1], 1), part * F + f * P:part * F + (f + 1) * P])
                            ins = five(bank[:, 2 * par + half, (f % 3) * P:(f % 3 + 1) * P],
                                       ((w(e_hi, 0), x0h), (w(e_lo, 0), x0h), (w(e_hi, 0), x0l),
                                        (w(e_lo, 1), x1h), (w(e_lo, 1), x1l)))
                        ins.then_inc(s_H[half], 1)
                if ranks and within(t - 1, NT):
                    b = t - 1
                    first = isinstance(b, int) and b == 0
                    pe.wait_ge(s_less, b + 1)
                    for n in range(NT):
                        ins = pe.matmul(bank[:, 6, n * E:(n + 1) * E], less[:, 1 - par, n * P:(n + 1) * P],
                                        wide(oh[:, ds(2 * b, 1), :]), start=(first and n == 0), stop=False,
                                        skip_group_check=True)
                    ins.then_inc(s_cnt, 1)
                if within(t - 1, TT):
                    o = t - 1
                    pe.wait_ge(s_glo, 2 * (o + 1))
                    upto(pe, s_yb, o)
                    for c in range(FC):
                        ah, al = act_hi[:, 1 - par, c * P:(c + 1) * P], act_lo[:, 1 - par, c * P:(c + 1) * P]
                        cols = slice(2 * F + c * D, 2 * F + (c + 1) * D)
                        wh, wl = wide(e_hi[:, ds(e[0], 1), cols]), wide(e_lo[:, ds(e[0], 1), cols])
                        pe.matmul(bank[:, 5, 0:D], ah, wh, start=(c == 0), stop=False)
                        pe.matmul(bank[:, 5, 0:D], ah, wl, start=False, stop=False)
                        ins = pe.matmul(bank[:, 5, 0:D], al, wh, start=False, stop=(c == FC - 1))
                    ins.then_inc(s_Y, 1)

            def last_rank():
                b = NT - 1
                pe.wait_ge(s_less, b + 1)
                for n in range(NT):
                    ins = pe.matmul(bank[:, 6, n * E:(n + 1) * E], less[:, b % 2, n * P:(n + 1) * P],
                                    oh[:, 2 * b, :], start=False, stop=True, skip_group_check=True)
                ins.then_inc(s_cnt, 1)
                counts(1)

            slot_steps(pe, tiles, {NT: last_rank, NT + 1: lambda: invert(1)}, mybir.EngineType.PE)


_ORDER = ["ids", "types", "word", "pos", "type_emb", "gamma", "beta", "wqkvp", "b_proj", "wr", "br",
          "wexp", "b1", "b2"]


def kernel(**inputs):
    import numpy as np
    import concourse.bacc as bacc
    from concourse import mybir as mb
    from concourse.bass_utils import run_bass_kernel_spmd as run

    a = {k: np.asarray(v) for k, v in inputs.items()}
    laid = {}
    laid["ids"] = a["x"].T
    laid["types"] = a["mask_BS_i1_0"].T
    laid["word"] = a["L0_tok_word_emb"]
    laid["pos"] = a["L0_tok_pos_emb"][:P]
    laid["type_emb"] = a["L0_tok_type_emb"]
    laid["gamma"] = a["L0_tok_ln_gamma"][None]
    laid["beta"] = a["L0_tok_ln_beta"][None]
    laid["b_proj"] = a["L0_attn_b_proj"][None]

    def halves(w):
        return np.stack([w[:P], np.concatenate([w[P:], w[P:]])])

    w = a["L0_attn_w_qkv"].T
    twice = [np.repeat(w[:, n * D:(n + 1) * D].reshape(D, HEADS, 1, HD), 2, axis=2).reshape(D, QC)
             for n in range(2)]
    laid["wqkvp"] = halves(np.concatenate(twice + [w[:, 2 * D:], a["L0_attn_w_proj"].T], axis=1))
    wr = np.concatenate([a["L0_ffn_Wsc"], a["L0_ffn_Wsu"]], axis=1)
    laid["wr"] = halves(wr).transpose(1, 0, 2)
    laid["br"] = np.concatenate([a["L0_ffn_bsc"], a["L0_ffn_bsu"]])[None]
    w1 = np.concatenate([a["L0_ffn_W1c"], a["L0_ffn_W1u"]])
    w2 = np.concatenate([a["L0_ffn_W2c"], a["L0_ffn_W2u"]])
    laid["wexp"] = np.concatenate([
        np.concatenate([*halves(w1[e]), w2[e].reshape(FC, P, D).transpose(1, 0, 2).reshape(P, FC * D)], axis=1)
        for e in range(2 * E)], axis=1)
    laid["b1"] = np.concatenate([a["L0_ffn_b1c"], a["L0_ffn_b1u"]]).reshape(2 * E, FC, P).transpose(2, 0, 1)
    laid["b2"] = np.concatenate([a["L0_ffn_b2c"], a["L0_ffn_b2u"]]).reshape(1, 2 * E * D)

    nc = bacc.Bacc("TRN2", target_bir_lowering=False, num_devices=1)
    arrays, args = {}, []
    for name in _ORDER:
        arrays[f"in_{name}"] = np.ascontiguousarray(laid[name])
        args.append(nc.dram_tensor(f"in_{name}", laid[name].shape, mb.dt.from_np(laid[name].dtype),
                                   kind="ExternalInput").ap())
    args.append(nc.dram_tensor("xrows", (N, DX), mb.dt.float32).ap())
    args.append(nc.dram_tensor("prow_dram", (N,), mb.dt.float32).ap())
    out = nc.dram_tensor("out_0", (N, D), mb.dt.float32, kind="ExternalOutput").ap()
    build(nc, *args, out)
    got = run(nc, [arrays], core_ids=[0]).results[0]["out_0"]
    return got.reshape(SEQS, P, D)
```

```python
from contextlib import ExitStack

import concourse.bass as bass
from concourse import mybir

F32 = mybir.dt.float32
F16 = mybir.dt.float16
BF16 = mybir.dt.bfloat16
I32 = mybir.dt.int32
ALU = mybir.AluOpType
ACT = mybir.ActivationFunctionType
AX = mybir.AxisListType.X
ds = bass.ds

P = 128
SEQS = 16
NT = SEQS
N = NT * P
D = 192
D2 = D - P
DX = 2 * P
HEADS = 12
HD = D // HEADS
RG = 4
CH = HEADS // RG
QC = CH * P
F = 768
FC = F // P
E = 4
CAP = N // E
TC = NT + E - 1
TU = (N - CAP) // P + E - 1
TT = TC + TU
EPS = 1e-5

XS = 2.0 ** 11
QS = 2.0 ** 4
VS = 2.0 ** -3
GS = 2.0 ** 6
UN = 1.0 / (XS * XS)
SCORE = HD ** -0.5 / (QS * QS)
TIE = 2.0 ** -28
LOWER = 1.0 - 2.0 ** -24
WE = 2 * F + FC * D


def upto(engine, semaphore, count):
    if not isinstance(count, int) or count > 0:
        engine.wait_ge(semaphore, count)


def alone(engine, passed):
    engine.sem_inc(passed, 1)


def stages(first, second, swapped):
    for stage in ((second, first) if swapped else (first, second)):
        stage()


def clip(count, most):
    return min(count, most) if isinstance(count, int) else count


def within(i, n):
    return not isinstance(i, int) or 0 <= i < n


def build(nc, ids, types, word, pos, type_emb, gamma, beta, wqkvp, b_proj,
          wr, br, wexp, b1, b2, xrows, prow_dram, out):
    with ExitStack() as ctx:
        def sb(name, shape, dt):
            return ctx.enter_context(nc.sbuf_tensor(name, shape, dt))

        def sem(name):
            return ctx.enter_context(nc.semaphore(name))

        ident = sb("ident", [P, P], F32)
        before = sb("before", [P, P], F16)
        ones = sb("ones", [P, P], F16)
        low_rows = sb("low_rows", [P, 1], F32)
        low_heads_i = sb("low_heads_i", [P, 1], I32)
        low_heads = sb("low_heads", [P, 1], F32)
        minus_half = sb("minus_half", [P, 1], F32)
        iota_s = sb("iota_s", [P, P], F32)
        iota_t = sb("iota_t", [P, TC], F32)
        token1 = sb("token1", [P, NT], F32)
        tie = sb("tie", [P, P], BF16)
        ids_sb = sb("ids_sb", [P, NT + 1], I32)
        types_sb = sb("types_sb", [P, NT + 1], I32)
        types_f = sb("types_f", [P, NT + 1], F32)
        pos_sb = sb("pos_sb", [P, D], F32)
        ty = sb("ty", [P, 2, D], F32)
        gamma_sb = sb("gamma_sb", [P, D], F32)
        beta_sb = sb("beta_sb", [P, D], F32)
        bproj_sb = sb("bproj_sb", [P, D], F32)
        wr_sb = sb("wr_sb", [P, 2, 2 * E], F32)
        br_sb = sb("br_sb", [P, 2 * E], F32)
        b1_sb = sb("b1_sb", [P, 2 * E, FC], F32)
        b2_sb = sb("b2_sb", [P, 2 * E, D], F32)
        AC = 2 * QC + D + D
        w_hi = sb("w_hi", [P, AC], F16)
        w_lo = sb("w_lo", [P, AC], F16)
        w_mix = sb("w_mix", [P, AC], F16)
        w_tmp = sb("w_tmp", [P, AC], F16)
        stage = sb("stage", [P, 2, WE], F32)
        e_hi = sb("e_hi", [P, 2 * E, WE], F16)
        e_lo = sb("e_lo", [P, 2 * E, WE], F16)
        piece_cols = ((0, 2 * F), (2 * F, WE))

        we = sb("we", [P, 2, D], F32)
        hg = sb("hg", [P, D], F32)
        h = sb("h", [P, 2, D], F32)
        hb = sb("hb", [P, 4, D], F32)
        stats = sb("stats", [P, 3, 6], F32)
        mv = sb("mv", [P, 3, 2], F32)
        vare = sb("vare", [P, 3, 1], F32)
        mneg = sb("mneg", [P, 3, 1], F32)
        rstd = sb("rstd", [P, 3, 1], F32)
        xn = sb("xn", [P, 2, DX], F32)
        att = sb("att", [P, DX], F32)
        t_hi = sb("t_hi", [P, 2 * DX], F16)
        t_lo = sb("t_lo", [P, 2 * DX], F16)
        q_low = sb("q_low", [P, QC], F16)
        q_sb = sb("q_sb", [P, 2, QC], F16)
        k_hi = sb("k_hi", [P, 2, QC], F16)
        k_lo = sb("k_lo", [P, 2, QC], F16)
        v_sb = sb("v_sb", [P, 2, HEADS, HD + 1], F32)
        rawmax = sb("rawmax", [P, RG, CH], F32)
        negmax = sb("negmax", [P, RG, CH], F32)
        probs = sb("probs", [P, RG, CH, P], F32)
        probs_t = sb("probs_t", [P, RG, CH, P], F32)
        rden = sb("rden", [P, HEADS, 1], F32)
        HS = F + 4 * DX + 3 * D
        hs = sb("hs", [P, HS], F32)
        h2 = hs[:, 0:2 * D].rearrange("p (a d) -> p a d", a=2)
        xn2 = sb("xn2", [P, 2, DX], F32)
        x2t = sb("x2t", [P, 2, P], F32)
        logits = sb("logits", [P, NT, 2 * E], F32)

        R2 = NT * 2
        top = sb("top", [P, R2], F32)
        lg = sb("lg", [P, R2, E], F32)
        ex = sb("ex", [P, R2, E], F32)
        den = sb("den", [P, R2], F32)
        rec = sb("rec", [P, R2], F32)
        pr = sb("pr", [P, R2, E], F32)
        pmax = sb("pmax", [P, R2], F32)
        eq = sb("eq", [P, R2, E], F32)
        seen = sb("seen", [P, 2, R2], F32)
        oh = sb("oh", [P, R2, E], F16)
        pm_rec = sb("pm_rec", [P, R2], F32)
        scale = sb("scale", [P, R2], F32)
        pm_c = sb("pm_c", [P, NT], F32)
        pmt = sb("pmt", [NT, P], F32)
        prow = sb("prow", [P, N], F32)
        crow = sb("crow", [P, N], F32)
        pml = sb("pml", [NT, P], F32)
        less = sb("less", [P, 2, N], F16)
        rank4 = sb("rank4", [P, NT, E], F32)
        rank = sb("rank", [P, NT], F32)
        dropped = sb("dropped", [P, NT], F32)
        ohx = sb("ohx", [P, NT + 1, E], F16)
        tot = sb("tot", [P, E], F32)
        tiles_i = sb("tiles_i", [P, E], I32)
        ends = sb("ends", [P, 3, 2 * E], F32)
        ge = sb("ge", [P, TC, E - 1], F32)
        tile_e = sb("tile_e", [P, TC], F32)
        pos2 = sb("pos2", [P, NT, E], F32)
        pos3 = sb("pos3", [P, NT, E], F32)
        slot = sb("slot", [P, NT], F32)
        slot_i = sb("slot_i", [P, NT], I32)
        slot_hi = sb("slot_hi", [P, NT], I32)
        slot_lo = sb("slot_lo", [P, NT], I32)
        slot_hf = sb("slot_hf", [P, NT], F32)
        slot_lf = sb("slot_lf", [P, NT], F32)
        valid = sb("valid", [P, NT], F32)
        tokv = sb("tokv", [P, NT], F32)
        scv = sb("scv", [P, NT], F32)
        st = stage[:, :, :].rearrange("p a n -> p (a n)")
        oh_s = st[:, 0:N // 2].bitcast(F16).rearrange("p (t s) -> p t s", t=NT)
        at0 = N // 2 + 3 * F
        oh_t = st[:, at0:at0 + NT * TC].rearrange("p (i t) -> p i t", i=NT)
        oh_m = st[:, at0 + NT * TC:at0 + 2 * NT * TC].bitcast(F16).rearrange("p (i a t) -> p i a t", i=NT, a=2)
        inv = sb("inv", [P, 2, TC], F32)
        empty = sb("empty", [P, TC], F32)
        out_f = sb("out_f", [P, TC], F32)
        experts = sb("experts", [1, TT], I32)
        idx_in = sb("idx_in", [P, TT], I32)
        idx_out = sb("idx_out", [P, TT], I32)
        slot_scale = sb("slot_scale", [P, TT], F32)

        now_in = sb("now_in", [P, 2, 1], I32)
        now_out = sb("now_out", [P, 2, 1], I32)
        act = st[:, N // 2:N // 2 + 2 * F].rearrange("p (a f) -> p a f", a=2)
        act_hi = st[:, N // 2 + 2 * F:N // 2 + 3 * F].bitcast(F16).rearrange("p (a f) -> p a f", a=2)
        act_lo = hs[:, 0:F].bitcast(F16).rearrange("p (a f) -> p a f", a=2)
        xg = hs[:, F:F + 2 * DX].rearrange("p (a d) -> p a d", a=2)
        xg_hi = hs[:, F + 2 * DX:F + 3 * DX].bitcast(F16).rearrange("p (a d) -> p a d", a=2)
        xg_lo = hs[:, F + 3 * DX:F + 4 * DX].bitcast(F16).rearrange("p (a d) -> p a d", a=2)
        yb = hs[:, F + 4 * DX:F + 4 * DX + D]
        y = hs[:, F + 4 * DX + D:F + 4 * DX + 3 * D].rearrange("p (a d) -> p a d", a=2)

        bank = ctx.enter_context(nc.psum_tensor("bank", [P, 8, 512], F32))
        V_BANK, X2_BANK, T_BANK, Q_BANK = 4, 5, 6, 7

        s_ids, s_emb, s_small, s_wqkv, s_biases, s_b2 = sem("s_ids"), sem("s_emb"), sem("s_small"), sem("s_wqkv"), sem("s_biases"), sem("s_b2")
        s_exp = [sem("s_exp0"), sem("s_exp1")]
        s_word = sem("s_word")
        s_out0, s_x = sem("s_out0"), sem("s_x")
        s_pm_st, s_pm_ld = [sem("s_pm_st0"), sem("s_pm_st1")], sem("s_pm_ld")
        s_gather, s_scatter = sem("s_gather"), sem("s_scatter")
        s_const, s_pconst, s_types, s_pt = sem("s_const"), sem("s_pconst"), sem("s_types"), sem("s_pt")
        s_dconst = sem("s_dconst")
        s_whi, s_wsplit, s_ehi, s_esplit = sem("s_whi"), sem("s_wsplit"), sem("s_ehi"), sem("s_esplit")
        s_warm = sem("s_warm")
        s_past_dve, s_past_pool, s_past_sp = sem("s_past_dve"), sem("s_past_pool"), sem("s_past_sp")
        s_tsel, s_e0 = sem("s_tsel"), sem("s_e0")
        s_st = [sem(f"s_st{n}") for n in range(3)]
        s_mv = [sem(f"s_mv{n}") for n in range(3)]
        s_ve = [sem(f"s_ve{n}") for n in range(3)]
        s_rs = [sem(f"s_rs{n}") for n in range(3)]
        s_mneg = [sem(f"s_mneg{n}") for n in range(3)]
        s_hg, s_h, s_hb, s_xn = sem("s_hg"), sem("s_h"), sem("s_hb"), sem("s_xn")
        s_T, s_Thi, s_Tlo = sem("s_T"), sem("s_Thi"), sem("s_Tlo")
        s_Q, s_K, s_VY = sem("s_Q"), sem("s_K"), sem("s_VY")
        s_qlow, s_q, s_khi, s_klo = sem("s_qlow"), sem("s_q"), sem("s_khi"), sem("s_klo")
        s_v, s_h2 = sem("s_v"), sem("s_h2")
        s_S = [sem(f"s_S{r}") for r in range(RG)]
        s_max, s_nmax = sem("s_max"), sem("s_nmax")
        s_P = [sem(f"s_P{r}") for r in range(RG)]
        s_PT = [sem(f"s_PT{r}") for r in range(RG)]
        s_PTe = [sem(f"s_PTe{r}") for r in range(RG)]
        s_O, s_rd, s_att = sem("s_O"), sem("s_rd"), sem("s_att")
        s_xn2 = sem("s_xn2")
        s_X2, s_x2t, s_lg = sem("s_X2"), sem("s_x2t"), sem("s_lg")
        s_r = sem("s_r")
        s_ex = sem("s_ex")
        s_ohx, s_pre, s_perm, s_inv = sem("s_ohx"), sem("s_pre"), sem("s_perm"), sem("s_inv")
        s_route, s_route_out = sem("s_route"), sem("s_route_out")
        s_pmc, s_pmT, s_pmt, s_pml = sem("s_pmc"), sem("s_pmT"), sem("s_pmt"), sem("s_pml")
        s_crow, s_lt, s_less, s_cnt = sem("s_crow"), sem("s_lt"), sem("s_less"), sem("s_cnt")
        s_now_in, s_now_out = sem("s_now_in"), sem("s_now_out")
        s_XT, s_xhi, s_xlo = sem("s_XT"), sem("s_xhi"), sem("s_xlo")
        s_H = [sem("s_H0"), sem("s_H1")]
        s_g = [sem("s_g0"), sem("s_g1")]
        s_ghi, s_glo = sem("s_ghi"), sem("s_glo")
        s_Y, s_yb, s_y = sem("s_Y"), sem("s_yb"), sem("s_y")
        N_CONST = 8

        wide = lambda t: t.rearrange("p t d -> p (t d)")
        all_hi, all_lo = wide(e_hi[:, :, :]), wide(e_lo[:, :, :])

        def steps(engine, body):
            for i in range(-2, 5):
                body(i, i % 2)
            with engine.Fori(5, NT - 4, 2) as i:
                body(i, 1)
                body(i + 1, 0)
            for i in range(NT - 3, NT + 4):
                body(i, i % 2)

        def has_piece(i):
            return within(i, 4 * E)

        def piece_at(i, par, tensor):
            a, b = piece_cols[par]
            return tensor[:, ds((i - par) * (WE // 2) + a, b - a)]

        def late(t):
            return isinstance(t, int) and t in (0, TC - 1, TC)

        def slot_steps(engine, body, after, looked_up=None):
            def lookup(first, n):
                return nc.values_load_multi_w_load_instructions(
                    experts[0:1, ds(first, n)], engines=[looked_up], min_val=0, max_val=2 * E - 1,
                    skip_runtime_bounds_check_because="a count of E - 1 comparisons, plus 0 or E")[1]

            def one(t, **kw):
                e = (None, None)
                if looked_up and 0 <= t <= TT:
                    if t in (0, TC):
                        engine.wait_ge(s_route, 1 + (t == TC))
                    first = max(t - 1, 0)
                    found = lookup(first, min(t, TT - 1) - first + 1)
                    e = (found[0] if t > 0 else None, found[-1] if t < TT else None)
                body(t, t % 2, e, **kw)

            def two(t, **kw):
                e = lookup(t - 1, 3) if looked_up else (None, None, None)
                body(t, 0, e[0:2], **kw)
                body(t + 1, 1, e[1:3], **kw)

            for t in range(-2, 4):
                one(t, ranks=True)
            with engine.Fori(4, NT - 1, 2) as t:
                two(t, ranks=True)
            if NT - 1 in after:
                after[NT - 1]()
            for t in range(NT, TC + 1):
                one(t)
                if t in after:
                    after[t]()
            with engine.Fori(TC + 1, TT - 3, 2) as t:
                two(t)
            for t in range(TT - 2, TT + 2):
                one(t)

        block = ctx.enter_context(nc.Block())

        @block.sync
        def _(sp):
            sp.dma_start(ids_sb[:, 0:NT], ids).then_inc(s_ids, 16)
            sp.dma_start(types_sb[:, 0:NT], types).then_inc(s_emb, 16)
            sp.dma_start(wide(ty[:, :, :]), type_emb.broadcast_to([P, 2 * D])).then_inc(s_emb, 16)
            sp.dma_start(pos_sb[:, :], pos).then_inc(s_emb, 16)
            sp.dma_start(st[:, 0:AC], wqkvp[0]).then_inc(s_wqkv, 16)
            sp.dma_start(st[:, AC:2 * AC], wqkvp[1]).then_inc(s_wqkv, 16)
            sp.dma_start(gamma_sb[:, :], gamma.broadcast_to([P, D])).then_inc(s_small, 16)
            sp.dma_start(beta_sb[:, :], beta.broadcast_to([P, D])).then_inc(s_small, 16)
            sp.dma_start(bproj_sb[:, :], b_proj.broadcast_to([P, D])).then_inc(s_small, 16)
            sp.wait_ge(s_word, 16)
            sp.dma_start(wr_sb[:, :, :], wr).then_inc(s_biases, 16)
            sp.dma_start(br_sb[:, :], br.broadcast_to([P, 2 * E])).then_inc(s_biases, 16)
            sp.dma_start(b1_sb[:, :, :], b1).then_inc(s_biases, 16)

            def load_piece(i, par):
                a, b = piece_cols[par]
                sp.dma_start(stage[:, 1, a:b], piece_at(i, par, wexp)).then_inc(s_exp[par], 16)

            sp.wait_ge(s_word, 16 * 2)
            load_piece(0, 0)

            def body(i, par):
                if has_piece(i + 1) and not (isinstance(i, int) and i < 0):
                    upto(sp, s_esplit, i)
                    alone(sp, s_past_sp)
                    load_piece(i + 1, 1 - par)
                if within(i - 2, NT):
                    b = i - 2
                    sp.wait_ge(s_h2, b + 1)
                    alone(sp, s_past_sp)
                    upto(sp, s_out0, 16 * b)
                    alone(sp, s_past_sp)
                    sp.dma_start(out[ds(b * P, P), :], h2[:, par, :]).then_inc(s_out0, 16)
                    sp.wait_ge(s_xn2, 2 * b + 2)
                    alone(sp, s_past_sp)
                    upto(sp, s_x, 16 * b)
                    alone(sp, s_past_sp)
                    sp.dma_start(xrows[ds(b * P, P), :], xn2[:, par, :]).then_inc(s_x, 16)

            steps(sp, body)
            sp.dma_start(wide(b2_sb[:, :, :]), b2.broadcast_to([P, 2 * E * D])).then_inc(s_b2, 16)
            for row, (source, ready) in enumerate(((pmt, s_pmt), (pml, s_pml))):
                sp.wait_ge(ready, 1)
                sp.dma_start(prow_dram[row].rearrange("(i p) -> i p", p=P), source[:, :]).then_inc(s_pm_st[row], 16)
            for row, to in enumerate((prow, crow)):
                sp.wait_ge(s_pm_st[row], 16)
                sp.dma_start(to[:, :], prow_dram[row:row + 1].broadcast_to([P, N])).then_inc(s_pm_ld, 16)
            sp.wait_ge(s_pm_ld, 32)

        @block.gpsimd
        def _(pool):
            pool.wait_ge(s_ids, 16)

            pool.memset(ids_sb[:, NT:], 0).then_inc(s_pconst, 1)
            pool.memset(types_sb[:, NT:], 0).then_inc(s_pconst, 1)
            pool.memset(minus_half[:, :], -0.5).then_inc(s_const, 1)
            pool.memset(ident[:, :], 0.0).then_inc(s_pconst, 1)
            pool.memset(ones[:, :], 1.0).then_inc(s_pconst, 1)
            pool.memset(tie[:, :], 0.0).then_inc(s_pconst, 1)
            pool.memset(low_rows[:, :], 0.0).then_inc(s_pconst, 1)
            pool.wait_ge(s_pconst, 6)
            pool.affine_select(out=ident[:, :], in_=ident[:, :], compare_op=ALU.not_equal, fill=1.0,
                               base=0, pattern=[[-1, P]], channel_multiplier=1).then_inc(s_const, 1)
            pool.affine_select(out=before[:, :], in_=ones[:, :], compare_op=ALU.is_gt, fill=0.0,
                               base=0, pattern=[[1, P]], channel_multiplier=-1).then_inc(s_const, 1)
            pool.wait_ge(s_const, 3)
            pool.memset(low_rows[P // 2:P, :], XS).then_inc(s_const, 1)
            pool.wait_ge(s_const, 4)
            pool.iota(low_heads_i[:, :], pattern=[[0, 1]], base=0, channel_multiplier=1).then_inc(s_const, 1)
            pool.wait_ge(s_emb, 16 * 3)
            pool.tensor_tensor(pos_sb[:, :], pos_sb[:, :], ty[:, 0, :], ALU.add).then_inc(s_pt, 1)
            pool.tensor_tensor(ty[:, 1, :], ty[:, 1, :], ty[:, 0, :], ALU.subtract).then_inc(s_pt, 1)
            pool.tensor_copy(types_f[:, :], types_sb[:, :]).then_inc(s_types, 1)
            pool.wait_ge(s_const, 1)
            pool.wait_ge(s_pt, 2)
            pool.wait_ge(s_types, 1)

            def embed(j, par):
                pool.tensor_tensor(we[:, par, :], ty[:, 1, :], types_f[:, ds(j, 1)].broadcast_to([P, D]),
                                   ALU.mult).then_inc(s_tsel, 1)
                pool.tensor_copy(now_in[:, par, :], ids_sb[:, ds(j, 1)]).then_inc(s_now_in, 1)
                pool.wait_ge(s_tsel, j + 1)
                pool.tensor_tensor(we[:, par, :], we[:, par, :], pos_sb[:, :], ALU.add).then_inc(s_e0, 1)
                pool.wait_ge(s_now_in, j + 1)
                alone(pool, s_past_pool)
                pool.wait_ge(s_e0, j + 1)
                alone(pool, s_past_pool)
                pool.indirect_dma_start(
                    out=we[:, par, :], out_offset=None, in_=word,
                    in_offset=bass.IndirectOffsetOnAxis(ap=now_in[:, par, :], axis=0),
                    compute_op=ALU.add).then_inc(s_word, 16)

            def rstd_of(n, count):
                pool.wait_ge(s_mv[n], count)
                alone(pool, s_past_pool)
                pool.tensor_scalar(vare[:, n, :], mv[:, n, 1:2], EPS, None, ALU.add).then_inc(s_ve[n], 1)
                if n > 0:
                    pool.tensor_scalar(mneg[:, n, :], mv[:, n, 0:1], -1.0, None, ALU.mult).then_inc(s_mneg[n], 1)
                pool.wait_ge(s_ve[n], count)
                pool.tensor_tensor(rstd[:, n, :], vare[:, n, :], minus_half[:, :], ALU.pow).then_inc(s_rs[n], 1)

            def centred(to, source, n, count, done):
                pool.wait_ge(s_rs[n], count)
                alone(pool, s_past_pool)
                pool.wait_ge(s_mneg[n], count)
                alone(pool, s_past_pool)
                for lo, at in ((0, 0), (P, D)):
                    pool.tensor_scalar(to[:, at:at + D - lo], source[:, lo:], mneg[:, n, :], rstd[:, n, :],
                                       ALU.add, ALU.mult).then_inc(done, 1)

            embed(0, 0)
            pool.wait_ge(s_word, 16)
            embed(1, 1)
            pool.wait_ge(s_small, 16 * 3)

            def body(i, par):
                j = i + 2
                if within(j, NT):
                    rstd_of(0, j + 1)
                    rstd_of(1, j + 1)
                    upto(pool, s_T, j - 1)
                    alone(pool, s_past_pool)
                    centred(xn[:, par, :], h[:, par, :], 1, j + 1, s_xn)
                    if within(j + 2, NT + 1):
                        pool.wait_ge(s_hg, j + 1)
                        alone(pool, s_past_pool)
                        pool.wait_ge(s_word, 16 * (j + 2))
                        embed(j + 2, par)
                    upto(pool, s_h2, j - 3)
                    pool.tensor_tensor(wide(hb[:, ds(j % 4, 1), :]), h[:, par, :], bproj_sb[:, :],
                                       ALU.add).then_inc(s_hb, 1)
                if within(i - 2, NT):
                    rstd_of(2, i - 1)
                    upto(pool, s_X2, i - 3)
                    alone(pool, s_past_pool)
                    upto(pool, s_x, 16 * (i - 3))
                    alone(pool, s_past_pool)
                    centred(xn2[:, par, :], h2[:, par, :], 2, i - 1, s_xn2)

            steps(pool, body)

            pool.iota(iota_s[:, :], pattern=[[1, P]], base=0, channel_multiplier=0,
                      allow_small_or_imprecise_dtypes=True).then_inc(s_const, 1)
            pool.iota(iota_t[:, :], pattern=[[1, TC]], base=0, channel_multiplier=0,
                      allow_small_or_imprecise_dtypes=True).then_inc(s_const, 1)
            pool.iota(token1[:, :], pattern=[[P, NT]], base=1, channel_multiplier=1,
                      allow_small_or_imprecise_dtypes=True).then_inc(s_const, 1)
            pool.affine_select(out=tie[:, :], in_=tie[:, :], compare_op=ALU.is_ge, fill=TIE,
                               base=0, pattern=[[-1, P]], channel_multiplier=1).then_inc(s_dconst, 1)

            pool.wait_ge(s_x, 16 * NT)
            pool.wait_ge(s_word, 16 * (NT + 1))
            pool.wait_ge(s_out0, 16 * NT)

            def tiles(t, par, e, ranks=False):
                g = t + 2
                if within(g, TT):
                    if isinstance(g, int) and g in (0, TC):
                        pool.wait_ge(s_route, 1 + (g == TC))
                    upto(pool, s_gather, 16 * g)
                    pool.tensor_copy(now_in[:, par, :], idx_in[:, ds(g, 1)]).then_inc(s_now_in, 1)
                    pool.wait_ge(s_now_in, NT + 1 + g + 1)
                    upto(pool, s_XT, g - 1)
                    alone(pool, s_past_pool)
                    pool.indirect_dma_start(
                        out=xg[:, par, :], out_offset=None, in_=xrows,
                        in_offset=bass.IndirectOffsetOnAxis(ap=now_in[:, par, :], axis=0)).then_inc(s_gather, 16)
                o = t - 2
                if within(o, TT):
                    if isinstance(o, int) and o in (0, TC):
                        pool.wait_ge(s_route_out, 1 + (o == TC))
                    upto(pool, s_scatter, 16 * o)
                    pool.tensor_copy(now_out[:, par, :], idx_out[:, ds(o, 1)]).then_inc(s_now_out, 1)
                    pool.wait_ge(s_now_out, o + 1)
                    pool.wait_ge(s_y, o + 1)
                    alone(pool, s_past_pool)
                    pool.indirect_dma_start(
                        out=out, out_offset=bass.IndirectOffsetOnAxis(ap=now_out[:, par, :], axis=0),
                        in_=y[:, par, :], in_offset=None, bounds_check=N - 1, oob_is_err=False,
                        compute_op=ALU.add).then_inc(s_scatter, 16)

            slot_steps(pool, tiles, {})
            pool.wait_ge(s_scatter, 16 * TT)

        @block.scalar
        def _(act_e):
            act_e.wait_ge(s_wqkv, 32)
            act_e.wait_ge(s_const, 5)
            act_e.activation(w_hi[:, :], st[:, 0:AC], ACT.Copy, scale=XS).then_inc(s_whi, 1)
            act_e.activation(w_tmp[:, :], st[:, AC:2 * AC], ACT.Copy, scale=low_rows[:, :]).then_inc(s_whi, 1)
            act_e.activation(q_low[0:1, 0:1], ident[0:1, 0:1], ACT.Exp).then_inc(s_warm, 1)
            act_e.wait_ge(s_warm, 1)
            act_e.wait_ge(s_dconst, 1)

            def body(i, par):
                def exps(r):
                    if within(i, NT):
                        act_e.wait_ge(s_nmax, 2 * i + r // 2 + 1)
                        upto(act_e, s_PT[r], i)
                        for c in range(CH):
                            ins = act_e.activation(probs[:, r, c, :], bank[:, r, c * P:(c + 1) * P], ACT.Exp,
                                                   bias=negmax[:, r, c:c + 1], scale=SCORE)
                        ins.then_inc(s_P[r], 1)

                def evac_pt(r):
                    if within(i, NT):
                        act_e.wait_ge(s_PT[r], i + 1)
                        upto(act_e, s_O, i)
                        act_e.activation(probs_t[:, r, :, :].rearrange("p c k -> p (c k)"),
                                         bank[:, r, 0:QC], ACT.Copy).then_inc(s_PTe[r], 1)

                if within(i - 4, NT):
                    act_e.wait_ge(s_X2, i - 3)
                    upto(act_e, s_VY, i + 1)
                    act_e.activation(x2t[:, :, :].rearrange("p a t -> p (a t)"), bank[:, X2_BANK, 0:DX],
                                     ACT.Copy).then_inc(s_x2t, 1)
                if has_piece(i):
                    act_e.wait_ge(s_exp[par], 8 * (i - par) + 16)
                    to, (a, b) = piece_at(i, par, all_hi), piece_cols[par]
                    if par == 0:
                        act_e.activation(to[:, 0:F], stage[:, 1, 0:F], ACT.Copy, scale=XS)
                        act_e.activation(to[:, F:2 * F], stage[:, 1, F:2 * F], ACT.Copy,
                                         scale=low_rows[:, :]).then_inc(s_ehi, 1)
                    else:
                        act_e.activation(to, stage[:, 1, a:b], ACT.Copy, scale=XS).then_inc(s_ehi, 1)
                exps(0)
                exps(1)
                if within(i + 1, NT):
                    act_e.wait_ge(s_K, i + 2)
                    act_e.activation(k_hi[:, 1 - par, :], bank[:, T_BANK, 0:QC], ACT.Copy,
                                     scale=UN * QS).then_inc(s_khi, 1)
                exps(2)
                if within(i + 1, NT):
                    act_e.wait_ge(s_Q, i + 2)
                    upto(act_e, s_q, i + 1)
                    act_e.activation(q_low[:, :], bank[:, Q_BANK, 0:QC], ACT.Copy,
                                     scale=low_heads[:, :]).then_inc(s_qlow, 1)
                evac_pt(0)
                exps(3)
                evac_pt(1)
                evac_pt(2)
                if within(i + 2, NT + 3):
                    act_e.wait_ge(s_T, i + 3)
                    upto(act_e, s_VY, i + 2)
                    lo, hi = (0 if within(i + 2, NT) else DX), (2 * DX if within(i - 1, NT) else DX)
                    act_e.activation(t_hi[:, lo:hi], bank[:, T_BANK, lo:hi], ACT.Copy, scale=XS).then_inc(s_Thi, 1)
                evac_pt(3)

            steps(act_e, body)

            act_e.wait_ge(s_r, 3)
            act_e.activation(ex[:, :, :], lg[:, :, :], ACT.Exp).then_inc(s_ex, 1)
            act_e.wait_ge(s_pmT, 1)
            act_e.activation(pmt[:, :], bank[0:NT, 2, 0:P], ACT.Copy).then_inc(s_pmt, 1)
            act_e.activation(q_low[0:1, 0:1], ident[0:1, 0:1], ACT.Gelu).then_inc(s_warm, 1)
            act_e.wait_ge(s_warm, 2)

            def tiles(t, par, e, ranks=False):
                def next_rows():
                    if within(t + 1, TT):
                        act_e.wait_ge(s_XT, t + 2)
                        upto(act_e, s_H[1], t)
                        act_e.activation(xg_hi[:, 1 - par, :], bank[:, 4, 0:DX], ACT.Copy, scale=XS).then_inc(s_xhi, 1)

                def this_tile():
                    if within(t - 2, TT):
                        o = t - 2
                        if isinstance(o, int) and o in (0, TC):
                            act_e.wait_ge(s_route_out, 1 + (o == TC))
                        act_e.wait_ge(s_yb, o + 1)
                        upto(act_e, s_scatter, 16 * (o - 1))
                        act_e.activation(y[:, par, :], yb[:, :], ACT.Copy, scale=slot_scale[:, ds(o, 1)]).then_inc(s_y, 1)
                    if within(t, TT):
                        upto(act_e, s_glo, t - 1)
                        for half in range(2):
                            act_e.wait_ge(s_H[half], t + 1)
                            for f in range(half * 3, half * 3 + 3):
                                ins = act_e.activation(
                                    act[:, par, f * P:(f + 1) * P],
                                    bank[:, 2 * par + half, (f % 3) * P:(f % 3 + 1) * P],
                                    ACT.Gelu, bias=b1_sb[:, ds(e[1], 1), f:f + 1].rearrange("p a b -> p (a b)"),
                                    scale=UN)
                            ins.then_inc(s_g[half], 1)
                        act_e.wait_ge(s_g[1], t + 1)
                        upto(act_e, s_Y, t - 1)
                        act_e.activation(act_hi[:, par, :], act[:, par, :], ACT.Copy, scale=GS).then_inc(s_ghi, 1)

                stages(next_rows, this_tile, late(t))

            slot_steps(act_e, tiles, {}, mybir.EngineType.Activation)

        @block.vector
        def _(dve):
            stt = dve.scalar_tensor_tensor
            dve.wait_ge(s_const, 5)
            dve.tensor_scalar(low_heads_i[:, :], low_heads_i[:, :], HD, None, ALU.bitwise_and).then_inc(s_r, 1)
            dve.wait_ge(s_r, 1)
            dve.memset(v_sb[:, :, :, HD:HD + 1], 1.0).then_inc(s_v, 1)
            dve.wait_ge(s_v, 1)
            dve.tensor_scalar(low_heads[:, :], low_heads_i[:, :], UN * QS / HD, None, ALU.mult).then_inc(s_dconst, 1)
            dve.wait_ge(s_whi, 1)
            stt(out=w_lo[:, :], in0=st[:, 0:AC], scalar=XS, in1=w_hi[:, :], op0=ALU.mult,
                op1=ALU.subtract).then_inc(s_wsplit, 1)
            dve.wait_ge(s_whi, 2)
            stt(out=w_mix[:, :], in0=st[:, AC:2 * AC], scalar=XS, in1=w_tmp[:, :], op0=ALU.mult,
                op1=ALU.subtract).then_inc(s_wsplit, 1)

            def bn_stats(n, source, ready, count):
                dve.wait_ge(ready, count)
                alone(dve, s_past_dve)
                dve.bn_stats(out=stats[:, n, :], in_=source).then_inc(s_st[n], 1)

            def bn_aggr(n, count, used, used_count):
                upto(dve, used, used_count)
                alone(dve, s_past_dve)
                dve.wait_ge(s_st[n], count)
                alone(dve, s_past_dve)
                dve.bn_aggr(out=mv[:, n, :], in_=stats[:, n, :]).then_inc(s_mv[n], 1)

            def body(i, par):
                j, k = i + 2, i + 1

                def maxima(r):
                    if within(i, NT):
                        dve.wait_ge(s_S[r], i + 1)
                        dve.tensor_reduce(rawmax[:, r, :], bank[:, r, 0:QC].rearrange("p (c k) -> p c k", c=CH),
                                          AX, ALU.max, negate=True).then_inc(s_max, 1)

                def scaled(r0, r1):
                    if within(i, NT):
                        dve.wait_ge(s_max, RG * i + r1)
                        upto(dve, s_P[r1 - 1], i)
                        dve.tensor_scalar(negmax[:, r0:r1, :], rawmax[:, r0:r1, :], SCORE, None,
                                          ALU.mult).then_inc(s_nmax, 1)

                if within(j, NT):
                    dve.wait_ge(s_mv[0], j + 1)
                    upto(dve, s_h, j)
                    stt(out=hg[:, :], in0=we[:, par, :], scalar=mv[:, 0, 0:1], in1=gamma_sb[:, :],
                        op0=ALU.subtract, op1=ALU.mult).then_inc(s_hg, 1)
                maxima(0)
                maxima(1)
                if within(i - 1, NT):
                    dve.wait_ge(s_O, i)
                    o = bank[:, Q_BANK, 0:HEADS * (HD + 1)].rearrange("p (h e) -> p h e", h=HEADS)
                    dve.reciprocal(rden[:, :, :], o[:, :, HD:HD + 1]).then_inc(s_rd, 1)
                scaled(0, 2)
                if within(i - 1, NT):
                    dve.wait_ge(s_rd, i)
                    dve.wait_ge(s_T, i + 2)
                    for h0, at in ((0, 0), (P // HD, D)):
                        n = HEADS - h0
                        dve.tensor_tensor(att[:, at:at + n * HD].rearrange("p (h e) -> p h e", h=n),
                                          o[:, h0:HEADS, 0:HD], rden[:, h0:HEADS, :].broadcast_to([P, n, HD]),
                                          ALU.mult).then_inc(s_att, 1)
                maxima(2)
                maxima(3)
                if within(j, NT):
                    dve.wait_ge(s_rs[0], j + 1)
                    dve.wait_ge(s_hg, j + 1)
                    upto(dve, s_hb, j - 1)
                    upto(dve, s_xn, 2 * (j - 1))
                    stt(out=h[:, par, :], in0=hg[:, :], scalar=rstd[:, 0, :], in1=beta_sb[:, :],
                        op0=ALU.mult, op1=ALU.add).then_inc(s_h, 1)
                scaled(2, RG)
                if within(j, NT):
                    bn_stats(1, h[:, par, :], s_h, j + 1)
                if within(j, NT):
                    bn_aggr(1, j + 1, s_xn, 2 * j)
                if within(k, NT):
                    upto(dve, s_S[RG - 1], k - 1)
                    dve.wait_ge(s_khi, k + 1)
                    stt(out=k_lo[:, 1 - par, :], in0=bank[:, T_BANK, 0:QC], scalar=UN * QS,
                        in1=k_hi[:, 1 - par, :], op0=ALU.mult, op1=ALU.subtract).then_inc(s_klo, 1)
                if within(k, NT):
                    dve.wait_ge(s_qlow, k + 1)
                    stt(out=q_sb[:, 1 - par, :], in0=bank[:, Q_BANK, 0:QC], scalar=UN * QS, in1=q_low[:, :],
                        op0=ALU.mult, op1=ALU.subtract).then_inc(s_q, 1)
                if within(k, NT + 5):
                    dve.wait_ge(s_VY, i + 2)
                if within(k, NT):
                    upto(dve, s_O, i)
                    dve.tensor_scalar(v_sb[:, 1 - par, :, 0:HD],
                                      bank[:, V_BANK, 0:D].rearrange("p (h e) -> p h e", h=HEADS),
                                      UN * VS, None, ALU.mult).then_inc(s_v, 1)
                if within(i - 2, NT):
                    dve.wait_ge(s_hb, i - 1)
                    upto(dve, s_out0, 16 * (i - 3))
                    upto(dve, s_xn2, 2 * (i - 3))
                    stt(out=h2[:, par, :], in0=bank[:, V_BANK, D:2 * D], scalar=UN / VS,
                        in1=wide(hb[:, ds((i - 2) % 4, 1), :]), op0=ALU.mult, op1=ALU.add).then_inc(s_h2, 1)
                if within(i - 4, NT):
                    dve.tensor_copy(wide(logits[:, ds(i - 4, 1), :]),
                                    bank[:, V_BANK, QC:QC + 2 * E]).then_inc(s_lg, 1)
                if within(i - 2, NT):
                    bn_stats(2, h2[:, par, :], s_h2, i - 1)
                if has_piece(i):
                    dve.wait_ge(s_ehi, i + 1)
                    a, b = piece_cols[par]
                    stt(out=piece_at(i, par, all_lo), in0=stage[:, 1, a:b], scalar=XS,
                        in1=piece_at(i, par, all_hi), op0=ALU.mult, op1=ALU.subtract).then_inc(s_esplit, 1)
                if within(i - 2, NT):
                    bn_aggr(2, i - 1, s_xn2, 2 * (i - 2))
                if within(j + 1, NT):
                    bn_stats(0, we[:, 1 - par, :], s_word, 16 * (j + 2))
                if within(j, NT + 3):
                    dve.wait_ge(s_Thi, i + 3)
                    lo, hi = (0 if within(j, NT) else DX), (2 * DX if within(i - 1, NT) else DX)
                    stt(out=t_lo[:, lo:hi], in0=bank[:, T_BANK, lo:hi], scalar=XS, in1=t_hi[:, lo:hi],
                        op0=ALU.mult, op1=ALU.subtract).then_inc(s_Tlo, 1)
                if within(j + 1, NT):
                    bn_aggr(0, j + 2, s_rs[0], j + 1)

            dve.wait_ge(s_small, 16 * 3)
            bn_stats(0, we[:, 0, :], s_word, 16)
            bn_aggr(0, 1, s_rs[0], 0)
            steps(dve, body)

            count = [1]

            def own(*written):
                for ins in written:
                    ins.then_inc(s_r, 1)
                count[0] += len(written)
                dve.wait_ge(s_r, count[0])

            dve.wait_ge(s_lg, NT)
            dve.wait_ge(s_biases, 16 * 3)
            by_router = logits[:, :, :].rearrange("p i (r e) -> p (i r) e", r=2)
            spread = lambda t, n: t.unsqueeze(2).broadcast_to([P, n, E])
            own(dve.tensor_tensor(logits[:, :, :], logits[:, :, :],
                                  br_sb[:, :].unsqueeze(1).broadcast_to([P, NT, 2 * E]), ALU.add))
            dve.tensor_reduce(top[:, :], by_router, AX, ALU.max).then_inc(s_rd, 1)
            dve.wait_ge(s_rd, NT + 1)
            own(dve.tensor_tensor(lg[:, :, :], by_router, spread(top[:, :], R2), ALU.subtract))
            dve.wait_ge(s_ex, 1)
            own(dve.tensor_reduce(den[:, :], ex[:, :, :], AX, ALU.add))
            own(dve.reciprocal(rec[:, :], den[:, :]))
            own(dve.tensor_tensor(pr[:, :, :], ex[:, :, :], spread(rec[:, :], R2), ALU.mult))
            own(dve.tensor_reduce(pmax[:, :], pr[:, :, :], AX, ALU.max))
            common = pmax[:, :].rearrange("p (i r) -> p i r", r=2)[:, :, 0]
            dve.tensor_copy(pm_c[:, :], common).then_inc(s_pmc, 1)
            own(dve.tensor_tensor(eq[:, :, :], pr[:, :, :], spread(pmax[:, :], R2), ALU.is_equal))
            own(dve.tensor_copy(oh[:, :, 0], eq[:, :, 0]),
                dve.tensor_tensor(oh[:, :, 1], eq[:, :, 1], eq[:, :, 0], ALU.is_gt),
                dve.tensor_tensor(seen[:, 0, :], eq[:, :, 1], eq[:, :, 0], ALU.max),
                dve.reciprocal(pm_rec[:, :], pmax[:, :]))
            own(dve.tensor_tensor(oh[:, :, 2], eq[:, :, 2], seen[:, 0, :], ALU.is_gt),
                dve.tensor_tensor(seen[:, 1, :], eq[:, :, 2], seen[:, 0, :], ALU.max),
                dve.tensor_tensor(scale[:, :], pmax[:, :], pm_rec[:, :], ALU.mult))
            own(dve.tensor_tensor(oh[:, :, 3], eq[:, :, 3], seen[:, 1, :], ALU.is_gt),
                dve.memset(ohx[:, NT, :], 0.0),
                dve.memset(ends[:, :, 0:E], 0.0))
            dve.wait_ge(s_pmt, 1)
            dve.tensor_scalar(pml[:, :], pmt[:, :], LOWER, None, ALU.mult).then_inc(s_pml, 1)
            dve.wait_ge(s_const, N_CONST)
            oh_r = oh[:, :, :].rearrange("p (i r) e -> p i r e", r=2)
            scale_r = scale[:, :].rearrange("p (i r) -> p i r", r=2)

            def route_in(u):
                if u == 0:
                    dve.tensor_copy(ohx[:, 0:NT, :], oh_r[:, :, 0, :]).then_inc(s_ohx, 1)
                    return
                dve.wait_ge(s_cnt, NT)
                own(dve.tensor_tensor(rank4[:, :, :], bank[:, 6, 0:NT * E].rearrange("p (i e) -> p i e", e=E),
                                      oh_r[:, :, 0, :], ALU.mult))
                own(dve.tensor_reduce(rank[:, :], rank4[:, :, :], AX, ALU.add))
                own(dve.tensor_scalar(dropped[:, :], rank[:, :], float(CAP), None, ALU.is_ge))
                dve.tensor_tensor(ohx[:, 0:NT, :], oh_r[:, :, 1, :], spread(dropped[:, :], NT),
                                  ALU.mult).then_inc(s_ohx, 1)

            def route_tiles(u):
                n_t, t0 = (TC, 0) if u == 0 else (TU, TC)
                dve.wait_ge(s_ohx, u + 1)
                own(dve.tensor_reduce(valid[:, :], ohx[:, 0:NT, :], AX, ALU.add))
                own(dve.tensor_tensor(tokv[:, :], token1[:, :], valid[:, :], ALU.mult),
                    dve.tensor_tensor(scv[:, :], scale_r[:, :, u], valid[:, :], ALU.mult))
                dve.wait_ge(s_pre, u + 1)
                own(dve.tensor_scalar(tot[:, :], bank[:, 7, NT * E:(NT + 1) * E], float(P - 1), None, ALU.add))
                own(dve.tensor_copy(tiles_i[:, :], tot[:, :]))
                own(dve.tensor_scalar(tiles_i[:, :], tiles_i[:, :], 7, None, ALU.logical_shift_right))
                own(dve.tensor_copy(ends[:, 0, E:], tiles_i[:, :]))
                own(dve.tensor_tensor(ends[:, 1, E:], ends[:, 0, E:], ends[:, 0, E - 1:2 * E - 1], ALU.add))
                own(dve.tensor_tensor(ends[:, 2, E:], ends[:, 1, E:], ends[:, 1, E - 2:2 * E - 2], ALU.add))
                pre = bank[:, 7, 0:NT * E].rearrange("p (i e) -> p i e", e=E)
                own(dve.tensor_tensor(ge[:, 0:n_t, :], iota_t[:, 0:n_t].unsqueeze(2).broadcast_to([P, n_t, E - 1]),
                                      ends[:, 2, E:2 * E - 1].unsqueeze(1).broadcast_to([P, n_t, E - 1]), ALU.is_ge),
                    stt(out=pos2[:, :, :], in0=ends[:, 2, E - 1:2 * E - 1].unsqueeze(1).broadcast_to([P, NT, E]),
                        scalar=float(P), in1=pre, op0=ALU.mult, op1=ALU.add))
                own(dve.tensor_reduce(tile_e[:, 0:n_t], ge[:, 0:n_t, :], AX, ALU.add),
                    dve.tensor_tensor(pos3[:, :, :], pos2[:, :, :], ohx[:, 0:NT, :], ALU.mult))
                own(dve.tensor_scalar(experts[0:1, t0:t0 + n_t], tile_e[0:1, 0:n_t], float(E * u), None, ALU.add),
                    dve.tensor_reduce(slot[:, :], pos3[:, :, :], AX, ALU.add))

            def route_one_hots(u):
                n_t = TC if u == 0 else TU
                own(dve.tensor_copy(slot_i[:, :], slot[:, :]))
                own(dve.tensor_scalar(slot_hi[:, :], slot_i[:, :], 7, None, ALU.logical_shift_right),
                    dve.tensor_scalar(slot_lo[:, :], slot_i[:, :], P - 1, None, ALU.bitwise_and))
                own(dve.tensor_copy(slot_hf[:, :], slot_hi[:, :]),
                    dve.tensor_copy(slot_lf[:, :], slot_lo[:, :]))
                own(dve.tensor_tensor(oh_t[:, :, 0:n_t], slot_hf[:, :].unsqueeze(2).broadcast_to([P, NT, n_t]),
                                      iota_t[:, 0:n_t].unsqueeze(1).broadcast_to([P, NT, n_t]), ALU.is_equal),
                    dve.tensor_tensor(oh_s[:, :, :], slot_lf[:, :].unsqueeze(2).broadcast_to([P, NT, P]),
                                      iota_s[:, :].unsqueeze(1).broadcast_to([P, NT, P]), ALU.is_equal))
                for a, value in enumerate((tokv, scv)):
                    ins = dve.tensor_tensor(oh_m[:, :, a, 0:n_t], oh_t[:, :, 0:n_t],
                                            value[:, :].unsqueeze(2).broadcast_to([P, NT, n_t]), ALU.mult)
                ins.then_inc(s_perm, 1)

            def route_out(u):
                n_t, t0 = (TC, 0) if u == 0 else (TU, TC)
                dve.wait_ge(s_inv, u + 1)
                own(dve.tensor_copy(inv[:, :, 0:n_t],
                                    bank[:, 7, 256:256 + 2 * n_t].rearrange("p (a t) -> p a t", a=2)))
                dve.tensor_scalar(idx_in[:, t0:t0 + n_t], inv[:, 0, 0:n_t], -1.0, 0.0, ALU.add,
                                  ALU.max).then_inc(s_route, 1)
                own(dve.tensor_scalar(empty[:, 0:n_t], inv[:, 0, 0:n_t], 0.0, float(2 * N), ALU.is_equal, ALU.mult),
                    dve.tensor_copy(slot_scale[:, t0:t0 + n_t], inv[:, 1, 0:n_t]))
                own(stt(out=out_f[:, 0:n_t], in0=inv[:, 0, 0:n_t], scalar=-1.0, in1=empty[:, 0:n_t],
                        op0=ALU.add, op1=ALU.add))
                dve.tensor_copy(idx_out[:, t0:t0 + n_t], out_f[:, 0:n_t]).then_inc(s_route_out, 1)

            route_in(0)
            route_tiles(0)
            route_one_hots(0)
            route_out(0)

            def tiles(t, par, e, ranks=False):
                def next_rows():
                    if within(t + 1, TT):
                        dve.wait_ge(s_xhi, t + 2)
                        stt(out=xg_lo[:, 1 - par, :], in0=bank[:, 4, 0:DX], scalar=XS, in1=xg_hi[:, 1 - par, :],
                            op0=ALU.mult, op1=ALU.subtract).then_inc(s_xlo, 1)

                def this_tile():
                    if ranks and within(t, NT):
                        if isinstance(t, int) and t == 0:
                            dve.wait_ge(s_pm_ld, 32)
                            dve.wait_ge(s_dconst, 2)
                        block = ds(t * P, P)
                        upto(dve, s_lt, t)
                        dve.tensor_copy(crow[:, block], prow[:, block]).then_inc(s_crow, 1)
                        upto(dve, s_cnt, t - 1)
                        dve.wait_ge(s_crow, t + 1)
                        dve.tensor_scalar(less[:, par, :], crow[:, :], pm_c[:, ds(t, 1)], None,
                                          ALU.is_lt).then_inc(s_lt, 1)
                        dve.wait_ge(s_lt, t + 1)
                        stt(out=less[:, par, block], in0=prow[:, block], scalar=pm_c[:, ds(t, 1)],
                            in1=tie[:, :], op0=ALU.subtract, op1=ALU.is_lt).then_inc(s_less, 1)
                    if within(t - 1, TT):
                        o = t - 1
                        dve.wait_ge(s_Y, o + 1)
                        upto(dve, s_y, o)
                        stt(out=yb[:, :], in0=bank[:, 5, 0:D], scalar=1.0 / (XS * GS),
                            in1=wide(b2_sb[:, ds(e[0], 1), :]), op0=ALU.mult, op1=ALU.add).then_inc(s_yb, 1)
                    if within(t, TT):
                        dve.wait_ge(s_ghi, t + 1)
                        upto(dve, s_Y, t - 1)
                        stt(out=act_lo[:, par, :], in0=act[:, par, :], scalar=GS, in1=act_hi[:, par, :],
                            op0=ALU.mult, op1=ALU.subtract).then_inc(s_glo, 1)

                stages(next_rows, this_tile, late(t))

            def second_in():
                route_in(1)
                route_tiles(1)

            dve.wait_ge(s_b2, 16)
            slot_steps(dve, tiles, {NT - 1: second_in, NT: lambda: route_one_hots(1), NT + 1: lambda: route_out(1)},
                       mybir.EngineType.DVE)

        @block.tensor
        def _(pe):
            pe.wait_ge(s_const, 5)
            pe.wait_ge(s_wsplit, 2)

            def transposed(b, at, rows):
                pe.transpose(bank[:, b, at:at + P], rows[:, 0:P], ident[:, :])
                return pe.transpose(bank[:, b, at + P:at + DX], rows[:, P:DX], ident[:, :])

            def five(out_ap, terms):
                for n, (lhs, rhs) in enumerate(terms):
                    ins = pe.matmul(out_ap, lhs, rhs, start=(n == 0), stop=(n == 4))
                return ins

            def parts(col, n):
                return w_hi[:, col:col + n], w_lo[:, col:col + n], w_mix[:, col:col + n]

            def body(i, par):
                j, k = i + 2, i + 1
                def scores(r):
                    if within(i, NT):
                        if r == 0:
                            pe.wait_ge(s_q, i + 1)
                            pe.wait_ge(s_klo, i + 1)
                        upto(pe, s_PTe[r], i)
                        rows = slice(32 * r, 32 * r + 32)
                        for c in range(CH):
                            cols, to = slice(c * P, (c + 1) * P), bank[:, r, c * P:(c + 1) * P]
                            pe.matmul(to, q_sb[rows, par, cols], k_hi[rows, par, cols], start=True, stop=False)
                            ins = pe.matmul(to, q_sb[rows, par, cols], k_lo[rows, par, cols],
                                            start=False, stop=True)
                        ins.then_inc(s_S[r], 1)

                def heads_of(c, base, b, done):
                    if within(k, NT):
                        hi, lo, mix = parts(base + c * P, P)
                        ins = five(bank[:, b, c * P:(c + 1) * P],
                                   ((hi, x0h), (lo, x0h), (hi, x0l), (mix, x1h), (mix, x1l)))
                        if c == CH - 1:
                            ins.then_inc(done, 1)

                def keys(c):
                    if within(k, NT) and c == 0:
                        pe.wait_ge(s_Tlo, i + 2)
                    heads_of(c, QC, T_BANK, s_K)

                def queries(c):
                    if within(k, NT) and c == 0:
                        upto(pe, s_att, 2 * i)
                    heads_of(c, 0, Q_BANK, s_Q)

                x0h, x1h = t_hi[:, 0:P], t_hi[:, P:DX]
                x0l, x1l = t_lo[:, 0:P], t_lo[:, P:DX]
                scores(0)
                scores(1)
                keys(0)
                keys(1)
                keys(2)
                scores(2)
                scores(3)
                queries(0)
                queries(1)
                queries(2)

                def transposes(r):
                    if within(i, NT):
                        pe.wait_ge(s_P[r], i + 1)
                        for c in range(CH):
                            ins = pe.transpose(bank[:, r, c * P:(c + 1) * P], probs[:, r, c, :], ident[:, :])
                        ins.then_inc(s_PT[r], 1)

                def weighted(r):
                    if within(i, NT):
                        pe.wait_ge(s_PTe[r], i + 1)
                        for c in range(CH):
                            hd = RG * c + r
                            ins = pe.matmul(bank[:, Q_BANK, hd * (HD + 1):(hd + 1) * (HD + 1)],
                                            probs_t[:, r, c, :], v_sb[:, par, hd, :], start=True, stop=True)
                        if r == RG - 1:
                            ins.then_inc(s_O, 1)

                if within(k, NT + 5):
                    upto(pe, s_v, clip(i + 2, NT + 1))
                    upto(pe, s_h2, clip(i - 2, NT))
                    upto(pe, s_lg, i - 4)
                    ins = None
                    if within(i - 4, NT):
                        pe.wait_ge(s_x2t, i - 3)
                        at = bank[:, V_BANK, QC:QC + 2 * E]
                        pe.matmul(at, x2t[:, 0, :], wr_sb[:, 0, :], start=True, stop=False)
                        ins = pe.matmul(at, x2t[0:D2, 1, :], wr_sb[0:D2, 1, :], start=False, stop=True)
                    if within(k, NT):
                        hi, lo, mix = parts(2 * QC, D)
                        ins = five(bank[:, V_BANK, 0:D],
                                   ((x0h, hi), (x0h, lo), (x0l, hi), (x1h, mix), (x1l, mix)))
                    if within(i - 2, NT):
                        pe.wait_ge(s_Tlo, i + 2)
                        a0h, a1h = t_hi[:, DX:DX + P], t_hi[:, DX + P:]
                        a0l, a1l = t_lo[:, DX:DX + P], t_lo[:, DX + P:]
                        hi, lo, mix = parts(2 * QC + D, D)
                        ins = five(bank[:, V_BANK, D:2 * D],
                                   ((a0h, hi), (a0h, lo), (a0l, hi), (a1h, mix), (a1l, mix)))
                    if ins is not None:
                        ins.then_inc(s_VY, 1)
                    else:
                        pe.sem_inc(s_VY, 1)

                transposes(0)
                transposes(1)
                if within(i, NT):
                    pe.wait_ge(s_v, i + 2)
                    pe.wait_ge(s_q, clip(i + 2, NT))
                    upto(pe, s_att, 2 * i)
                weighted(0)
                transposes(2)
                if within(j, NT + 3):
                    upto(pe, s_klo, clip(i + 2, NT))
                    upto(pe, s_Tlo, i + 2)
                    if within(j, NT):
                        pe.wait_ge(s_xn, 2 * j + 2)
                        ins = transposed(T_BANK, 0, xn[:, par, :])
                    if within(i - 1, NT):
                        pe.wait_ge(s_att, 2 * i)
                        ins = transposed(T_BANK, DX, att[:, :])
                    ins.then_inc(s_T, 1)
                transposes(3)
                weighted(1)
                if within(i - 3, NT):
                    pe.wait_ge(s_xn2, 2 * (i - 2))
                    upto(pe, s_x2t, i - 3)
                    ins = transposed(X2_BANK, 0, xn2[:, 1 - par, :])
                    ins.then_inc(s_X2, 1)
                weighted(2)
                weighted(3)

            pe.wait_ge(s_biases, 16 * 3)
            steps(pe, body)

            pe.wait_ge(s_pmc, 1)
            pe.transpose(bank[0:NT, 2, 0:P], pm_c[:, :], ident[:, :]).then_inc(s_pmT, 1)

            def counts(u):
                pe.wait_ge(s_ohx, u + 1)
                at = bank[:, 7, 0:(NT + 1) * E]
                pe.matmul(at, before[:, :], ohx[:, :, :].rearrange("p i e -> p (i e)"), start=True, stop=False)
                for n in range(NT):
                    pe.matmul(bank[:, 7, (n + 1) * E:(NT + 1) * E], ones[:, :],
                              ohx[:, n:n + 1, :].broadcast_to([P, NT - n, E]), start=False, stop=False,
                              skip_group_check=True)
                ins = pe.matmul(at, ones[:, :], ohx[:, NT:, :].broadcast_to([P, NT + 1, E]), start=False, stop=True)
                ins.then_inc(s_pre, 1)

            def invert(u):
                n_t = TC if u == 0 else TU
                pe.wait_ge(s_perm, u + 1)
                at = bank[:, 7, 256:256 + 2 * n_t].rearrange("p (a t) -> p a t", a=2)
                for n in range(NT):
                    ins = pe.matmul(at, oh_s[:, n, :], oh_m[:, n, :, 0:n_t], start=(n == 0), stop=(n == NT - 1))
                ins.then_inc(s_inv, 1)

            counts(0)
            invert(0)

            pe.wait_ge(s_esplit, 4 * E)
            pe.wait_ge(s_route, 1)
            pe.wait_ge(s_pmt, 1)

            def tiles(t, par, e, ranks=False):
                def next_rows():
                    if within(t + 1, TT):
                        pe.wait_ge(s_gather, 16 * (t + 2))
                        upto(pe, s_xlo, t + 1)
                        ins = transposed(4, 0, xg[:, 1 - par, :])
                        ins.then_inc(s_XT, 1)

                def this_tile():
                    if within(t, TT):
                        x0h, x1h = xg_hi[:, par, 0:P], xg_hi[:, par, P:DX]
                        x0l, x1l = xg_lo[:, par, 0:P], xg_lo[:, par, P:DX]
                        pe.wait_ge(s_xlo, t + 1)
                        for half in range(2):
                            upto(pe, s_g[half], t - 1)
                            for f in range(3 * half, 3 * half + 3):
                                def w(src, part, f=f):
                                    return wide(src[:, ds(e[1], 1), part * F + f * P:part * F + (f + 1) * P])
                                ins = five(bank[:, 2 * par + half, (f % 3) * P:(f % 3 + 1) * P],
                                           ((w(e_hi, 0), x0h), (w(e_lo, 0), x0h), (w(e_hi, 0), x0l),
                                            (w(e_lo, 1), x1h), (w(e_lo, 1), x1l)))
                            ins.then_inc(s_H[half], 1)
                    if ranks and within(t - 1, NT):
                        b = t - 1
                        first = isinstance(b, int) and b == 0
                        pe.wait_ge(s_less, b + 1)
                        for n in range(NT):
                            ins = pe.matmul(bank[:, 6, n * E:(n + 1) * E], less[:, 1 - par, n * P:(n + 1) * P],
                                            wide(oh[:, ds(2 * b, 1), :]), start=(first and n == 0), stop=False,
                                            skip_group_check=True)
                        ins.then_inc(s_cnt, 1)
                    if within(t - 1, TT):
                        o = t - 1
                        pe.wait_ge(s_glo, o + 1)
                        upto(pe, s_yb, o)
                        for c in range(FC):
                            ah, al = act_hi[:, 1 - par, c * P:(c + 1) * P], act_lo[:, 1 - par, c * P:(c + 1) * P]
                            cols = slice(2 * F + c * D, 2 * F + (c + 1) * D)
                            wh, wl = wide(e_hi[:, ds(e[0], 1), cols]), wide(e_lo[:, ds(e[0], 1), cols])
                            pe.matmul(bank[:, 5, 0:D], ah, wh, start=(c == 0), stop=False)
                            pe.matmul(bank[:, 5, 0:D], ah, wl, start=False, stop=False)
                            ins = pe.matmul(bank[:, 5, 0:D], al, wh, start=False, stop=(c == FC - 1))
                        ins.then_inc(s_Y, 1)

                stages(next_rows, this_tile, late(t))

            def last_rank():
                b = NT - 1
                pe.wait_ge(s_less, b + 1)
                for n in range(NT):
                    ins = pe.matmul(bank[:, 6, n * E:(n + 1) * E], less[:, b % 2, n * P:(n + 1) * P],
                                    oh[:, 2 * b, :], start=False, stop=True, skip_group_check=True)
                ins.then_inc(s_cnt, 1)
                counts(1)

            slot_steps(pe, tiles, {NT - 1: last_rank, NT + 1: lambda: invert(1)}, mybir.EngineType.PE)


_ORDER = ["ids", "types", "word", "pos", "type_emb", "gamma", "beta", "wqkvp", "b_proj", "wr", "br",
          "wexp", "b1", "b2"]


def kernel(**inputs):
    import numpy as np
    import concourse.bacc as bacc
    from concourse import mybir as mb
    from concourse.bass_utils import run_bass_kernel_spmd as run

    a = {k: np.asarray(v) for k, v in inputs.items()}
    laid = {}
    laid["ids"] = a["x"].T
    laid["types"] = a["mask_BS_i1_0"].T
    laid["word"] = a["L0_tok_word_emb"]
    laid["pos"] = a["L0_tok_pos_emb"][:P]
    laid["type_emb"] = a["L0_tok_type_emb"].reshape(1, 2 * D)
    laid["gamma"] = a["L0_tok_ln_gamma"][None]
    laid["beta"] = a["L0_tok_ln_beta"][None]
    laid["b_proj"] = a["L0_attn_b_proj"][None]

    def halves(w):
        return np.stack([w[:P], np.concatenate([w[P:], w[P:]])])

    w = a["L0_attn_w_qkv"].T
    twice = [np.repeat(w[:, n * D:(n + 1) * D].reshape(D, HEADS, 1, HD), 2, axis=2).reshape(D, QC)
             for n in range(2)]
    laid["wqkvp"] = halves(np.concatenate(twice + [w[:, 2 * D:], a["L0_attn_w_proj"].T], axis=1))
    wr = np.concatenate([a["L0_ffn_Wsc"], a["L0_ffn_Wsu"]], axis=1)
    laid["wr"] = halves(wr).transpose(1, 0, 2)
    laid["br"] = np.concatenate([a["L0_ffn_bsc"], a["L0_ffn_bsu"]])[None]
    w1 = np.concatenate([a["L0_ffn_W1c"], a["L0_ffn_W1u"]])
    w2 = np.concatenate([a["L0_ffn_W2c"], a["L0_ffn_W2u"]])
    laid["wexp"] = np.concatenate([
        np.concatenate([*halves(w1[e]), w2[e].reshape(FC, P, D).transpose(1, 0, 2).reshape(P, FC * D)], axis=1)
        for e in range(2 * E)], axis=1)
    laid["b1"] = np.concatenate([a["L0_ffn_b1c"], a["L0_ffn_b1u"]]).reshape(2 * E, FC, P).transpose(2, 0, 1)
    laid["b2"] = np.concatenate([a["L0_ffn_b2c"], a["L0_ffn_b2u"]]).reshape(1, 2 * E * D)

    nc = bacc.Bacc("TRN2", target_bir_lowering=False, num_devices=1)
    arrays, args = {}, []
    for name in _ORDER:
        arrays[f"in_{name}"] = np.ascontiguousarray(laid[name])
        args.append(nc.dram_tensor(f"in_{name}", laid[name].shape, mb.dt.from_np(laid[name].dtype),
                                   kind="ExternalInput").ap())
    args.append(nc.dram_tensor("xrows", (N, DX), mb.dt.float32).ap())
    args.append(nc.dram_tensor("prow_dram", (2, N), mb.dt.float32).ap())
    out = nc.dram_tensor("out_0", (N, D), mb.dt.float32, kind="ExternalOutput").ap()
    build(nc, *args, out)
    got = run(nc, [arrays], core_ids=[0]).results[0]["out_0"]
    return got.reshape(SEQS, P, D)
```
